# Optimizing a Trainium2 kernel written in Bass

```python
import numpy as np
import jax
import jax.numpy as jnp

def _softmax(x, axis=-1):
    return jax.nn.softmax(x, axis=axis)

def _gelu(x):
    return jax.nn.gelu(x, approximate=True)

def _silu(x):
    return jax.nn.silu(x)

def _sigmoid(x):
    return jax.nn.sigmoid(x)

def _layernorm(x, axis=-1, eps=1e-05):
    m = jnp.mean(x, axis=axis, keepdims=True)
    v = jnp.var(x, axis=axis, keepdims=True)
    return (x - m) / jnp.sqrt(v + eps)

def _scatter_add(tgt, idx, src, axis=0):
    return tgt.at[idx].add(src)

def _segment_sum(src, seg, n):
    return jax.ops.segment_sum(src, seg, n)
kernel_name = 'mk_prb_d1_jaxref_r8_cb12b9'

def setup_inputs(seed: int=0):
    np.random.seed(seed)
    _w = jnp.asarray

    def _L0_attn_setup():
        import jax, jax.numpy as jnp
        import numpy as np
        D_MODEL, N_HEADS, N_KV, HEAD_DIM, D_LAT = (128, 8, 2, 128, 32)
        N_REP = N_HEADS // N_KV
        B, T = (2, 256)
        key = jax.random.key(seed)
        ks = jax.random.split(key, 8)
        s = lambda fan_in: 1.0 / np.sqrt(fan_in)
        return {'x': jax.random.normal(ks[0], (B, T, D_MODEL), jnp.float32), 'wq': jax.random.normal(ks[1], (D_MODEL, N_HEADS * HEAD_DIM), jnp.float32) * s(D_MODEL), 'wk_down': jax.random.normal(ks[2], (D_MODEL, N_KV * D_LAT), jnp.float32) * s(D_MODEL), 'wv_down': jax.random.normal(ks[3], (D_MODEL, N_KV * D_LAT), jnp.float32) * s(D_MODEL), 'wk_up': jax.random.normal(ks[4], (D_LAT, HEAD_DIM), jnp.float32) * s(D_LAT), 'wv_up': jax.random.normal(ks[5], (D_LAT, HEAD_DIM), jnp.float32) * s(D_LAT), 'wo': jax.random.normal(ks[6], (N_HEADS * HEAD_DIM, D_MODEL), jnp.float32) * s(N_HEADS * HEAD_DIM)}
    _L0_attn_in = _L0_attn_setup()

    def _L0_ffn_setup():
        import jax, jax.numpy as jnp
        import numpy as np
        DIM = 128
        DEPTH = 6
        HEADS = 16
        DIM_HEAD = 64
        WINDOW = 32
        INNER = HEADS * DIM_HEAD
        DIM_INNER = int(DIM * 4 * 2 / 3)
        QK_SCALE = 8.0

        def shift_tokens(t):
            a, s = jnp.split(t, 2, -1)
            s = jnp.pad(s, ((0, 0), (1, 0), (0, 0)))[:, :-1]
            return jnp.concatenate([a, s], -1)

        def l2norm(t):
            return t / jnp.maximum(jnp.linalg.norm(t, axis=-1, keepdims=True), 1e-12)

        def rotate_half(x):
            x1, x2 = jnp.split(x, 2, -1)
            return jnp.concatenate([-x2, x1], -1)

        def rotary_tables(n):
            half = jnp.arange(0, DIM_HEAD, 2, dtype=jnp.float32)
            inv_freq = 1.0 / 10000.0 ** (half / DIM_HEAD)
            t = jnp.arange(n, dtype=jnp.float32)
            freqs = t[:, None] * inv_freq[None, :]
            freqs = jnp.concatenate([freqs, freqs], -1)
            base_scale = (half + 0.4 * DIM_HEAD) / (1.4 * DIM_HEAD)
            power = (t - n // 2) / (WINDOW // 2)
            scale = base_scale[None, :] ** power[:, None]
            scale = jnp.concatenate([scale, scale], -1)
            return (freqs, scale)

        def local_attention(q, k, v):
            b, h, n, d = q.shape
            w = WINDOW
            nw = n // w
            bq = q.reshape(b, h, nw, w, d)
            bk = k.reshape(b, h, nw, w, d)
            bv = v.reshape(b, h, nw, w, d)

            def look(t):
                p = jnp.pad(t, ((0, 0), (0, 0), (1, 0), (0, 0), (0, 0)))
                return jnp.concatenate([p[:, :, :nw], p[:, :, 1:]], axis=3)
            bk2, bv2 = (look(bk), look(bv))
            seq = jnp.arange(n).reshape(nw, w)
            seq_p = jnp.pad(seq, ((1, 0), (0, 0)), constant_values=-1)
            jt = jnp.concatenate([seq_p[:nw], seq_p[1:]], axis=1)
            it = seq[:, :, None]
            jb = jt[:, None, :]
            mask = (it < jb) | (it > jb + w) | (jb == -1)
            sim = jnp.einsum('bhwie,bhwje->bhwij', bq, bk2) * QK_SCALE
            sim = jnp.where(mask, -jnp.finfo(sim.dtype).max, sim)
            attn = jax.nn.softmax(sim, -1)
            out = jnp.einsum('bhwij,bhwje->bhwie', attn, bv2)
            return out.reshape(b, h, n, d)

        def attn_layer(x, Wqkv, qs, ksc, Wo):
            b, n, _ = x.shape
            qkv = x @ Wqkv
            q, k, v = jnp.split(qkv, 3, -1)
            sh = lambda t: t.reshape(b, n, HEADS, DIM_HEAD).transpose(0, 2, 1, 3)
            q, k, v = (sh(q), sh(k), sh(v))
            q = l2norm(q) * qs
            k = l2norm(k) * ksc
            freqs, scale = rotary_tables(n)
            cos, sin = (jnp.cos(freqs), jnp.sin(freqs))
            q = q * cos * scale + rotate_half(q) * sin * scale
            inv = 1.0 / scale
            k = k * cos * inv + rotate_half(k) * sin * inv
            out = local_attention(q, k, v)
            out = out.transpose(0, 2, 1, 3).reshape(b, n, INNER)
            return out @ Wo

        def ffn_layer(x, g, bln, W1, b1, W2, b2):
            mu = x.mean(-1, keepdims=True)
            var = ((x - mu) ** 2).mean(-1, keepdims=True)
            xn = (x - mu) / jnp.sqrt(var + 1e-05) * g + bln
            hg = xn @ W1 + b1
            a, gate = jnp.split(hg, 2, -1)
            return a * jax.nn.gelu(gate, approximate=False) @ W2 + b2
        key = jax.random.key(seed)
        ks = jax.random.split(key, 8)
        B, N = (2, 256)
        init = lambda k, shape: jax.random.normal(k, shape, jnp.float32) * 0.02
        return {'x': jax.random.normal(ks[0], (B, N, DIM), jnp.float32), 'Wqkv': init(ks[1], (DEPTH, DIM, 3 * INNER)), 'q_scale': jnp.ones((DEPTH, DIM_HEAD), jnp.float32), 'k_scale': jnp.ones((DEPTH, DIM_HEAD), jnp.float32), 'Wo': init(ks[2], (DEPTH, INNER, DIM)), 'ln_g': jnp.ones((DEPTH, DIM), jnp.float32), 'ln_b': jnp.zeros((DEPTH, DIM), jnp.float32), 'W1': init(ks[3], (DEPTH, DIM, 2 * DIM_INNER)), 'b1': jnp.zeros((DEPTH, 2 * DIM_INNER), jnp.float32), 'W2': init(ks[4], (DEPTH, DIM_INNER, DIM)), 'b2': jnp.zeros((DEPTH, DIM), jnp.float32)}
    _L0_ffn_in = _L0_ffn_setup()
    _d = {'L0_attn_x': _L0_attn_in['x'], 'L0_attn_wq': _L0_attn_in['wq'], 'L0_attn_wk_down': _L0_attn_in['wk_down'], 'L0_attn_wv_down': _L0_attn_in['wv_down'], 'L0_attn_wk_up': _L0_attn_in['wk_up'], 'L0_attn_wv_up': _L0_attn_in['wv_up'], 'L0_attn_wo': _L0_attn_in['wo'], 'L0_ffn_Wqkv': _L0_ffn_in['Wqkv'], 'L0_ffn_q_scale': _L0_ffn_in['q_scale'], 'L0_ffn_k_scale': _L0_ffn_in['k_scale'], 'L0_ffn_Wo': _L0_ffn_in['Wo'], 'L0_ffn_ln_g': _L0_ffn_in['ln_g'], 'L0_ffn_ln_b': _L0_ffn_in['ln_b'], 'L0_ffn_W1': _L0_ffn_in['W1'], 'L0_ffn_b1': _L0_ffn_in['b1'], 'L0_ffn_W2': _L0_ffn_in['W2'], 'L0_ffn_b2': _L0_ffn_in['b2']}
    _x0 = _d['L0_attn_x']
    _d['L0_attn_x'] = jax.random.normal(jax.random.fold_in(jax.random.key(seed), 1), (2, 1024, 128), dtype=_x0.dtype)
    del _x0
    return _d

def reference(L0_attn_x, L0_attn_wq, L0_attn_wk_down, L0_attn_wv_down, L0_attn_wk_up, L0_attn_wv_up, L0_attn_wo, L0_ffn_Wqkv, L0_ffn_q_scale, L0_ffn_k_scale, L0_ffn_Wo, L0_ffn_ln_g, L0_ffn_ln_b, L0_ffn_W1, L0_ffn_b1, L0_ffn_W2, L0_ffn_b2):

    def _L0_attn_ref(x, wq, wk_down, wv_down, wk_up, wv_up, wo):
        import jax, jax.numpy as jnp
        import numpy as np
        D_MODEL, N_HEADS, N_KV, HEAD_DIM, D_LAT = (128, 8, 2, 128, 32)
        N_REP = N_HEADS // N_KV
        B, T = (2, 256)
        Bq, Tq, _ = x.shape
        scale = HEAD_DIM ** (-0.5)
        q = (x @ wq).reshape(Bq, Tq, N_KV, N_REP, HEAD_DIM)
        k_lat = (x @ wk_down).reshape(Bq, Tq, N_KV, D_LAT)
        v_lat = (x @ wv_down).reshape(Bq, Tq, N_KV, D_LAT)
        k = jnp.einsum('bkhl,ld->bkhd', k_lat, wk_up)
        v = jnp.einsum('bkhl,ld->bkhd', v_lat, wv_up)
        scores = jnp.einsum('bqhrd,bkhd->bhrqk', q, k) * scale
        causal = jnp.tril(jnp.ones((Tq, Tq), dtype=bool))
        scores = jnp.where(causal, scores, jnp.finfo(scores.dtype).min)
        probs = jax.nn.softmax(scores, axis=-1)
        y = jnp.einsum('bhrqk,bkhd->bqhrd', probs, v)
        y = y.reshape(Bq, Tq, N_HEADS * HEAD_DIM)
        return y @ wo

    def _L0_ffn_ref(x, Wqkv, q_scale, k_scale, Wo, ln_g, ln_b, W1, b1, W2, b2):
        import jax, jax.numpy as jnp
        import numpy as np
        DIM = 128
        DEPTH = 6
        HEADS = 16
        DIM_HEAD = 64
        WINDOW = 32
        INNER = HEADS * DIM_HEAD
        DIM_INNER = int(DIM * 4 * 2 / 3)
        QK_SCALE = 8.0

        def shift_tokens(t):
            a, s = jnp.split(t, 2, -1)
            s = jnp.pad(s, ((0, 0), (1, 0), (0, 0)))[:, :-1]
            return jnp.concatenate([a, s], -1)

        def l2norm(t):
            return t / jnp.maximum(jnp.linalg.norm(t, axis=-1, keepdims=True), 1e-12)

        def rotate_half(x):
            x1, x2 = jnp.split(x, 2, -1)
            return jnp.concatenate([-x2, x1], -1)

        def rotary_tables(n):
            half = jnp.arange(0, DIM_HEAD, 2, dtype=jnp.float32)
            inv_freq = 1.0 / 10000.0 ** (half / DIM_HEAD)
            t = jnp.arange(n, dtype=jnp.float32)
            freqs = t[:, None] * inv_freq[None, :]
            freqs = jnp.concatenate([freqs, freqs], -1)
            base_scale = (half + 0.4 * DIM_HEAD) / (1.4 * DIM_HEAD)
            power = (t - n // 2) / (WINDOW // 2)
            scale = base_scale[None, :] ** power[:, None]
            scale = jnp.concatenate([scale, scale], -1)
            return (freqs, scale)

        def local_attention(q, k, v):
            b, h, n, d = q.shape
            w = WINDOW
            nw = n // w
            bq = q.reshape(b, h, nw, w, d)
            bk = k.reshape(b, h, nw, w, d)
            bv = v.reshape(b, h, nw, w, d)

            def look(t):
                p = jnp.pad(t, ((0, 0), (0, 0), (1, 0), (0, 0), (0, 0)))
                return jnp.concatenate([p[:, :, :nw], p[:, :, 1:]], axis=3)
            bk2, bv2 = (look(bk), look(bv))
            seq = jnp.arange(n).reshape(nw, w)
            seq_p = jnp.pad(seq, ((1, 0), (0, 0)), constant_values=-1)
            jt = jnp.concatenate([seq_p[:nw], seq_p[1:]], axis=1)
            it = seq[:, :, None]
            jb = jt[:, None, :]
            mask = (it < jb) | (it > jb + w) | (jb == -1)
            sim = jnp.einsum('bhwie,bhwje->bhwij', bq, bk2) * QK_SCALE
            sim = jnp.where(mask, -jnp.finfo(sim.dtype).max, sim)
            attn = jax.nn.softmax(sim, -1)
            out = jnp.einsum('bhwij,bhwje->bhwie', attn, bv2)
            return out.reshape(b, h, n, d)

        def attn_layer(x, Wqkv, qs, ksc, Wo):
            b, n, _ = x.shape
            qkv = x @ Wqkv
            q, k, v = jnp.split(qkv, 3, -1)
            sh = lambda t: t.reshape(b, n, HEADS, DIM_HEAD).transpose(0, 2, 1, 3)
            q, k, v = (sh(q), sh(k), sh(v))
            q = l2norm(q) * qs
            k = l2norm(k) * ksc
            freqs, scale = rotary_tables(n)
            cos, sin = (jnp.cos(freqs), jnp.sin(freqs))
            q = q * cos * scale + rotate_half(q) * sin * scale
            inv = 1.0 / scale
            k = k * cos * inv + rotate_half(k) * sin * inv
            out = local_attention(q, k, v)
            out = out.transpose(0, 2, 1, 3).reshape(b, n, INNER)
            return out @ Wo

        def ffn_layer(x, g, bln, W1, b1, W2, b2):
            mu = x.mean(-1, keepdims=True)
            var = ((x - mu) ** 2).mean(-1, keepdims=True)
            xn = (x - mu) / jnp.sqrt(var + 1e-05) * g + bln
            hg = xn @ W1 + b1
            a, gate = jnp.split(hg, 2, -1)
            return a * jax.nn.gelu(gate, approximate=False) @ W2 + b2
        for i in range(DEPTH):
            x = attn_layer(shift_tokens(x), Wqkv[i], q_scale[i], k_scale[i], Wo[i]) + x
            x = ffn_layer(shift_tokens(x), ln_g[i], ln_b[i], W1[i], b1[i], W2[i], b2[i]) + x
        return x
    x = L0_attn_x
    xn = _layernorm(x, axis=-1)
    x = x + _L0_attn_ref(xn, L0_attn_wq, L0_attn_wk_down, L0_attn_wv_down, L0_attn_wk_up, L0_attn_wv_up, L0_attn_wo) + _L0_ffn_ref(xn, L0_ffn_Wqkv, L0_ffn_q_scale, L0_ffn_k_scale, L0_ffn_Wo, L0_ffn_ln_g, L0_ffn_ln_b, L0_ffn_W1, L0_ffn_b1, L0_ffn_W2, L0_ffn_b2)
    return x

_drawn_inputs = setup_inputs


def setup_inputs(seed=0):
    import zlib

    import numpy as np

    out = dict(_drawn_inputs(seed))
    spreads = {'L0_ffn_q_scale': (1.0, 0.6),
     'L0_ffn_k_scale': (1.0, 0.6),
     'L0_ffn_ln_g': (1.0, 0.6),
     'L0_ffn_ln_b': (0.0, 0.8),
     'L0_ffn_b1': (0.0, 0.8),
     'L0_ffn_b2': (0.0, 0.1)}
    factors = {'L0_ffn_W1': 3.651,
     'L0_ffn_W2': 3.583,
     'L0_attn_wq': 2.827,
     'L0_attn_wk_down': 2.765,
     'L0_attn_wk_up': 2.817}
    for name, (base, spread) in spreads.items():
        noise = np.random.default_rng([zlib.crc32(name.encode()), seed]).standard_normal(out[name].shape)
        drawn = base * np.exp(spread * noise) if base else spread * noise
        out[name] = jnp.asarray(drawn.astype(out[name].dtype))
    for name, factor in factors.items():
        out[name] = (out[name] * factor).astype(out[name].dtype)
    return out
```

```python
from contextlib import ExitStack

import numpy as np

import concourse.bass as bass
from concourse import mybir

F32 = mybir.dt.float32
ALU = mybir.AluOpType
ACT = mybir.ActivationFunctionType
AXX = mybir.AxisListType.X

P = 128
B, T, D = 2, 1024, 128
NT = T // P
TILES = B * NT
GH, KV, GD, LAT = 8, 2, 128, 32
REP = GH // KV
G_SCALE = float(GD) ** -0.5
DEPTH, LH, LD, WIN = 6, 16, 64, 32
HALF = LD // 2
NG = LH // 4
NP = LH // 2
NW = P // WIN
QK_SCALE = 8.0
FF = int(D * 4 * 2 / 3)
FJ = [(0, 128), (128, 128), (256, FF - 256)]
CH = 512
NC = B * T // CH
CR = 8
NEG = -1.0e30

C_ID, C_CEN, C_CAUS, C_ONE, C_CAP, C_MEAN = 0, 128, 256, 384, 416, 416 + 64 * NT
C_N = C_MEAN + 1
(V_QA, V_QB, V_KA, V_KB, V_NKA, V_NKB, V_G, V_B, V_B1A, V_B1G, V_B2) = 0, 1, 2, 3, 4, 5, 6, 7, 8, 11, 14
V_N = 15


def shape_constants():
    c = np.zeros((P, C_N), np.float32)
    i = np.arange(P)
    c[:, C_ID:C_ID + P] = np.eye(P)
    c[:, C_CEN:C_CEN + P] = np.eye(P) - 1.0 / D
    c[:, C_MEAN] = 1.0 / D
    c[:, C_CAUS:C_CAUS + P] = np.where(i[None, :] <= i[:, None], 3.0e38, NEG)
    c[i, C_ONE + i // 32] = 1.0
    r, k = i[:, None] % WIN, np.arange(2 * WIN)[None, :]
    inside = (k >= r) & (k <= r + WIN)
    for n in range(NT):
        ok = inside & ((i[:, None] >= WIN) | (k >= WIN)) if n == 0 else inside
        c[:, C_CAP + 64 * n:C_CAP + 64 * (n + 1)] = np.where(ok, 3.0e38, NEG)
    f = np.float32
    half = np.arange(0, LD, 2, dtype=f)
    inv_freq = f(1.0) / np.power(f(10000.0), half / f(LD))
    t = np.arange(T, dtype=f)
    freqs = t[:, None] * inv_freq[None, :]
    base = (half + f(0.4 * LD)) / f(1.4 * LD)
    power = (t - f(T // 2)) / f(WIN // 2)
    scale = np.power(base[None, :], power[:, None])
    cos, sin = np.cos(freqs), np.sin(freqs)
    tabs = [cos * scale, sin * scale, cos / scale, sin / scale]
    tabs = np.stack([np.tile(x.T, (4, 1)) for x in tabs]).astype(f)
    return c, np.ascontiguousarray(tabs)


def build(nc, x, wq, wkd, wvd, wku, wvuT, wo, wqkv, lwo, w1, w2, par, cst_d, tab_d, out):
    ctx = ExitStack()
    with ctx:
        def sb(name, shape):
            return ctx.enter_context(nc.sbuf_tensor(name, shape, F32))

        def sem(name):
            return ctx.enter_context(nc.semaphore(name))

        cst = sb("cst", [P, C_N])
        parv = sb("parv", [P, V_N])
        Wqkv = sb("Wqkv", [P, 3 * LH * LD])
        Wo = sb("Wo", [P, NP, D])
        W1 = sb("W1", [P, 2 * FF])
        W2 = sb("W2", [P, 3, D])
        tabs = sb("tabs", [P, 2, 2, 2, T])
        ident = cst[:, C_ID:C_ID + P]
        centre = cst[:, C_CEN:C_CEN + P]
        meanw = cst[:, C_MEAN:C_MEAN + 1]
        caus = cst[:, C_CAUS:C_CAUS + P]
        ones4 = cst[:, C_ONE:C_ONE + 32]

        X = sb("X", [P, B, T + 1])
        X1 = sb("X1", [P, B, T + 1])
        res = sb("res", [P, TILES, D])
        arena = sb("arena", [P, 4 * 4096])
        kd = [arena[:, 4096 * i:4096 * (i + 1)].rearrange("p (j h t) -> p j h t", j=2 * NG, h=4)
              for i in range(2)]
        vd = [arena[:, 8192 + 4096 * i:8192 + 4096 * (i + 1)]
              .rearrange("p (w o n) -> p w o n", w=NW, o=2) for i in range(2)]
        vs = sb("vs", [P, 2, LH * LD])
        xs = sb("xs", [P, 2, P])
        qr = sb("qr", [P, 2, 2 * NG, P])
        kr = sb("kr", [P, 2 * NG, P])
        sq = sb("sq", [P, 2, CH])
        swp = sb("swp", [P, 2, CH])
        ssc = sb("ssc", [P, 2 * P])
        rs = sb("rs", [P, 4, 2 * LH])
        rke = sb("rke", [P, NG, 4, HALF])
        rq8 = sb("rq8", [P, 2, LH])
        prob = sb("prob", [P, 2, LH * 64])
        nmax = sb("nmax", [P, LH])
        den = sb("den", [P, 2, LH])
        ptile = sb("ptile", [P, NP, P])
        osb = sb("osb", [P, LH, LD])
        otile = sb("otile", [P, NP, P])
        fs = sb("fs", [P, CH])
        xc = sb("xc", [P, CH])
        fsq = sb("fsq", [P, CH])
        fr = sb("fr", [P, 4, NT])
        fre = sb("fre", [P, 4, P])
        xn = sb("xn", [P, CH])
        gl = [ptile[:, 0:4, :].rearrange("p a b -> p (a b)"),
              ptile[:, 4:8, :].rearrange("p a b -> p (a b)"),
              osb[:, 0:8, :].rearrange("p a b -> p (a b)")]
        hb = [otile[:, 0:4, :].rearrange("p a b -> p (a b)"),
              otile[:, 4:8, :].rearrange("p a b -> p (a b)"),
              osb[:, 8:16, :].rearrange("p a b -> p (a b)")]
        gq = arena[:, 0:4096].rearrange("p (h t) -> p h t", h=REP)
        gk = arena[:, 4096:5120]
        gx = arena[:, 5120:6144]
        gpt = arena[:, 6144:10240].rearrange("p (h k t) -> p h k t", h=REP, k=NT)
        gwo = arena[:, 10240:11264].rearrange("p (h n) -> p h n", h=GH)
        gkl = arena[0:LAT, 11264:12288]
        gwq = arena[:, 12288:12800]
        gwk = arena[:, 12800:12832]
        gwv = arena[:, 12832:12864]
        gwku = arena[0:LAT, 12864:12992]
        gwvu = arena[:, 12992:13024]
        gvo = arena[:, 13056:13312].rearrange("p (k n) -> p k n", k=KV)
        gvl = arena[:, 13312:13568].rearrange("p (t n) -> p t n", t=NT)
        gy = arena[:, 13568:13696]
        gp = prob
        gst = ssc

        banks = ctx.enter_context(nc.psum_tensor("banks", [P, 8 * 512], F32))

        def bk(i):
            return banks[:, 512 * i:512 * i + 512]

        def two(i):
            return banks[:, 512 * i:512 * i + 1024]

        scores_ps = two(3).rearrange("p (h k) -> p h k", h=LH)
        outputs_ps = two(5).rearrange("p (h d) -> p h d", h=LH)

        counted = {
            "pe": ("ln_xT wvo_mm lq_mm lk_mm lkk_mm lvl_mm ls_mm lt_mm ly_mm lo_mm v_mm u_mm ss_mm ssT_mm "
                   "rkb_mm s_mm pt_mm pv_mm ot_mm wo_mm f_mu f_rb f_var f_a f_g f_out_mm fin_mm").split(),
            "act": ("xs_cp x_init wvo_cp lx_cp lq_cp lkl_cp lvl_cp ls_exp lt_cp ly_cp v_cp u_sq s_exp pt_cp ot_cp ss_cp rk_cp f_re f_xc "
                   "f_sq f_gl").split(),
            "dve": ("lo_add st_bn st_ag st_eps ln_x ls_cap ls_max ls_neg ls_rec ls_nrm u_c u_s rs_0 rs_n rs_f ss_cl rqT_cp k_nrm s_rq "
                   "s_cap s_max s_sub s_sum s_inv o_nrm wo_add tab_sc f_cp f_eps f_xn f_aff f_h x_new "
                   "fin_add").split(),
            "pool": ("zeroed u_rot").split(),
        }
        s = {n: sem(n) for v in counted.values() for n in v}

        def credit(eng, name):
            for n in counted[name]:
                eng.sem_inc(s[n], CR)
        c_in, w_in, ffw_in, qkvw_in, tab_in = (sem(n) for n in ("c_in", "w_in", "ffw_in", "qkvw_in", "tab_in"))
        xl_in, lat_w, lat_wq, out_in = (sem(n) for n in ("xl_in", "lat_w", "lat_wq", "out_in"))
        kd_in, vd_in = [sem("kd_in0"), sem("kd_in1")], [sem("vd_in0"), sem("vd_in1")]

        block = ctx.enter_context(nc.Block())

        def slots(eng, layer, slot):
            slot(layer, 0, 0, True, False, False)
            slot(layer, 0, 1, True, True, False)
            with eng.Fori(1, TILES // 2) as k:
                slot(layer, k, 0, True, True, True)
                slot(layer, k, 1, True, True, True)
            slot(layer, TILES // 2, 0, False, True, True)
            slot(layer, TILES // 2, 1, False, False, True)

        def column(n):
            return n * P + n // NT

        Xf = X[:, :, :].rearrange("p b t -> p (b t)")
        X1f = X1[:, :, :].rearrange("p b t -> p (b t)")
        bodies = [(i, h) for i in range(NT) for h in range(REP)]

        def groups(i):
            return (i + 4) // 4

        def done_groups(j):
            return sum(groups(bodies[k][0]) for k in range(j))

        NTR = done_groups(len(bodies))

        @block.sync
        def _(sp):
            for q in kd_in + vd_in:
                sp.sem_inc(q, CR)
            sp.dma_start(cst[:, :], cst_d).then_inc(c_in, 16)
            sp.dma_start(res[:, :, :], x.rearrange("b (t p) d -> p (b t) d", p=P)).then_inc(xl_in, 16)
            sp.dma_start(gwo, wo.rearrange("(h p) n -> p h n", p=P)).then_inc(lat_w, 16)
            sp.dma_start(gwku, wku).then_inc(lat_w, 16)
            sp.dma_start(gwvu, wvuT).then_inc(lat_w, 16)
            with sp.Fori(0, B * KV) as it:
                kv = sp.snap(it % KV)
                sp.wait_ge(s["lvl_mm"], CR + it)
                sp.dma_start(gwq, wq[bass.ds(kv, 1), :, :].rearrange("a p n -> p (a n)")).then_inc(lat_wq, 16)
                sp.dma_start(gwk, wkd[bass.ds(kv, 1), :, :].rearrange("a p n -> p (a n)")).then_inc(lat_wq, 16)
                sp.dma_start(gwv, wvd[bass.ds(kv, 1), :, :].rearrange("a p n -> p (a n)")).then_inc(lat_wq, 16)

            def load_attention(layer):
                sp.dma_start(Wqkv[:, :], wqkv[bass.ds(layer, 1), :, :].rearrange("a p n -> p (a n)")).then_inc(qkvw_in, 16)
                sp.dma_start(Wo[:, :, :], lwo[bass.ds(layer, 1), :, :].rearrange("a (k p) n -> p (a k) n", p=P)).then_inc(qkvw_in, 16)
                for kind in range(2):
                    for fn in range(2):
                        for hf in range(2):
                            sp.dma_start(tabs[:, kind, fn, hf, :], tab_d[2 * kind + fn, :, :]).then_inc(tab_in, 16)

            sp.wait_ge(s["zeroed"], CR + 7)
            load_attention(0)
            with sp.Fori(0, DEPTH) as layer:
                sp.wait_ge(s["x_new"], CR + layer * NC + NC)
                sp.dma_start(parv[:, :], par[bass.ds(layer, 1), :, :].rearrange("a p n -> p (a n)")).then_inc(w_in, 16)
                sp.dma_start(W1[:, :], w1[bass.ds(layer, 1), :, :].rearrange("a p n -> p (a n)")).then_inc(ffw_in, 16)
                sp.dma_start(W2[:, :, :], w2[bass.ds(layer, 1), :, :, :].rearrange("a p k n -> p (a k) n")).then_inc(ffw_in, 16)

                def slot(layer, k, par_, a, b, c):
                    n = k * 2 + par_
                    G, GK = layer * TILES + n, layer * (TILES // 2) + k
                    if a:
                        sp.wait_ge(s["pv_mm"], CR + G - 1)
                        sp.wait_ge(s["v_cp"], CR + G * 2 + 2)
                        for o in range(2):
                            r = 64 * o
                            src = vs[:, par_, 512 * o:512 * (o + 1)]
                            prev = vs[:, 1 - par_, 512 * o:512 * (o + 1)]
                            for w in range(NW):
                                sp.dma_start(vd[par_][r + 32:r + 64, w, o, :], src[32 * w:32 * w + 32, :]).then_inc(vd_in[par_], 16)
                                before = src[32 * w - 32:32 * w, :] if w else prev[96:128, :]
                                sp.dma_start(vd[par_][r:r + 32, w, o, :], before).then_inc(vd_in[par_], 16)
                        sp.wait_ge(s["k_nrm"], CR + G * 2 + 2)
                        for h in range(4):
                            sp.dma_start(kd[par_][32 * h:32 * h + 32, :, h, :], kr[32 * h:32 * h + 32, :, :]).then_inc(kd_in[par_], 16)

                slots(sp, layer, slot)
                following = sp.snap((layer + 1) % DEPTH)
                sp.wait_ge(s["wo_mm"], CR + layer * TILES + TILES)
                sp.wait_ge(s["u_s"], CR + (layer + 1) * TILES * 4)
                load_attention(following)
            sp.wait_ge(qkvw_in, 32 * (DEPTH + 1))
            sp.wait_ge(tab_in, 128 * (DEPTH + 1))
            for g4 in range(TILES // 4):
                sp.wait_ge(s["fin_add"], CR + g4 + 1)
                sp.dma_start(out.rearrange("b (t p) d -> p (b t) d", p=P)[:, 4 * g4:4 * g4 + 4, :],
                             res[:, 4 * g4:4 * g4 + 4, :]).then_inc(out_in, 16)
            sp.wait_ge(out_in, 16 * (TILES // 4))

        @block.gpsimd
        def _(pool):
            credit(pool, "pool")
            pool.memset(X[:, :, 0:1], 0.0).then_inc(s["zeroed"], 1)
            pool.memset(X1[:, :, 0:1], 0.0).then_inc(s["zeroed"], 1)
            pool.memset(vs[:, 1, :], 0.0).then_inc(s["zeroed"], 1)
            pool.wait_ge(s["lo_add"], CR + B * KV * NT)
            pool.wait_ge(lat_wq, 16 * 3 * B * KV)
            pool.wait_ge(s["lq_mm"], CR + B * KV * 8)
            for i in range(4):
                pool.memset(arena[:, 4096 * i:4096 * (i + 1)], 0.0).then_inc(s["zeroed"], 1)

            with pool.Fori(0, DEPTH) as layer:
                def slot(layer, k, par_, a, b, c):
                    n = k * 2 + par_
                    G, GK = layer * TILES + n, layer * (TILES // 2) + k
                    if not a:
                        return
                    for u in range(4):
                        pool.wait_ge(s["u_s"], CR + G * 4 + u + 1)
                        if u < 2:
                            dst = qr[:, par_, 4 * u:4 * u + 4, :]
                        else:
                            dst = kr[:, 4 * (u - 2):4 * (u - 2) + 4, :]
                        pool.tensor_tensor(dst, dst, swp[:, u % 2, :].rearrange("p (j t) -> p j t", j=4),
                                           ALU.add).then_inc(s["u_rot"], 1)

                slots(pool, layer, slot)

        @block.scalar
        def _(act):
            credit(act, "act")
            for g4 in range(TILES // 4):
                act.wait_ge(s["ln_xT"], CR + g4 + 1)
                b, t0 = divmod(4 * g4, NT)
                ins = act.activation(X[:, b, 1 + P * t0:1 + P * (t0 + 4)], bk(g4 % 2), ACT.Copy)
                ins.then_inc(s["x_init"], 1)
            act.wait_ge(s["wvo_mm"], CR + 2)
            act.activation(gvo, bk(2)[:, 0:2 * D].rearrange("p (k n) -> p k n", k=KV), ACT.Copy).then_inc(s["wvo_cp"], 1)
            with act.Fori(0, B * KV) as it:
                act.wait_ge(s["x_init"], CR + TILES // 4)
                act.wait_ge(s["lvl_mm"], CR + it)
                act.wait_ge(s["lq_mm"], CR + it * 8)
                act.activation(gx, Xf[:, bass.ds((it // KV) * (T + 1) + 1, T)], ACT.Copy).then_inc(s["lx_cp"], 1)
                act.wait_ge(s["ls_mm"], CR + it * len(bodies))
                for i in range(8):
                    act.wait_ge(s["lq_mm"], CR + it * 8 + i + 1)
                    act.activation(gq[:, i // 2, 512 * (i % 2):512 * (i % 2) + 512], bk(i % 2), ACT.Copy).then_inc(s["lq_cp"], 1)
                act.wait_ge(s["lk_mm"], CR + it + 1)
                act.activation(gkl, two(2)[0:LAT, :], ACT.Copy).then_inc(s["lkl_cp"], 1)
                act.wait_ge(s["lkk_mm"], CR + it + 1)
                act.activation(gk, two(4), ACT.Copy).then_inc(s["lkl_cp"], 1)
                act.wait_ge(s["lvl_mm"], CR + it + 1)
                act.wait_ge(s["ly_mm"], CR + it * NT)
                act.activation(gvl, bk(6)[:, 0:NT * LAT].rearrange("p (t n) -> p t n", t=NT), ACT.Copy).then_inc(s["lvl_cp"], 1)

                def exps(j):
                    J = it * len(bodies) + j
                    n = (bodies[j][0] + 1) * P
                    act.wait_ge(s["ls_neg"], CR + J + 1)
                    act.wait_ge(s["lt_mm"], CR + it * NTR + (done_groups(j - 1) if j >= 2 else 0))
                    act.activation(gp[:, j % 2, 0:n], two(2 * (j % 2))[:, 0:n], ACT.Exp, bias=gst[:, 8 + j % 2:9 + j % 2],
                                   scale=G_SCALE, accum_out=gst[:, 12 + j % 2:13 + j % 2]).then_inc(s["ls_exp"], 1)

                def evacuate(j):
                    i, h = bodies[j]
                    if h == 0:
                        act.wait_ge(s["ly_mm"], CR + it * NT + i)
                    for g in range(groups(i)):
                        k = done_groups(j) + g
                        act.wait_ge(s["lt_mm"], CR + it * NTR + k + 1)
                        nb = min(4, i + 1 - 4 * g)
                        act.activation(gpt[:, h, 4 * g:4 * g + nb, :],
                                       bk(4 + k % 2)[:, 0:P * nb].rearrange("p (k t) -> p k t", k=nb), ACT.Copy)\
                           .then_inc(s["lt_cp"], 1)
                    if h == REP - 1:
                        act.wait_ge(s["ly_mm"], CR + it * NT + i + 1)
                        act.wait_ge(s["lo_mm"], CR + it * NT + i)
                        act.activation(gy, bk(6)[:, 256:256 + P], ACT.Copy).then_inc(s["ly_cp"], 1)

                exps(0)
                for j in range(len(bodies)):
                    if j + 1 < len(bodies):
                        exps(j + 1)
                    evacuate(j)

            act.wait_ge(s["zeroed"], CR + 7)

            def shift(layer, n, par_):
                act.wait_ge(s["x_new"], CR + layer * NC + n // 4 + 1)
                act.wait_ge(s["u_mm"], CR + (layer * TILES + n) * 4 - 4)
                act.activation(xs[0:64, par_, :], Xf[0:64, bass.ds(column(n) + 1, P)], ACT.Copy).then_inc(s["xs_cp"], 1)
                act.activation(xs[64:128, par_, :], Xf[64:128, bass.ds(column(n), P)], ACT.Copy).then_inc(s["xs_cp"], 1)

            with act.Fori(0, DEPTH) as layer:
                def slot(layer, k, par_, a, b, c):
                    n = k * 2 + par_
                    G, GK = layer * TILES + n, layer * (TILES // 2) + k
                    if a:
                        shift(layer, n, par_)
                        act.wait_ge(vd_in[1 - par_], CR + (GK + par_) * 256)
                        for i in range(2):
                            act.wait_ge(s["v_mm"], CR + G * 2 + i + 1)
                            act.activation(vs[:, par_, 512 * i:512 * (i + 1)], bk(i), ACT.Copy).then_inc(s["v_cp"], 1)
                        for u in range(2):
                            square(G, u)
                    if c:
                        for i in range(2):
                            act.wait_ge(s["pt_mm"], CR + (G - 2) * 2 + i + 1)
                            act.activation(ptile[:, 4 * i:4 * i + 4, :], bk(5 + i).rearrange("p (k t) -> p k t", k=4),
                                           ACT.Copy).then_inc(s["pt_cp"], 1)
                    if a:
                        for u in range(2, 4):
                            square(G, u)
                    if b:
                        act.wait_ge(s["s_sub"], CR + G)
                        act.activation(prob[:, 1 - par_, :], prob[:, 1 - par_, :], ACT.Exp).then_inc(s["s_exp"], 1)
                    if a:
                        act.wait_ge(s["ss_mm"], CR + G * 4 + 4)
                        act.activation(ssc[:, :], bk(2)[:, 0:2 * P], ACT.Copy).then_inc(s["ss_cp"], 1)
                    if c:
                        for i in range(2):
                            act.wait_ge(s["ot_mm"], CR + (G - 2) * 2 + i + 1)
                            act.activation(otile[:, 4 * i:4 * i + 4, :], bk(7 - 2 * i).rearrange("p (k t) -> p k t", k=4),
                                           ACT.Copy).then_inc(s["ot_cp"], 1)
                    if a:
                        act.wait_ge(s["rs_n"], CR + (G + 1) * 11)
                        act.activation(rke[:, :, :, :].rearrange("p g h r -> p (g h) r"),
                                       rs[:, 2, LH:2 * LH].rearrange("p (h o) -> p h o", o=1).to_broadcast([P, LH, HALF]),
                                       ACT.Copy).then_inc(s["rk_cp"], 1)

                def square(G, u):
                    act.wait_ge(s["u_mm"], CR + G * 4 + u + 1)
                    act.wait_ge(s["ss_mm"], CR + G * 4 + u - 1)
                    act.activation(sq[:, u % 2, :], bk(u % 2), ACT.Square).then_inc(s["u_sq"], 1)

                slots(act, layer, slot)

                def ln_square(c):
                    F = layer * NC + c
                    act.wait_ge(s["f_mu"], CR + F + 1)
                    act.wait_ge(s["f_xn"], CR + F)
                    act.activation(xc[:, :], bk(2), ACT.Copy).then_inc(s["f_xc"], 1)
                    act.activation(fsq[:, :], bk(2), ACT.Square).then_inc(s["f_sq"], 1)

                def spread_rstd(c):
                    act.wait_ge(s["rs_f"], CR + (layer * NC + c + 1) * 11)
                    act.activation(fre[:, :, :], fr[:, 2, 0:4].rearrange("p (t o) -> p t o", o=1).to_broadcast([P, 4, P]),
                                   ACT.Copy).then_inc(s["f_re"], 1)

                ln_square(0)
                spread_rstd(0)
                for c in range(NC):
                    F = layer * NC + c
                    if c + 1 < NC:
                        ln_square(c + 1)
                    for j, (_, m) in enumerate(FJ):
                        if j == 2 and c + 1 < NC:
                            spread_rstd(c + 1)
                        act.wait_ge(s["f_g"], CR + F * 3 + j + 1)
                        act.wait_ge(s["f_h"], CR + F * 3 + j - 2)
                        act.activation(gl[j][0:m, :], bk(3 + j % 2)[0:m, :], ACT.Gelu,
                                       bias=parv[0:m, V_B1G + j:V_B1G + j + 1]).then_inc(s["f_gl"], 1)


        @block.vector
        def _(dve):
            credit(dve, "dve")
            def rsqrt(w, n, name, count):
                x, h, y, q = (w[:, k, 0:n] for k in range(4))
                dve.tensor_scalar(h, x, -0.5, None, ALU.mult).then_inc(s[name], 1)
                dve.tensor_scalar(y.bitcast(mybir.dt.int32), x.bitcast(mybir.dt.int32), -0.5, float(0x5F3759DF),
                                  ALU.mult, ALU.add).then_inc(s[name], 1)
                for k in range(3):
                    dve.wait_ge(s[name], count + 3 * k + 2)
                    dve.tensor_tensor(q, y, y, ALU.mult).then_inc(s[name], 1)
                    dve.wait_ge(s[name], count + 3 * k + 3)
                    dve.tensor_tensor(q, q, h, ALU.mult).then_inc(s[name], 1)
                    dve.wait_ge(s[name], count + 3 * k + 4)
                    dve.scalar_tensor_tensor(y, q, 1.5, y, ALU.add, ALU.mult).then_inc(s[name], 1)
                dve.wait_ge(s[name], count + 11)

            dve.wait_ge(xl_in, 16)
            st6 = fsq[:, 0:6 * TILES].rearrange("p (t k) -> p t k", k=6)
            ag = fs[:, 0:2 * TILES].rearrange("p (t k) -> p t k", k=2)
            for t in range(TILES):
                dve.bn_stats(st6[:, t, :], res[:, t, :]).then_inc(s["st_bn"], 1)
            for t in range(TILES):
                dve.wait_ge(s["st_bn"], CR + t + 1)
                dve.bn_aggr(ag[:, t, :], st6[:, t, :]).then_inc(s["st_ag"], 1)
            dve.wait_ge(s["st_ag"], CR + TILES)
            dve.tensor_scalar(rs[:, 0, 0:TILES], ag[:, :, 1], 1e-5, None, ALU.add).then_inc(s["st_eps"], 1)
            dve.wait_ge(s["st_eps"], CR + 1)
            rsqrt(rs, TILES, "rs_0", CR)
            xln = prob[:, :, :].rearrange("p a (t d) -> p (a t) d", d=D)
            for t in range(TILES):
                dve.tensor_scalar(xln[:, t, :], res[:, t, :], ag[:, t, 0:1], rs[:, 2, t:t + 1], ALU.subtract, ALU.mult)\
                   .then_inc(s["ln_x"], 1)
            dve.wait_ge(s["x_init"], CR + TILES // 4)
            dve.sem_inc(s["x_new"], NC)

            def add_out(it, i):
                tile = (it // KV) * NT + i
                r = res[:, bass.ds(tile, 1), :].rearrange("p a d -> p (a d)")
                dve.wait_ge(s["lo_mm"], CR + it * NT + i + 1)
                dve.tensor_tensor(r, bk(7)[:, 0:D], r, ALU.add).then_inc(s["lo_add"], 1)

            with dve.Fori(0, B * KV) as it:
                def peak(j):
                    i, h = bodies[j]
                    J = it * len(bodies) + j
                    n = (i + 1) * P
                    S = two(2 * (j % 2))
                    dve.wait_ge(s["ls_mm"], CR + J + 1)
                    dve.tensor_tensor(S[:, i * P:n], S[:, i * P:n], caus, ALU.min).then_inc(s["ls_cap"], 1)
                    dve.wait_ge(s["ls_cap"], CR + J + 1)
                    dve.reduce_max(gst[:, 4 + j % 2:5 + j % 2], S[:, 0:n], AXX).then_inc(s["ls_max"], 1)
                    dve.wait_ge(s["ls_max"], CR + J + 1)
                    dve.tensor_scalar(gst[:, 8 + j % 2:9 + j % 2], gst[:, 4 + j % 2:5 + j % 2], -G_SCALE, None, ALU.mult)\
                       .then_inc(s["ls_neg"], 1)

                def normalise(j):
                    J = it * len(bodies) + j
                    n = (bodies[j][0] + 1) * P
                    dve.wait_ge(s["ls_exp"], CR + J + 1)
                    dve.reciprocal(gst[:, 16 + j % 2:17 + j % 2], gst[:, 12 + j % 2:13 + j % 2]).then_inc(s["ls_rec"], 1)
                    dve.wait_ge(s["ls_rec"], CR + J + 1)
                    dve.tensor_scalar(gp[:, j % 2, 0:n], gp[:, j % 2, 0:n], gst[:, 16 + j % 2:17 + j % 2], None, ALU.mult)\
                       .then_inc(s["ls_nrm"], 1)

                peak(0)
                for j in range(len(bodies)):
                    if j + 1 < len(bodies):
                        peak(j + 1)
                    normalise(j)
                    i, h = bodies[j]
                    if h == 0 and i:
                        add_out(it, i - 1)
                add_out(it, NT - 1)

            with dve.Fori(0, DEPTH) as layer:
                dve.wait_ge(w_in, layer * 16 + 16)
                dve.wait_ge(tab_in, layer * 128 + 128)
                dve.tensor_scalar(parv[:, V_NKA:V_NKA + 1], parv[:, V_QB:V_QB + 1], -1.0, None, ALU.mult).then_inc(s["tab_sc"], 1)
                dve.tensor_scalar(parv[:, V_NKB:V_NKB + 1], parv[:, V_KB:V_KB + 1], -1.0, None, ALU.mult).then_inc(s["tab_sc"], 1)
                dve.wait_ge(s["tab_sc"], CR + layer * 10 + 2)
                for kind in range(2):
                    for fn in range(2):
                        for hf in range(2):
                            v = (V_QA, V_KA)[kind] if hf == 0 else ((V_QB, V_KB) if fn == 0 else (V_NKA, V_NKB))[kind]
                            dve.tensor_scalar(tabs[:, kind, fn, hf, :], tabs[:, kind, fn, hf, :], parv[:, v:v + 1], None,
                                              ALU.mult).then_inc(s["tab_sc"], 1)
                dve.wait_ge(s["tab_sc"], CR + layer * 10 + 10)

                def rotate(G, GK, n, par_, u):
                    kind = u // 2
                    tb = tabs[:, kind, :, :, bass.ds((n % NT) * P, P)]
                    src = bk(u % 2).rearrange("p (g a t) -> p g a t", g=2, a=2)
                    dve.wait_ge(s["u_sq"], CR + G * 4 + u + 1)
                    if u < 2:
                        dve.wait_ge(s["s_mm"], CR + G - 1)
                        dst = qr[:, par_, 4 * u:4 * u + 4, :]
                    else:
                        dve.wait_ge(kd_in[1 - par_], CR + (GK + par_) * 64)
                        dst = kr[:, 4 * (u - 2):4 * (u - 2) + 4, :]
                    dst = dst.rearrange("p (g a) t -> p g a t", g=2)
                    for g in range(2):
                        ins = dve.tensor_tensor(dst[:, g, :, :], src[:, g, :, :], tb[:, 0, :, :], ALU.mult)
                    ins.then_inc(s["u_c"], 1)
                    dve.wait_ge(s["u_rot"], CR + G * 4 + u - 1)
                    sw = swp[:, u % 2, :].rearrange("p (g a t) -> p g a t", g=2, a=2)[:, :, ::-1, :]
                    for g in range(2):
                        ins = dve.tensor_tensor(sw[:, g, :, :], src[:, g, :, :], tb[:, 1, :, :], ALU.mult)
                    ins.then_inc(s["u_s"], 1)

                def slot(layer, k, par_, a, b, c):
                    n = k * 2 + par_
                    G, GK = layer * TILES + n, layer * (TILES // 2) + k
                    sm = prob[:, 1 - par_, :]
                    sm3 = sm.rearrange("p (h k) -> p h k", h=LH)
                    if a:
                        rotate(G, GK, n, par_, 0)
                        rotate(G, GK, n, par_, 1)
                    if b:
                        dve.wait_ge(s["s_mm"], CR + G)
                        dve.wait_ge(s["pt_mm"], CR + G * 2 - 4)
                        dve.wait_ge(s["rqT_cp"], CR + G)
                        dve.tensor_tensor(sm3, scores_ps,
                                          rq8[:, 1 - par_, :].rearrange("p (h o) -> p h o", o=1).to_broadcast([P, LH, 64]),
                                          ALU.mult).then_inc(s["s_rq"], 1)
                    if a:
                        rotate(G, GK, n, par_, 2)
                        rotate(G, GK, n, par_, 3)
                    if b:
                        cap = cst[:, bass.ds(((n - 1) % NT) * 64 + C_CAP, 64)]
                        dve.wait_ge(s["s_rq"], CR + G)
                        dve.tensor_tensor(sm3, sm3, cap.rearrange("p (o k) -> p o k", o=1).to_broadcast([P, LH, 64]),
                                          ALU.min).then_inc(s["s_cap"], 1)
                        dve.wait_ge(s["s_cap"], CR + G)
                        dve.reduce_max(nmax[:, :], sm3, AXX).then_inc(s["s_max"], 1)
                        dve.wait_ge(s["s_max"], CR + G)
                        dve.tensor_tensor(sm3, sm3, nmax[:, :].rearrange("p (h o) -> p h o", o=1).to_broadcast([P, LH, 64]),
                                          ALU.subtract).then_inc(s["s_sub"], 1)
                    if c:
                        dve.wait_ge(s["pv_mm"], CR + G - 1)
                        dve.wait_ge(s["s_inv"], CR + G - 1)
                        dve.tensor_tensor(osb[:, :, :], outputs_ps,
                                          den[:, par_, :].rearrange("p (h o) -> p h o", o=1).to_broadcast([P, LH, LD]),
                                          ALU.mult).then_inc(s["o_nrm"], 1)
                    if a:
                        dve.wait_ge(s["ssT_mm"], CR + G + 1)
                        dve.wait_ge(s["rk_cp"], CR + G)
                        dve.tensor_scalar(rs[:, 0, :].rearrange("p (g h) -> p g h", g=2 * NG),
                                          bk(2)[:, 0:2 * P].rearrange("p (g h) -> p g h", g=2 * NG)[:, :, 0:4], 1e-24, None,
                                          ALU.max).then_inc(s["ss_cl"], 1)
                        dve.wait_ge(s["ss_cl"], CR + G + 1)
                        rsqrt(rs, 2 * LH, "rs_n", CR + G * 11)
                        dve.tensor_scalar(rq8[:, par_, :], rs[:, 2, 0:LH], QK_SCALE, None, ALU.mult).then_inc(s["rqT_cp"], 1)
                    if b:
                        dve.wait_ge(s["s_exp"], CR + G)
                        dve.reduce_sum(den[:, 1 - par_, :], sm3, AXX).then_inc(s["s_sum"], 1)
                        dve.wait_ge(s["s_sum"], CR + G)
                        dve.reciprocal(den[:, 1 - par_, :], den[:, 1 - par_, :]).then_inc(s["s_inv"], 1)
                    if a:
                        dve.wait_ge(s["rkb_mm"], CR + G + 1)
                        dve.wait_ge(s["u_rot"], CR + G * 4 + 4)
                        rk = bk(2).rearrange("p (g o t) -> p g o t", g=NG, o=1)
                        for i in range(2):
                            k4 = kr[:, 4 * i:4 * i + 4, :].rearrange("p (g a) t -> p g a t", g=2)
                            dve.tensor_tensor(k4, rk[:, 2 * i:2 * i + 2, :, :].to_broadcast([P, 2, 2, P]), k4, ALU.mult)\
                               .then_inc(s["k_nrm"], 1)
                    if c:
                        dve.wait_ge(s["wo_mm"], CR + G - 1)
                        at = column(n - 2) + 1
                        dve.tensor_tensor(X1f[:, bass.ds(at, P)], bk(6)[:, 0:P], Xf[:, bass.ds(at, P)], ALU.add)\
                           .then_inc(s["wo_add"], 1)

                slots(dve, layer, slot)

                def shifted(c):
                    F = layer * NC + c
                    b, t0 = divmod(c * CH, T)
                    dve.wait_ge(s["wo_add"], CR + layer * TILES + TILES)
                    dve.wait_ge(s["f_mu"], CR + F)
                    dve.tensor_copy(fs[0:64, :], X1[0:64, b, 1 + t0:1 + t0 + CH]).then_inc(s["f_cp"], 1)
                    dve.tensor_copy(fs[64:128, :], X1[64:128, b, t0:t0 + CH]).then_inc(s["f_cp"], 1)

                def variance(c):
                    F = layer * NC + c
                    dve.wait_ge(s["f_var"], CR + F + 1)
                    dve.wait_ge(s["f_re"], CR + F)
                    dve.tensor_scalar(fr[:, 0, 0:4], bk(7)[:, 0:4], 1e-5, None, ALU.add).then_inc(s["f_eps"], 1)
                    dve.wait_ge(s["f_eps"], CR + F + 1)
                    rsqrt(fr, 4, "rs_f", CR + F * 11)

                def affine(c):
                    F = layer * NC + c
                    dve.wait_ge(s["f_rb"], CR + F + 1)
                    dve.tensor_tensor(xn[:, :], bk(7), xc[:, :], ALU.mult).then_inc(s["f_xn"], 1)
                    dve.wait_ge(s["f_xn"], CR + F + 1)
                    dve.tensor_scalar(xn[:, :], xn[:, :], parv[:, V_G:V_G + 1], parv[:, V_B:V_B + 1], ALU.mult, ALU.add)\
                       .then_inc(s["f_aff"], 1)

                def gated(c, j):
                    F = layer * NC + c
                    m = FJ[j][1]
                    dve.wait_ge(s["f_a"], CR + F * 3 + j + 1)
                    dve.wait_ge(s["f_gl"], CR + F * 3 + j + 1)
                    dve.wait_ge(s["f_out_mm"], CR + F)
                    dve.scalar_tensor_tensor(hb[j][0:m, :], bk(j % 2)[0:m, :], parv[0:m, V_B1A + j:V_B1A + j + 1],
                                             gl[j][0:m, :], ALU.add, ALU.mult).then_inc(s["f_h"], 1)

                shifted(0)
                variance(0)
                affine(0)
                for c in range(NC):
                    F = layer * NC + c
                    more = c + 1 < NC
                    if more:
                        shifted(c + 1)
                    gated(c, 0)
                    gated(c, 1)
                    if more:
                        variance(c + 1)
                    gated(c, 2)
                    if more:
                        affine(c + 1)
                    b, t0 = divmod(c * CH, T)
                    dve.wait_ge(s["f_out_mm"], CR + F + 1)
                    dve.wait_ge(s["xs_cp"], CR + (layer + 1) * TILES * 2)
                    dve.scalar_tensor_tensor(X[:, b, 1 + t0:1 + t0 + CH], bk(5 + c % 2), parv[:, V_B2:V_B2 + 1],
                                             X1[:, b, 1 + t0:1 + t0 + CH], ALU.add, ALU.add).then_inc(s["x_new"], 1)

            for g4 in range(TILES // 4):
                dve.wait_ge(s["fin_mm"], CR + g4 + 1)
                r4 = res[:, 4 * g4:4 * g4 + 4, :]
                dve.tensor_tensor(r4, bk(g4 % 2).rearrange("p (t d) -> p t d", t=4), r4, ALU.add).then_inc(s["fin_add"], 1)

        @block.tensor
        def _(pe):
            credit(pe, "pe")
            def mm(o, l, r, start=True, stop=True):
                return pe.matmul(o, l, r, start=start, stop=stop)

            pe.wait_ge(c_in, 16)
            xln = prob[:, :, :].rearrange("p a (t d) -> p (a t) d", d=D)
            for g4 in range(TILES // 4):
                if g4 >= 2:
                    pe.wait_ge(s["x_init"], CR + g4 - 1)
                pe.wait_ge(s["ln_x"], CR + 4 * g4 + 4)
                for k in range(4):
                    ins = pe.transpose(bk(g4 % 2)[:, P * k:P * k + P], xln[:, 4 * g4 + k, :], ident)
                ins.then_inc(s["ln_xT"], 1)
            pe.wait_ge(lat_w, 48)
            for kv in range(KV):
                for h in range(REP):
                    ins = mm(bk(2)[32 * h:32 * h + 32, D * kv:D * kv + D], gwvu, gwo[:, kv * REP + h, :])
                ins.then_inc(s["wvo_mm"], 1)
            with pe.Fori(0, B * KV) as it:
                pe.wait_ge(lat_wq, it * 48 + 48)
                pe.wait_ge(s["lx_cp"], CR + it + 1)
                pe.wait_ge(s["wvo_cp"], CR + 1)
                pe.wait_ge(s["ls_exp"], CR + it * len(bodies))
                for i in range(8):
                    if i >= 2:
                        pe.wait_ge(s["lq_cp"], CR + it * 8 + i - 1)
                    mm(bk(i % 2), gwq[:, P * (i // 2):P * (i // 2) + P], gx[:, 512 * (i % 2):512 * (i % 2) + 512])\
                        .then_inc(s["lq_mm"], 1)
                for i in range(2):
                    ins = mm(bk(2 + i)[0:LAT, :], gwk, gx[:, 512 * i:512 * (i + 1)])
                ins.then_inc(s["lk_mm"], 1)
                pe.wait_ge(s["lt_cp"], CR + it * NTR)
                pe.wait_ge(s["lkl_cp"], CR + it * 2 + 1)
                for i in range(2):
                    ins = mm(bk(4 + i), gwku, gkl[:, 512 * i:512 * (i + 1)])
                ins.then_inc(s["lkk_mm"], 1)
                pe.wait_ge(s["ly_cp"], CR + it * NT)
                for t in range(NT):
                    ins = mm(bk(6)[:, LAT * t:LAT * t + LAT], gx[:, P * t:P * t + P], gwv)
                ins.then_inc(s["lvl_mm"], 1)
                pe.wait_ge(s["lq_cp"], CR + it * 8 + 8)
                pe.wait_ge(s["lkl_cp"], CR + it * 2 + 2)

                def scores(j):
                    i, h = bodies[j]
                    n = (i + 1) * P
                    if j >= 2:
                        pe.wait_ge(s["ls_exp"], CR + it * len(bodies) + j - 1)
                    for k in range(0, n, 512):
                        w = min(512, n - k)
                        ins = mm(two(2 * (j % 2))[:, k:k + w], gq[:, h, P * i:P * i + P], gk[:, k:k + w])
                    ins.then_inc(s["ls_mm"], 1)

                def finish(j):
                    i, h = bodies[j]
                    pe.wait_ge(s["ls_nrm"], CR + it * len(bodies) + j + 1)
                    for g in range(groups(i)):
                        k = done_groups(j) + g
                        if k >= 2:
                            pe.wait_ge(s["lt_cp"], CR + it * NTR + k - 1)
                        for q in range(min(4, i + 1 - 4 * g)):
                            kb = 4 * g + q
                            ins = pe.transpose(bk(4 + k % 2)[:, P * q:P * q + P], gp[:, j % 2, P * kb:P * kb + P], ident)
                        ins.then_inc(s["lt_mm"], 1)
                    if h == REP - 1:
                        pe.wait_ge(s["lt_cp"], CR + it * NTR + done_groups(j + 1))
                        pe.wait_ge(s["lvl_cp"], CR + it + 1)
                        pe.wait_ge(s["ly_cp"], CR + it * NT + i)
                        for kb in range(i + 1):
                            for hh in range(REP):
                                ins = mm(bk(6)[32 * hh:32 * hh + 32, 256:256 + P], gvl[:, kb, :], gpt[:, hh, kb, :],
                                         kb == 0, kb == i)
                        ins.then_inc(s["ly_mm"], 1)

                def project(i):
                    pe.wait_ge(s["ly_cp"], CR + it * NT + i + 1)
                    pe.wait_ge(s["lo_add"], CR + it * NT + i)
                    mm(bk(7)[:, 0:D], gy, gvo[:, bass.ds(it % KV, 1), :].rearrange("p a n -> p (a n)")).then_inc(s["lo_mm"], 1)

                scores(0)
                for j in range(len(bodies)):
                    if j + 1 < len(bodies):
                        scores(j + 1)
                    finish(j)
                    i, h = bodies[j]
                    if h == 0 and i:
                        project(i - 1)
                project(NT - 1)

            pe.wait_ge(s["zeroed"], CR + 7)
            pe.wait_ge(s["lo_add"], CR + B * KV * NT)
            with pe.Fori(0, DEPTH) as layer:
                def unit(G, par_, u):
                    if u < 2:
                        pe.wait_ge(s["v_cp"], CR + G * 2 + 1 + u)
                    else:
                        pe.wait_ge(s["u_s"], CR + G * 4 + u - 1)
                    for j in range(4):
                        w = Wqkv[:, (4 * u + j) * P:(4 * u + j + 1) * P]
                        ins = mm(bk(u % 2)[:, P * j:P * j + P], w, xs[:, par_, :])
                    ins.then_inc(s["u_mm"], 1)

                def square_sums(G, u):
                    if u == 0:
                        pe.wait_ge(s["k_nrm"], CR + G * 2)
                    pe.wait_ge(s["u_sq"], CR + G * 4 + u + 1)
                    for gg in range(2):
                        g = 2 * (u % 2) + gg
                        for a_ in range(2):
                            ins = mm(bk(2)[32 * g:32 * g + 32, P * (u // 2):P * (u // 2) + P], ones4,
                                     sq[:, u % 2, P * (2 * gg + a_):P * (2 * gg + a_ + 1)], a_ == 0, a_ == 1)
                    ins.then_inc(s["ss_mm"], 1)

                def slot(layer, k, par_, a, b, c):
                    n = k * 2 + par_
                    G, GK = layer * TILES + n, layer * (TILES // 2) + k
                    if a:
                        pe.wait_ge(s["xs_cp"], CR + G * 2 + 2)
                        for i in range(2):
                            pe.wait_ge(s["u_s"], CR + G * 4 - 1 + i)
                            mm(bk(i), xs[:, par_, :], Wqkv[:, 2048 + 512 * i:2048 + 512 * (i + 1)]).then_inc(s["v_mm"], 1)
                        unit(G, par_, 0)
                        unit(G, par_, 1)
                    if c:
                        pe.wait_ge(s["s_exp"], CR + G - 1)
                        pe.wait_ge(s["ot_cp"], CR + G * 2 - 4)
                        pe.wait_ge(s["wo_add"], CR + G - 2)
                        for i in range(2):
                            for k in range(4):
                                ins = pe.transpose(bk(5 + i)[:, P * k:P * k + P],
                                                   prob[:, par_, P * (4 * i + k):P * (4 * i + k + 1)], ident)
                            ins.then_inc(s["pt_mm"], 1)
                    if b:
                        q = 1 - par_
                        pe.wait_ge(kd_in[q], CR + (GK + par_) * 64)
                        pe.wait_ge(s["u_rot"], CR + G * 4)
                        pe.wait_ge(s["s_rq"], CR + G - 1)
                        for g in range(NG):
                            half = bk(3 + g // 2)[:, 256 * (g % 2):256 * (g % 2) + 256].rearrange("p (h k) -> p h k", h=4)
                            for a_ in range(2):
                                j = 2 * g + a_
                                for w in range(NW):
                                    o = half[32 * w:32 * w + 32, :, :]
                                    l = qr[:, q, j, 32 * w:32 * w + 32]
                                    if w:
                                        ins = mm(o, l, kd[q][:, j, :, 32 * w - 32:32 * w + 32], a_ == 0, a_ == 1)
                                    else:
                                        pe.matmul(o[:, :, 0:32], l, kd[1 - q][:, j, :, 96:128], start=a_ == 0,
                                                  stop=a_ == 1, skip_group_check=True)
                                        ins = pe.matmul(o[:, :, 32:64], l, kd[q][:, j, :, 0:32], start=False,
                                                        stop=a_ == 1, skip_group_check=True)
                        ins.then_inc(s["s_mm"], 1)
                    if a:
                        square_sums(G, 0)
                        square_sums(G, 1)
                        unit(G, par_, 2)
                        unit(G, par_, 3)
                    if c:
                        pe.wait_ge(vd_in[par_], CR + GK * 256)
                        for i in range(2):
                            pe.wait_ge(s["pt_cp"], CR + (G - 2) * 2 + i + 1)
                            for k in range(4):
                                for w in range(NW):
                                    pr = 4 * i + k
                                    rhs = vd[par_][:, w, :, 64 * pr:64 * pr + 64]
                                    ins = mm(bk(5 + i)[32 * w:32 * w + 32, P * k:P * k + P].rearrange("p (o d) -> p o d", o=2),
                                             ptile[:, pr, 32 * w:32 * w + 32], rhs)
                        ins.then_inc(s["pv_mm"], 1)
                    if a:
                        square_sums(G, 2)
                        square_sums(G, 3)
                    if c:
                        pe.wait_ge(s["o_nrm"], CR + G - 1)
                        for i in range(2):
                            for k in range(4):
                                pr = 4 * i + k
                                ins = pe.transpose(bk(7 - 2 * i)[:, P * k:P * k + P],
                                                   osb[:, 2 * pr:2 * pr + 2, :].rearrange("p a d -> p (a d)"), ident)
                            ins.then_inc(s["ot_mm"], 1)
                    if a:
                        pe.wait_ge(s["ss_cp"], CR + G + 1)
                        pe.transpose(bk(2)[:, 0:P], ssc[:, 0:P], ident)
                        pe.transpose(bk(2)[:, P:2 * P], ssc[:, P:2 * P], ident).then_inc(s["ssT_mm"], 1)
                    if c:
                        pe.wait_ge(s["ot_cp"], CR + (G - 1) * 2)
                        for k in range(NP):
                            ins = mm(bk(6)[:, 0:P], Wo[:, k, :], otile[:, k, :], k == 0, k == NP - 1)
                        ins.then_inc(s["wo_mm"], 1)
                    if a:
                        pe.wait_ge(s["rk_cp"], CR + G + 1)
                        for g in range(NG):
                            ins = pe.transpose(bk(2)[:, P * g:P * g + P], rke[:, g, :, :].rearrange("p h r -> p (h r)"), ident)
                        ins.then_inc(s["rkb_mm"], 1)

                pe.wait_ge(qkvw_in, layer * 32 + 32)
                slots(pe, layer, slot)

                def mean(c):
                    F = layer * NC + c
                    pe.wait_ge(s["f_cp"], CR + F * 2 + 2)
                    if c == 0:
                        pe.wait_ge(s["k_nrm"], CR + (layer + 1) * TILES * 2)
                        pe.wait_ge(ffw_in, layer * 32 + 32)
                    else:
                        pe.wait_ge(s["f_sq"], CR + F)
                    mm(bk(2), centre, fs[:, :]).then_inc(s["f_mu"], 1)

                def var(c):
                    F = layer * NC + c
                    pe.wait_ge(s["f_sq"], CR + F + 1)
                    if c == 0:
                        pe.wait_ge(s["ot_cp"], CR + (layer + 1) * TILES * 2)
                    else:
                        pe.wait_ge(s["f_xn"], CR + F)
                    for k in range(4):
                        ins = mm(bk(7)[:, k:k + 1], fsq[:, P * k:P * k + P], meanw)
                    ins.then_inc(s["f_var"], 1)

                def rstd_rows(c):
                    F = layer * NC + c
                    pe.wait_ge(s["f_re"], CR + F + 1)
                    for k in range(4):
                        ins = pe.transpose(bk(7)[:, P * k:P * k + P], fre[:, k, :], ident)
                    ins.then_inc(s["f_rb"], 1)

                def up(c, j):
                    F = layer * NC + c
                    j0, m = FJ[j]
                    pe.wait_ge(s["f_aff"], CR + F + 1)
                    if c == 0 and j < 2:
                        pe.wait_ge(s["u_s"], CR + (layer + 1) * TILES * 4)
                        pe.wait_ge(s["s_rq"], CR + (layer + 1) * TILES)
                    pe.wait_ge(s["f_h"], CR + F * 3 + (j - 1 if j == 2 else 0))
                    mm(bk(3 + j % 2)[0:m, :], W1[:, FF + j0:FF + j0 + m], xn[:, :]).then_inc(s["f_g"], 1)
                    mm(bk(j % 2)[0:m, :], W1[:, j0:j0 + m], xn[:, :]).then_inc(s["f_a"], 1)

                mean(0)
                var(0)
                rstd_rows(0)
                for c in range(NC):
                    F = layer * NC + c
                    more = c + 1 < NC
                    if more:
                        mean(c + 1)
                    up(c, 0)
                    up(c, 1)
                    if more:
                        var(c + 1)
                    up(c, 2)
                    if more:
                        rstd_rows(c + 1)
                    if c == 0:
                        pe.wait_ge(s["wo_add"], CR + (layer + 1) * TILES)
                        pe.wait_ge(s["ot_cp"], CR + (layer + 1) * TILES * 2)
                    if c >= 2:
                        pe.wait_ge(s["x_new"], CR + NC + F - 1)
                    for j, (j0, m) in enumerate(FJ):
                        pe.wait_ge(s["f_h"], CR + F * 3 + j + 1)
                        ins = mm(bk(5 + c % 2), W2[0:m, j, :], hb[j][0:m, :], j == 0, j == 2)
                    ins.then_inc(s["f_out_mm"], 1)
                pe.wait_ge(s["x_new"], CR + NC + layer * NC + NC)

            for g4 in range(TILES // 4):
                if g4 >= 2:
                    pe.wait_ge(s["fin_add"], CR + g4 - 1)
                b, t0 = divmod(4 * g4, NT)
                for k in range(4):
                    ins = pe.transpose(bk(g4 % 2)[:, P * k:P * k + P], X[:, b, 1 + P * (t0 + k):1 + P * (t0 + k + 1)], ident)
                ins.then_inc(s["fin_mm"], 1)


_OUT = ("out_0_dram", (B, T, D))


def kernel(L0_attn_x, L0_attn_wq, L0_attn_wk_down, L0_attn_wv_down, L0_attn_wk_up, L0_attn_wv_up, L0_attn_wo,
           L0_ffn_Wqkv, L0_ffn_q_scale, L0_ffn_k_scale, L0_ffn_Wo, L0_ffn_ln_g, L0_ffn_ln_b, L0_ffn_W1, L0_ffn_b1,
           L0_ffn_W2, L0_ffn_b2):
    import concourse.bacc as bacc
    from concourse.bass_utils import run_bass_kernel_spmd

    a = np.asarray
    w = a(L0_ffn_Wqkv).reshape(DEPTH, D, 3, NG, 4, 2, HALF)
    qk = w[:, :, 0:2].transpose(0, 1, 2, 3, 5, 4, 6).reshape(DEPTH, D, -1)
    v = a(L0_ffn_Wqkv)[:, :, 2 * LH * LD:].reshape(DEPTH, D, NP, 2, LD).transpose(0, 1, 3, 2, 4).reshape(DEPTH, D, -1)
    w2 = np.zeros((DEPTH, 3 * P, D), np.float32)
    w2[:, :FF] = a(L0_ffn_W2)
    par = np.zeros((DEPTH, P, V_N), np.float32)
    for col, src, half in ((V_QA, L0_ffn_q_scale, 0), (V_QB, L0_ffn_q_scale, 1), (V_KA, L0_ffn_k_scale, 0),
                           (V_KB, L0_ffn_k_scale, 1)):
        par[:, :, col] = np.tile(a(src)[:, HALF * half:HALF * (half + 1)], (1, 4))
    par[:, :, V_G], par[:, :, V_B], par[:, :, V_B2] = a(L0_ffn_ln_g), a(L0_ffn_ln_b), a(L0_ffn_b2)
    for j, (j0, m) in enumerate(FJ):
        par[:, 0:m, V_B1A + j] = a(L0_ffn_b1)[:, j0:j0 + m]
        par[:, 0:m, V_B1G + j] = a(L0_ffn_b1)[:, FF + j0:FF + j0 + m]
    cst, tabs = shape_constants()
    ins = {
        "x": a(L0_attn_x),
        "wq": a(L0_attn_wq).reshape(D, KV, REP * GD).transpose(1, 0, 2),
        "wkd": a(L0_attn_wk_down).reshape(D, KV, LAT).transpose(1, 0, 2),
        "wvd": a(L0_attn_wv_down).reshape(D, KV, LAT).transpose(1, 0, 2),
        "wku": a(L0_attn_wk_up),
        "wvuT": a(L0_attn_wv_up).T,
        "wo": a(L0_attn_wo),
        "wqkv": np.concatenate([qk, v], axis=2),
        "lwo": a(L0_ffn_Wo),
        "w1": a(L0_ffn_W1),
        "w2": w2.reshape(DEPTH, 3, P, D).transpose(0, 2, 1, 3),
        "par": par,
        "cst": cst,
        "tab": tabs,
    }
    nc = bacc.Bacc("TRN2", target_bir_lowering=False, num_devices=1)
    arrays, args = {}, []
    for name, arr in ins.items():
        arr = np.ascontiguousarray(arr)
        arrays[f"in_{name}_dram"] = arr
        args.append(nc.dram_tensor(f"in_{name}_dram", arr.shape, mybir.dt.from_np(arr.dtype), kind="ExternalInput").ap())
    args.append(nc.dram_tensor(_OUT[0], _OUT[1], F32, kind="ExternalOutput").ap())
    build(nc, *args)
    r = run_bass_kernel_spmd(nc, [arrays], core_ids=[0])
    return r.results[0][_OUT[0]]
```

```python
from contextlib import ExitStack

import numpy as np

import concourse.bass as bass
from concourse import mybir

F32 = mybir.dt.float32
ALU = mybir.AluOpType
ACT = mybir.ActivationFunctionType
AXX = mybir.AxisListType.X

P = 128
B, T, D = 2, 1024, 128
NT = T // P
TILES = B * NT
GH, KV, GD, LAT = 8, 2, 128, 32
REP = GH // KV
G_SCALE = float(GD) ** -0.5
DEPTH, LH, LD, WIN = 6, 16, 64, 32
HALF = LD // 2
NG = LH // 4
NP = LH // 2
NW = P // WIN
QK_SCALE = 8.0
FF = int(D * 4 * 2 / 3)
FJ = [(0, 128), (128, 128), (256, FF - 256)]
CH = 512
NC = B * T // CH
CR = 8
NEG = -1.0e30

C_ID, C_CEN, C_CAUS, C_ONE, C_CAP, C_MEAN = 0, 128, 256, 384, 416, 416 + 64 * NT
C_N = C_MEAN + 1
(V_QA, V_QB, V_KA, V_KB, V_G, V_B, V_B1A, V_B1G, V_B2) = 0, 1, 2, 3, 4, 5, 6, 9, 12
V_N = 13


def shape_constants():
    c = np.zeros((P, C_N), np.float32)
    i = np.arange(P)
    c[:, C_ID:C_ID + P] = np.eye(P)
    c[:, C_CEN:C_CEN + P] = np.eye(P) - 1.0 / D
    c[:, C_MEAN] = 1.0 / D
    c[:, C_CAUS:C_CAUS + P] = np.where(i[None, :] <= i[:, None], 3.0e38, NEG)
    c[i, C_ONE + i // 32] = 1.0
    r, k = i[:, None] % WIN, np.arange(2 * WIN)[None, :]
    inside = (k >= r) & (k <= r + WIN)
    for n in range(NT):
        ok = inside & ((i[:, None] >= WIN) | (k >= WIN)) if n == 0 else inside
        c[:, C_CAP + 64 * n:C_CAP + 64 * (n + 1)] = np.where(ok, 3.0e38, NEG)
    f = np.float32
    half = np.arange(0, LD, 2, dtype=f)
    inv_freq = f(1.0) / np.power(f(10000.0), half / f(LD))
    t = np.arange(T, dtype=f)
    freqs = t[:, None] * inv_freq[None, :]
    base = (half + f(0.4 * LD)) / f(1.4 * LD)
    power = (t - f(T // 2)) / f(WIN // 2)
    scale = np.power(base[None, :], power[:, None])
    cos, sin = np.cos(freqs), np.sin(freqs)
    tabs = [cos * scale, sin * scale, -sin * scale, cos / scale, sin / scale, -sin / scale]
    tabs = np.stack([np.tile(x.T, (4, 1)) for x in tabs]).astype(f)
    return c, np.ascontiguousarray(tabs)


def build(nc, x, wq, wkd, wvd, wku, wvuT, wo, wqkv, lwo, w1, w2, par, cst_d, tab_d, out):
    ctx = ExitStack()
    with ctx:
        def sb(name, shape):
            return ctx.enter_context(nc.sbuf_tensor(name, shape, F32))

        def sem(name):
            return ctx.enter_context(nc.semaphore(name))

        cst = sb("cst", [P, C_N])
        parv = sb("parv", [P, V_N])
        scales = sb("scales", [P, 4])
        Wqkv = sb("Wqkv", [P, 3 * LH * LD])
        Wo = sb("Wo", [P, NP, D])
        W1 = sb("W1", [P, 2 * FF])
        W2 = sb("W2", [P, 3, D])
        tabs = sb("tabs", [P, 2, 2, 2, T])
        ident = cst[:, C_ID:C_ID + P]
        centre = cst[:, C_CEN:C_CEN + P]
        meanw = cst[:, C_MEAN:C_MEAN + 1]
        caus = cst[:, C_CAUS:C_CAUS + P]
        ones4 = cst[:, C_ONE:C_ONE + 32]

        X = sb("X", [P, B, T + 1])
        X1 = sb("X1", [P, B, T + 1])
        res = sb("res", [P, TILES, D])
        arena = sb("arena", [P, 4 * 4096])
        kd = [arena[:, 4096 * i:4096 * (i + 1)].rearrange("p (j h t) -> p j h t", j=2 * NG, h=4)
              for i in range(2)]
        vd = [arena[:, 8192 + 4096 * i:8192 + 4096 * (i + 1)]
              .rearrange("p (w o n) -> p w o n", w=NW, o=2) for i in range(2)]
        vs = sb("vs", [P, 2, LH * LD])
        xs = sb("xs", [P, 2, P])
        qr = sb("qr", [P, 2 * NG, P])
        kr = sb("kr", [P, 2 * NG, P])
        sq = sb("sq", [P, 2, CH])
        swp = sb("swp", [P, 2, CH])
        ssc = sb("ssc", [P, 2 * P])
        rs = sb("rs", [P, 4, 2 * LH])
        rke = sb("rke", [P, NG, 4, HALF])
        rq8 = sb("rq8", [P, LH])
        prob = sb("prob", [P, 2, LH * 64])
        nmax = sb("nmax", [P, LH])
        den = sb("den", [P, LH])
        ptile = sb("ptile", [P, NP, P])
        osb = sb("osb", [P, LH, LD])
        otile = sb("otile", [P, NP, P])
        fs = sb("fs", [P, CH])
        xc = sb("xc", [P, CH])
        fsq = sb("fsq", [P, CH])
        fr = sb("fr", [P, 4, NT])
        fre = sb("fre", [P, 4, P])
        xn = sb("xn", [P, CH])
        gl = [sq[:, 0, :], sq[:, 1, :], kr[:, 0:4, :].rearrange("p a b -> p (a b)")]
        hb = [swp[:, 0, :], swp[:, 1, :], kr[:, 4:8, :].rearrange("p a b -> p (a b)")]
        gq = arena[:, 0:4096].rearrange("p (h t) -> p h t", h=REP)
        gk = arena[:, 4096:5120]
        gx = arena[:, 5120:6144]
        gpt = arena[:, 6144:10240].rearrange("p (h k t) -> p h k t", h=REP, k=NT)
        gwo = arena[:, 10240:11264].rearrange("p (h n) -> p h n", h=GH)
        gkl = arena[0:LAT, 11264:12288]
        gwq = arena[:, 12288:12800]
        gwk = arena[:, 12800:12832]
        gwv = arena[:, 12832:12864]
        gwku = arena[0:LAT, 12864:12992]
        gwvu = arena[:, 12992:13024]
        gvo = arena[:, 13056:13312].rearrange("p (k n) -> p k n", k=KV)
        gvl = arena[:, 13312:13568].rearrange("p (t n) -> p t n", t=NT)
        gy = arena[:, 13568:13696]
        gp = prob
        gst = ssc

        banks = ctx.enter_context(nc.psum_tensor("banks", [P, 8 * 512], F32))

        def bk(i):
            return banks[:, 512 * i:512 * i + 512]

        def two(i):
            return banks[:, 512 * i:512 * i + 1024]

        scores_ps = two(3).rearrange("p (h k) -> p h k", h=LH)
        outputs_ps = two(5).rearrange("p (h d) -> p h d", h=LH)

        counted = {
            "pe": ("ln_xT wvo_mm lq_mm lk_mm lkk_mm lvl_mm ls_mm lt_mm ly_mm lo_mm v_mm u_mm ss_mm qs_mm ssT_mm "
                   "rkb_mm s_mm pt_mm pv_mm ot_mm wo_mm f_mu f_rb f_var f_a f_g f_out_mm fin_mm").split(),
            "act": ("xs_cp x_init wvo_cp lx_cp lq_cp lkl_cp lvl_cp ls_exp lt_cp ly_cp v_cp u_sq s_exp pt_cp ot_cp ss_cp qs_cp rk_cp f_re f_xc "
                   "f_sq f_gl").split(),
            "dve": ("lo_add st_bn st_ag st_eps ln_x ls_cap ls_max ls_neg ls_rec ls_nrm u_c u_s rs_0 rs_n rs_f ss_cl rqT_cp k_nrm "
                   "s_cap s_max s_sum s_inv o_nrm wo_add zeroed_v f_cp f_eps f_xn f_aff f_h x_new "
                   "fin_add").split(),
            "pool": ("zeroed tab_sc u_rot s_sub s_rq").split(),
        }
        s = {n: sem(n) for v in counted.values() for n in v}

        def credit(eng, name):
            for n in counted[name]:
                eng.sem_inc(s[n], CR)
        c_in, w_in, ffw_in, qkvw_in, tab_in = (sem(n) for n in ("c_in", "w_in", "ffw_in", "qkvw_in", "tab_in"))
        xl_in, lat_w, lat_wq, out_in = (sem(n) for n in ("xl_in", "lat_w", "lat_wq", "out_in"))
        kd_in, vd_in = [sem("kd_in0"), sem("kd_in1")], [sem("vd_in0"), sem("vd_in1")]

        block = ctx.enter_context(nc.Block())

        def slots(eng, layer, slot, after=lambda n, where: None):
            def steps(n):
                return lambda where: after(n, where)

            def flags(n):
                return n < TILES, 1 <= n <= TILES, 2 <= n <= TILES + 1, n >= 3, n + 1 < TILES, steps(n)
            for n in range(4):
                slot(layer, n // 2, n % 2, *flags(n))
            with eng.Fori(2, TILES // 2 - 1) as k:
                slot(layer, k, 0, True, True, True, True, True, lambda where: None)
                slot(layer, k, 1, True, True, True, True, True, lambda where: None)
            for n in range(TILES - 2, TILES + 3):
                slot(layer, n // 2, n % 2, *flags(n))

        def column(n):
            return n * P + n // NT

        def unit_ps(u):
            return bk((0, 1, 3, 4)[u])

        def centred_ps(c):
            return bk((0, 4, 2, 2)[c])

        def rstd_ps(c):
            return bk((1, 1, 7, 7)[c])

        def out_ps(c):
            return bk((2, 5, 6, 5)[c])

        Xf = X[:, :, :].rearrange("p b t -> p (b t)")
        X1f = X1[:, :, :].rearrange("p b t -> p (b t)")
        bodies = [(i, h) for i in range(NT) for h in range(REP)]

        def groups(i):
            return (i + 4) // 4

        def done_groups(j):
            return sum(groups(bodies[k][0]) for k in range(j))

        NTR = done_groups(len(bodies))

        @block.sync
        def _(sp):
            for q in kd_in + vd_in:
                sp.sem_inc(q, CR)
            sp.dma_start(cst[:, :], cst_d).then_inc(c_in, 16)
            sp.dma_start(res[:, :, :], x.rearrange("b (t p) d -> p (b t) d", p=P)).then_inc(xl_in, 16)
            sp.dma_start(gwo, wo.rearrange("(h p) n -> p h n", p=P)).then_inc(lat_w, 16)
            sp.dma_start(gwku, wku).then_inc(lat_w, 16)
            sp.dma_start(gwvu, wvuT).then_inc(lat_w, 16)

            def load_tables(layer):
                sp.dma_start(scales[:, :], par[bass.ds(layer, 1), :, 0:4].rearrange("a p n -> p (a n)")).then_inc(tab_in, 16)
                for kind in range(2):
                    for fn in range(2):
                        for hf in range(2):
                            sp.dma_start(tabs[:, kind, fn, hf, :], tab_d[3 * kind + fn * (1 + hf), :, :]).then_inc(tab_in, 16)

            def load_attention(layer):
                sp.dma_start(Wqkv[:, :], wqkv[bass.ds(layer, 1), :, :].rearrange("a p n -> p (a n)")).then_inc(qkvw_in, 16)
                sp.dma_start(Wo[:, :, :], lwo[bass.ds(layer, 1), :, :].rearrange("a (k p) n -> p (a k) n", p=P)).then_inc(qkvw_in, 16)
                load_tables(layer)

            with sp.Fori(0, B * KV) as it:
                kv = sp.snap(it % KV)
                sp.wait_ge(s["lvl_mm"], CR + it)
                sp.dma_start(gwq, wq[bass.ds(kv, 1), :, :].rearrange("a p n -> p (a n)")).then_inc(lat_wq, 16)
                sp.dma_start(gwk, wkd[bass.ds(kv, 1), :, :].rearrange("a p n -> p (a n)")).then_inc(lat_wq, 16)
                sp.dma_start(gwv, wvd[bass.ds(kv, 1), :, :].rearrange("a p n -> p (a n)")).then_inc(lat_wq, 16)

            load_attention(0)
            sp.wait_ge(s["zeroed"], CR + 7)
            sp.wait_ge(s["zeroed_v"], CR + 1)
            with sp.Fori(0, DEPTH) as layer:
                sp.wait_ge(s["x_new"], CR + layer * NC + NC)
                sp.dma_start(parv[:, :], par[bass.ds(layer, 1), :, :].rearrange("a p n -> p (a n)")).then_inc(w_in, 16)
                sp.dma_start(W1[:, :], w1[bass.ds(layer, 1), :, :].rearrange("a p n -> p (a n)")).then_inc(ffw_in, 16)
                sp.dma_start(W2[:, :, :], w2[bass.ds(layer, 1), :, :, :].rearrange("a p k n -> p (a k) n")).then_inc(ffw_in, 16)

                def slot(layer, k, par_, a, b, c, d, more, step):
                    n = k * 2 + par_
                    G, GK = layer * TILES + n, layer * (TILES // 2) + k
                    if a:
                        sp.wait_ge(s["k_nrm"], CR + G * 2 + 2)
                        for h in range(4):
                            sp.dma_start(kd[par_][32 * h:32 * h + 32, :, h, :], kr[32 * h:32 * h + 32, :, :]).then_inc(kd_in[par_], 16)
                        sp.wait_ge(s["pv_mm"], CR + G - 1)
                        sp.wait_ge(s["v_cp"], CR + G * 2 + 2)
                        for o in range(2):
                            r = 64 * o
                            src = vs[:, par_, 512 * o:512 * (o + 1)]
                            prev = vs[:, 1 - par_, 512 * o:512 * (o + 1)]
                            for w in range(NW):
                                sp.dma_start(vd[par_][r + 32:r + 64, w, o, :], src[32 * w:32 * w + 32, :]).then_inc(vd_in[par_], 16)
                                before = src[32 * w - 32:32 * w, :] if w else prev[96:128, :]
                                sp.dma_start(vd[par_][r:r + 32, w, o, :], before).then_inc(vd_in[par_], 16)

                slots(sp, layer, slot)
                following = sp.snap((layer + 1) % DEPTH)
                sp.wait_ge(s["wo_mm"], CR + layer * TILES + TILES)
                sp.wait_ge(s["u_s"], CR + (layer + 1) * TILES * 4)
                load_attention(following)
            sp.wait_ge(qkvw_in, 32 * (DEPTH + 1))
            sp.wait_ge(tab_in, 144 * (DEPTH + 1))
            for g4 in range(TILES // 4):
                sp.wait_ge(s["fin_add"], CR + g4 + 1)
                sp.dma_start(out.rearrange("b (t p) d -> p (b t) d", p=P)[:, 4 * g4:4 * g4 + 4, :],
                             res[:, 4 * g4:4 * g4 + 4, :]).then_inc(out_in, 16)
            sp.wait_ge(out_in, 16 * (TILES // 4))

        @block.gpsimd
        def _(pool):
            credit(pool, "pool")
            pool.memset(X[:, :, 0:1], 0.0).then_inc(s["zeroed"], 1)
            pool.memset(X1[:, :, 0:1], 0.0).then_inc(s["zeroed"], 1)
            pool.memset(vs[:, 1, :], 0.0).then_inc(s["zeroed"], 1)
            pool.memset(arena[:, 13696:], 0.0).then_inc(s["zeroed"], 1)

            def scale_tables(layer):
                pool.wait_ge(tab_in, layer * 144 + 144)
                for kind in range(2):
                    for fn in range(2):
                        for hf in range(2):
                            v = 2 * kind + hf
                            pool.tensor_tensor(tabs[:, kind, fn, hf, :], tabs[:, kind, fn, hf, :],
                                               scales[:, v:v + 1].to_broadcast([P, T]), ALU.mult).then_inc(s["tab_sc"], 1)

            scale_tables(0)
            pool.wait_ge(s["lo_add"], CR + B * KV * NT)
            pool.wait_ge(lat_wq, 16 * 3 * B * KV)
            pool.wait_ge(s["lq_mm"], CR + B * KV * 8)
            pool.memset(ssc[:, :], 0.0).then_inc(s["zeroed"], 1)
            for i in range(2):
                pool.memset(arena[:, 4096 * i:4096 * (i + 1)], 0.0).then_inc(s["zeroed"], 1)

            with pool.Fori(0, DEPTH) as layer:
                def slot(layer, k, par_, a, b, c, d, more, step):
                    n = k * 2 + par_
                    G, GK = layer * TILES + n, layer * (TILES // 2) + k

                    def add(u):
                        pool.wait_ge(s["u_s"], CR + G * 4 + u + 1)
                        dst = kr[:, 4 * u:4 * u + 4, :] if u < 2 else qr[:, 4 * (u - 2):4 * (u - 2) + 4, :]
                        pool.tensor_tensor(dst, dst, swp[:, u % 2, :].rearrange("p (j t) -> p j t", j=4),
                                           ALU.add).then_inc(s["u_rot"], 1)

                    if a:
                        add(0)
                        add(1)
                    if b:
                        sm3 = prob[:, 1 - par_, :].rearrange("p (i h k) -> p i h k", i=2, h=LH // 2)
                        for i in range(2):
                            pool.wait_ge(s["s_max"], CR + G * 2 - 1 + i)
                            m = nmax[:, 8 * i:8 * i + 8].rearrange("p (h o) -> p h o", o=1).to_broadcast([P, LH // 2, 64])
                            pool.tensor_tensor(sm3[:, i, :, :], sm3[:, i, :, :], m, ALU.subtract).then_inc(s["s_sub"], 1)
                        pool.wait_ge(s["rqT_cp"], CR + G)
                        for i in range(2):
                            pool.wait_ge(s["s_sub"], CR + G * 2 - 1 + i)
                            r = rq8[:, 8 * i:8 * i + 8].rearrange("p (h o) -> p h o", o=1).to_broadcast([P, LH // 2, 64])
                            pool.tensor_tensor(sm3[:, i, :, :], sm3[:, i, :, :], r, ALU.mult).then_inc(s["s_rq"], 1)
                    if a:
                        add(2)
                        add(3)

                slots(pool, layer, slot)
                scale_tables(layer + 1)

        @block.scalar
        def _(act):
            credit(act, "act")
            for g4 in range(TILES // 4):
                act.wait_ge(s["ln_xT"], CR + g4 + 1)
                b, t0 = divmod(4 * g4, NT)
                ins = act.activation(X[:, b, 1 + P * t0:1 + P * (t0 + 4)], bk(g4 % 2), ACT.Copy)
                ins.then_inc(s["x_init"], 1)
            act.wait_ge(s["wvo_mm"], CR + 2)
            act.activation(gvo, bk(2)[:, 0:2 * D].rearrange("p (k n) -> p k n", k=KV), ACT.Copy).then_inc(s["wvo_cp"], 1)
            with act.Fori(0, B * KV) as it:
                act.wait_ge(s["x_init"], CR + TILES // 4)
                act.wait_ge(s["lvl_mm"], CR + it)
                act.wait_ge(s["lq_mm"], CR + it * 8)
                act.activation(gx, Xf[:, bass.ds((it // KV) * (T + 1) + 1, T)], ACT.Copy).then_inc(s["lx_cp"], 1)
                act.wait_ge(s["ls_mm"], CR + it * len(bodies))
                for i in range(8):
                    act.wait_ge(s["lq_mm"], CR + it * 8 + i + 1)
                    act.activation(gq[:, i // 2, 512 * (i % 2):512 * (i % 2) + 512], bk(i % 2), ACT.Copy).then_inc(s["lq_cp"], 1)
                act.wait_ge(s["lk_mm"], CR + it + 1)
                act.activation(gkl, two(2)[0:LAT, :], ACT.Copy).then_inc(s["lkl_cp"], 1)
                act.wait_ge(s["lkk_mm"], CR + it + 1)
                act.activation(gk, two(4), ACT.Copy).then_inc(s["lkl_cp"], 1)
                act.wait_ge(s["lvl_mm"], CR + it + 1)
                act.wait_ge(s["ly_mm"], CR + it * NT)
                act.activation(gvl, bk(6)[:, 0:NT * LAT].rearrange("p (t n) -> p t n", t=NT), ACT.Copy).then_inc(s["lvl_cp"], 1)

                def exps(j):
                    J = it * len(bodies) + j
                    n = (bodies[j][0] + 1) * P
                    act.wait_ge(s["ls_neg"], CR + J + 1)
                    act.wait_ge(s["lt_mm"], CR + it * NTR + (done_groups(j - 1) if j >= 2 else 0))
                    act.activation(gp[:, j % 2, 0:n], two(2 * (j % 2))[:, 0:n], ACT.Exp, bias=gst[:, 8 + j % 2:9 + j % 2],
                                   scale=G_SCALE, accum_out=gst[:, 12 + j % 2:13 + j % 2]).then_inc(s["ls_exp"], 1)

                def evacuate(j):
                    i, h = bodies[j]
                    if h == 0:
                        act.wait_ge(s["ly_mm"], CR + it * NT + i)
                    for g in range(groups(i)):
                        k = done_groups(j) + g
                        act.wait_ge(s["lt_mm"], CR + it * NTR + k + 1)
                        nb = min(4, i + 1 - 4 * g)
                        act.activation(gpt[:, h, 4 * g:4 * g + nb, :],
                                       bk(4 + k % 2)[:, 0:P * nb].rearrange("p (k t) -> p k t", k=nb), ACT.Copy)\
                           .then_inc(s["lt_cp"], 1)

                def copy_outputs(i):
                    act.wait_ge(s["ly_mm"], CR + it * NT + i + 1)
                    act.wait_ge(s["lo_mm"], CR + it * NT + i)
                    act.activation(gy, bk(6)[:, 256:256 + P], ACT.Copy).then_inc(s["ly_cp"], 1)

                exps(0)
                for j in range(len(bodies)):
                    if j + 1 < len(bodies):
                        exps(j + 1)
                    evacuate(j)
                    if bodies[j][1] == 0 and j:
                        copy_outputs(bodies[j][0] - 1)
                copy_outputs(NT - 1)

            act.wait_ge(s["zeroed"], CR + 5)

            def shift(layer, n, par_):
                act.wait_ge(s["x_new"], CR + layer * NC + n // 4 + 1)
                act.wait_ge(s["u_mm"], CR + (layer * TILES + n) * 4 - 4)
                act.activation(xs[0:64, par_, :], Xf[0:64, bass.ds(column(n) + 1, P)], ACT.Copy).then_inc(s["xs_cp"], 1)
                act.activation(xs[64:128, par_, :], Xf[64:128, bass.ds(column(n), P)], ACT.Copy).then_inc(s["xs_cp"], 1)

            with act.Fori(0, DEPTH) as layer:
                def slot(layer, k, par_, a, b, c, d, more, step):
                    n = k * 2 + par_
                    G, GK = layer * TILES + n, layer * (TILES // 2) + k
                    if a:
                        square(G, 0)
                        square(G, 1)
                    if c:
                        for i in range(2):
                            act.wait_ge(s["pt_mm"], CR + (G - 2) * 2 + i + 1)
                            act.activation(ptile[:, 4 * i:4 * i + 4, :], bk(5 + i).rearrange("p (k t) -> p k t", k=4),
                                           ACT.Copy).then_inc(s["pt_cp"], 1)
                    step("mid")
                    if a:
                        act.wait_ge(s["ss_mm"], CR + G * 2 + 2)
                        act.activation(ssc[:, P:2 * P], bk(2)[:, P:2 * P], ACT.Copy).then_inc(s["ss_cp"], 1)
                        act.wait_ge(s["rs_n"], CR + (layer * (TILES + 1) + n + 1) * 11)
                        act.activation(rke[:, :, :, :].rearrange("p g h r -> p (g h) r"),
                                       rs[:, 2, LH:2 * LH].rearrange("p (h o) -> p h o", o=1).to_broadcast([P, LH, HALF]),
                                       ACT.Copy).then_inc(s["rk_cp"], 1)
                        act.wait_ge(vd_in[1 - par_], CR + (GK + par_) * 256)
                        for i in range(2):
                            act.wait_ge(s["v_mm"], CR + G * 2 + i + 1)
                            act.activation(vs[:, par_, 512 * i:512 * (i + 1)], bk(i), ACT.Copy).then_inc(s["v_cp"], 1)
                        if more:
                            shift(layer, n + 1, 1 - par_)
                        square(G, 2)
                        square(G, 3)
                    step("late")
                    if c:
                        for i in range(2):
                            act.wait_ge(s["ot_mm"], CR + (G - 2) * 2 + i + 1)
                            act.activation(otile[:, 4 * i:4 * i + 4, :], bk(5 + 2 * i).rearrange("p (k t) -> p k t", k=4),
                                           ACT.Copy).then_inc(s["ot_cp"], 1)
                    if a:
                        act.wait_ge(s["qs_mm"], CR + G * 2 + 2)
                        act.activation(ssc[:, 0:P], bk(2)[:, 0:P], ACT.Copy).then_inc(s["qs_cp"], 1)
                    if b:
                        act.wait_ge(s["s_rq"], CR + G * 2)
                        act.activation(prob[:, 1 - par_, :], prob[:, 1 - par_, :], ACT.Exp).then_inc(s["s_exp"], 1)
                    step("end")

                def square(G, u):
                    act.wait_ge(s["u_mm"], CR + G * 4 + u + 1)
                    if u < 2:
                        act.wait_ge(s["qs_mm"], CR + G * 2 + u - 1)
                    else:
                        act.wait_ge(s["ss_mm"], CR + G * 2 + u - 1)
                    act.activation(sq[:, u % 2, :], unit_ps(u), ACT.Square).then_inc(s["u_sq"], 1)

                def ln_square(c):
                    F = layer * NC + c
                    act.wait_ge(s["f_mu"], CR + F + 1)
                    act.wait_ge(s["f_xn"], CR + F)
                    act.activation(xc[:, :], centred_ps(c), ACT.Copy).then_inc(s["f_xc"], 1)
                    act.activation(fsq[:, :], centred_ps(c), ACT.Square).then_inc(s["f_sq"], 1)

                def spread_rstd(c):
                    if c:
                        act.wait_ge(s["rs_f"], CR + (layer * (NC - 1) + c) * 11)
                        rstd = fr[:, 2, 0:4]
                    else:
                        act.wait_ge(s["rs_n"], CR + (layer + 1) * (TILES + 1) * 11)
                        rstd = rs[:, 2, LH:LH + 4]
                    act.activation(fre[:, :, :], rstd.rearrange("p (t o) -> p t o", o=1).to_broadcast([P, 4, P]),
                                   ACT.Copy).then_inc(s["f_re"], 1)

                def gelu(c, j):
                    F, m = layer * NC + c, FJ[j][1]
                    act.wait_ge(s["f_g"], CR + F * 3 + j + 1)
                    act.wait_ge(s["f_h"], CR + F * 3 + j - 2)
                    act.activation(gl[j][0:m, :], bk(3 + j % 2)[0:m, :], ACT.Gelu,
                                   bias=parv[0:m, V_B1G + j:V_B1G + j + 1]).then_inc(s["f_gl"], 1)

                def early(n, where):
                    if (n, where) == (TILES - 1, "end"):
                        ln_square(0)
                    if (n, where) == (TILES, "mid"):
                        spread_rstd(0)
                    if (n, where) == (TILES, "end"):
                        gelu(0, 0)
                    if (n, where) == (TILES + 1, "mid"):
                        gelu(0, 1)
                    if (n, where) == (TILES + 1, "late"):
                        gelu(0, 2)
                        ln_square(1)

                shift(layer, 0, 0)
                slots(act, layer, slot, early)
                for c in range(NC):
                    if c:
                        for j in range(3):
                            gelu(c, j)
                    if c + 1 < NC:
                        spread_rstd(c + 1)
                    if c + 2 < NC:
                        ln_square(c + 2)

        @block.vector
        def _(dve):
            credit(dve, "dve")
            def rsqrt(w, n, name, count):
                x, h, y, q = (w[:, k, 0:n] for k in range(4))
                dve.tensor_scalar(h, x, -0.5, None, ALU.mult).then_inc(s[name], 1)
                dve.tensor_scalar(y.bitcast(mybir.dt.int32), x.bitcast(mybir.dt.int32), -0.5, float(0x5F3759DF),
                                  ALU.mult, ALU.add).then_inc(s[name], 1)
                for k in range(3):
                    dve.wait_ge(s[name], count + 3 * k + 2)
                    dve.tensor_tensor(q, y, y, ALU.mult).then_inc(s[name], 1)
                    dve.wait_ge(s[name], count + 3 * k + 3)
                    dve.tensor_tensor(q, q, h, ALU.mult).then_inc(s[name], 1)
                    dve.wait_ge(s[name], count + 3 * k + 4)
                    dve.scalar_tensor_tensor(y, q, 1.5, y, ALU.add, ALU.mult).then_inc(s[name], 1)
                dve.wait_ge(s[name], count + 11)

            dve.wait_ge(xl_in, 16)
            st6 = fsq[:, 0:6 * TILES].rearrange("p (t k) -> p t k", k=6)
            ag = fs[:, 0:2 * TILES].rearrange("p (t k) -> p t k", k=2)
            for t in range(TILES):
                dve.bn_stats(st6[:, t, :], res[:, t, :]).then_inc(s["st_bn"], 1)
            for t in range(TILES):
                dve.wait_ge(s["st_bn"], CR + t + 1)
                dve.bn_aggr(ag[:, t, :], st6[:, t, :]).then_inc(s["st_ag"], 1)
            dve.wait_ge(s["st_ag"], CR + TILES)
            dve.tensor_scalar(rs[:, 0, 0:TILES], ag[:, :, 1], 1e-5, None, ALU.add).then_inc(s["st_eps"], 1)
            dve.wait_ge(s["st_eps"], CR + 1)
            rsqrt(rs, TILES, "rs_0", CR)
            xln = prob[:, :, :].rearrange("p a (t d) -> p (a t) d", d=D)
            for t in range(TILES):
                dve.tensor_scalar(xln[:, t, :], res[:, t, :], ag[:, t, 0:1], rs[:, 2, t:t + 1], ALU.subtract, ALU.mult)\
                   .then_inc(s["ln_x"], 1)
            dve.wait_ge(s["x_init"], CR + TILES // 4)
            dve.sem_inc(s["x_new"], NC)

            def add_out(it, i):
                tile = (it // KV) * NT + i
                r = res[:, bass.ds(tile, 1), :].rearrange("p a d -> p (a d)")
                dve.wait_ge(s["lo_mm"], CR + it * NT + i + 1)
                dve.tensor_tensor(r, bk(7)[:, 0:D], r, ALU.add).then_inc(s["lo_add"], 1)

            with dve.Fori(0, B * KV) as it:
                def peak(j):
                    i, h = bodies[j]
                    J = it * len(bodies) + j
                    n = (i + 1) * P
                    S = two(2 * (j % 2))
                    dve.wait_ge(s["ls_mm"], CR + J + 1)
                    dve.tensor_tensor(S[:, i * P:n], S[:, i * P:n], caus, ALU.min).then_inc(s["ls_cap"], 1)
                    dve.wait_ge(s["ls_cap"], CR + J + 1)
                    dve.reduce_max(gst[:, 4 + j % 2:5 + j % 2], S[:, 0:n], AXX).then_inc(s["ls_max"], 1)
                    dve.wait_ge(s["ls_max"], CR + J + 1)
                    dve.tensor_scalar(gst[:, 8 + j % 2:9 + j % 2], gst[:, 4 + j % 2:5 + j % 2], -G_SCALE, None, ALU.mult)\
                       .then_inc(s["ls_neg"], 1)

                def normalise(j):
                    J = it * len(bodies) + j
                    n = (bodies[j][0] + 1) * P
                    dve.wait_ge(s["ls_exp"], CR + J + 1)
                    dve.reciprocal(gst[:, 16 + j % 2:17 + j % 2], gst[:, 12 + j % 2:13 + j % 2]).then_inc(s["ls_rec"], 1)
                    dve.wait_ge(s["ls_rec"], CR + J + 1)
                    dve.tensor_scalar(gp[:, j % 2, 0:n], gp[:, j % 2, 0:n], gst[:, 16 + j % 2:17 + j % 2], None, ALU.mult)\
                       .then_inc(s["ls_nrm"], 1)

                peak(0)
                peak(1)
                for j in range(len(bodies)):
                    normalise(j)
                    if j + 2 < len(bodies):
                        peak(j + 2)
                    i, h = bodies[j]
                    if h == 1 and i:
                        add_out(it, i - 1)
                add_out(it, NT - 1)

            dve.memset(arena[:, 8192:13696], 0.0).then_inc(s["zeroed_v"], 1)
            with dve.Fori(0, DEPTH) as layer:
                dve.wait_ge(s["tab_sc"], CR + layer * 8 + 8)

                def rotate(G, GK, n, par_, u):
                    tb = tabs[:, 1 - u // 2, :, :, bass.ds((n % NT) * P, P)]
                    src = unit_ps(u).rearrange("p (g a t) -> p g a t", g=2, a=2)
                    dve.wait_ge(s["u_sq"], CR + G * 4 + u + 1)
                    if u < 2:
                        dve.wait_ge(kd_in[1 - par_], CR + (GK + par_) * 64)
                        dst = kr[:, 4 * u:4 * u + 4, :]
                    else:
                        dve.wait_ge(s["s_mm"], CR + G * 2)
                        dst = qr[:, 4 * (u - 2):4 * (u - 2) + 4, :]
                    dst = dst.rearrange("p (g a) t -> p g a t", g=2)
                    for g in range(2):
                        ins = dve.tensor_tensor(dst[:, g, :, :], src[:, g, :, :], tb[:, 0, :, :], ALU.mult)
                    ins.then_inc(s["u_c"], 1)
                    dve.wait_ge(s["u_rot"], CR + G * 4 + u - 1)
                    sw = swp[:, u % 2, :].rearrange("p (g a t) -> p g a t", g=2, a=2)[:, :, ::-1, :]
                    for g in range(2):
                        ins = dve.tensor_tensor(sw[:, g, :, :], src[:, g, :, :], tb[:, 1, :, :], ALU.mult)
                    ins.then_inc(s["u_s"], 1)

                def slot(layer, k, par_, a, b, c, d, more, step):
                    n = k * 2 + par_
                    G, GK = layer * TILES + n, layer * (TILES // 2) + k
                    sm3 = prob[:, 1 - par_, :].rearrange("p (i h k) -> p i h k", i=2, h=LH // 2)
                    if a:
                        rotate(G, GK, n, par_, 0)
                        rotate(G, GK, n, par_, 1)
                    if d:
                        dve.wait_ge(s["wo_mm"], CR + G - 2)
                        at = column(n - 3) + 1
                        dve.tensor_tensor(X1f[:, bass.ds(at, P)], bk(7)[:, 0:P], Xf[:, bass.ds(at, P)], ALU.add)\
                           .then_inc(s["wo_add"], 1)
                    if c:
                        dve.wait_ge(s["s_exp"], CR + G - 1)
                        dve.reduce_sum(den[:, :], prob[:, par_, :].rearrange("p (h k) -> p h k", h=LH), AXX).then_inc(s["s_sum"], 1)
                        dve.wait_ge(s["s_sum"], CR + G - 1)
                        dve.reciprocal(den[:, :], den[:, :]).then_inc(s["s_inv"], 1)
                    step("mid")
                    if a or b:
                        N = layer * (TILES + 1) + n
                        dve.wait_ge(s["ssT_mm"], CR + N + 1)
                        dve.wait_ge(s["rk_cp"], CR + G)
                        gs = 2 * NG if a else NG
                        dve.tensor_scalar(rs[:, 0, 0:4 * gs].rearrange("p (g h) -> p g h", g=gs),
                                          bk(2)[:, 0:32 * gs].rearrange("p (g h) -> p g h", g=gs)[:, :, 0:4], 1e-24, None,
                                          ALU.max).then_inc(s["ss_cl"], 1)
                        step("norms")
                        dve.wait_ge(s["ss_cl"], CR + N + 1)
                        rsqrt(rs, 2 * LH, "rs_n", CR + N * 11)
                    if b:
                        dve.wait_ge(s["s_rq"], CR + G * 2 - 2)
                        dve.tensor_scalar(rq8[:, :], rs[:, 2, 0:LH], QK_SCALE, None, ALU.mult).then_inc(s["rqT_cp"], 1)
                        cap = cst[:, bass.ds(((n - 1) % NT) * 64 + C_CAP, 64)]
                        dve.wait_ge(s["pt_mm"], CR + G * 2 - 4)
                        for i in range(2):
                            dve.wait_ge(s["s_mm"], CR + G * 2 - 1 + i)
                            dve.tensor_tensor(sm3[:, i, :, :], bk(3 + i).rearrange("p (h k) -> p h k", h=LH // 2),
                                              cap.rearrange("p (o k) -> p o k", o=1).to_broadcast([P, LH // 2, 64]),
                                              ALU.min).then_inc(s["s_cap"], 1)
                        dve.wait_ge(s["s_sub"], CR + G * 2 - 2)
                        for i in range(2):
                            dve.wait_ge(s["s_cap"], CR + G * 2 - 1 + i)
                            dve.reduce_max(nmax[:, 8 * i:8 * i + 8], sm3[:, i, :, :], AXX).then_inc(s["s_max"], 1)
                    if a:
                        dve.wait_ge(s["rkb_mm"], CR + G + 1)
                        dve.wait_ge(s["u_rot"], CR + G * 4 + 2)
                        rk = bk(2).rearrange("p (g o t) -> p g o t", g=NG, o=1)
                        for i in range(2):
                            k4 = kr[:, 4 * i:4 * i + 4, :].rearrange("p (g a) t -> p g a t", g=2)
                            dve.tensor_tensor(k4, rk[:, 2 * i:2 * i + 2, :, :].to_broadcast([P, 2, 2, P]), k4, ALU.mult)\
                               .then_inc(s["k_nrm"], 1)
                    if c:
                        dve.wait_ge(s["pv_mm"], CR + G - 1)
                        dve.wait_ge(s["s_inv"], CR + G - 1)
                        dve.tensor_tensor(osb[:, :, :], outputs_ps,
                                          den[:, :].rearrange("p (h o) -> p h o", o=1).to_broadcast([P, LH, LD]),
                                          ALU.mult).then_inc(s["o_nrm"], 1)
                    if a:
                        rotate(G, GK, n, par_, 2)
                        rotate(G, GK, n, par_, 3)
                    step("end")

                def shifted(c):
                    F = layer * NC + c
                    b, t0 = divmod(c * CH, T)
                    dve.wait_ge(s["wo_add"], CR + layer * TILES + (c + 1) * CH // P)
                    dve.wait_ge(s["f_mu"], CR + F)
                    dve.tensor_copy(fs[0:64, :], X1[0:64, b, 1 + t0:1 + t0 + CH]).then_inc(s["f_cp"], 1)
                    dve.tensor_copy(fs[64:128, :], X1[64:128, b, t0:t0 + CH]).then_inc(s["f_cp"], 1)

                def variance(c):
                    F = layer * NC + c
                    dve.wait_ge(s["f_var"], CR + F + 1)
                    dve.wait_ge(s["f_re"], CR + F)
                    to = fr[:, 0, 0:4] if c else rs[:, 0, LH:LH + 4]
                    dve.tensor_scalar(to, rstd_ps(c)[:, 0:4], 1e-5, None, ALU.add).then_inc(s["f_eps"], 1)
                    dve.wait_ge(s["f_eps"], CR + F + 1)
                    if c:
                        rsqrt(fr, 4, "rs_f", CR + (layer * (NC - 1) + c - 1) * 11)

                def affine(c):
                    F = layer * NC + c
                    dve.wait_ge(s["f_rb"], CR + F + 1)
                    dve.tensor_tensor(xn[:, :], rstd_ps(c), xc[:, :], ALU.mult).then_inc(s["f_xn"], 1)
                    dve.wait_ge(s["f_xn"], CR + F + 1)
                    dve.tensor_scalar(xn[:, :], xn[:, :], parv[:, V_G:V_G + 1], parv[:, V_B:V_B + 1], ALU.mult, ALU.add)\
                       .then_inc(s["f_aff"], 1)

                def gated(c, j):
                    F = layer * NC + c
                    m = FJ[j][1]
                    dve.wait_ge(s["f_a"], CR + F * 3 + j + 1)
                    dve.wait_ge(s["f_gl"], CR + F * 3 + j + 1)
                    dve.wait_ge(s["f_out_mm"], CR + F)
                    dve.scalar_tensor_tensor(hb[j][0:m, :], bk(j % 2)[0:m, :], parv[0:m, V_B1A + j:V_B1A + j + 1],
                                             gl[j][0:m, :], ALU.add, ALU.mult).then_inc(s["f_h"], 1)

                def finish(c):
                    F = layer * NC + c
                    b, t0 = divmod(c * CH, T)
                    dve.wait_ge(s["f_out_mm"], CR + F + 1)
                    dve.wait_ge(s["xs_cp"], CR + (layer + 1) * TILES * 2)
                    dve.scalar_tensor_tensor(X[:, b, 1 + t0:1 + t0 + CH], out_ps(c), parv[:, V_B2:V_B2 + 1],
                                             X1[:, b, 1 + t0:1 + t0 + CH], ALU.add, ALU.add).then_inc(s["x_new"], 1)

                def early(n, where):
                    if (n, where) == (TILES - 2, "end"):
                        shifted(0)
                    if (n, where) == (TILES, "mid"):
                        shifted(1)
                    if (n, where) == (TILES, "norms"):
                        variance(0)
                    if (n, where) == (TILES, "end"):
                        dve.wait_ge(w_in, layer * 16 + 16)
                        affine(0)
                    if (n, where) == (TILES + 1, "mid"):
                        gated(0, 0)
                        gated(0, 1)
                    if (n, where) == (TILES + 1, "end"):
                        gated(0, 2)
                        variance(1)
                        finish(0)

                slots(dve, layer, slot, early)
                for c in range(NC):
                    if c:
                        gated(c, 0)
                        if c + 1 < NC:
                            variance(c + 1)
                        gated(c, 1)
                        gated(c, 2)
                    if c + 2 < NC:
                        shifted(c + 2)
                    if c + 1 < NC:
                        affine(c + 1)
                    if c:
                        finish(c)

            for g4 in range(TILES // 4):
                dve.wait_ge(s["fin_mm"], CR + g4 + 1)
                r4 = res[:, 4 * g4:4 * g4 + 4, :]
                dve.tensor_tensor(r4, bk(g4 % 2).rearrange("p (t d) -> p t d", t=4), r4, ALU.add).then_inc(s["fin_add"], 1)

        @block.tensor
        def _(pe):
            credit(pe, "pe")
            def mm(o, l, r, start=True, stop=True):
                return pe.matmul(o, l, r, start=start, stop=stop)

            pe.wait_ge(c_in, 16)
            xln = prob[:, :, :].rearrange("p a (t d) -> p (a t) d", d=D)
            for g4 in range(TILES // 4):
                if g4 >= 2:
                    pe.wait_ge(s["x_init"], CR + g4 - 1)
                pe.wait_ge(s["ln_x"], CR + 4 * g4 + 4)
                for k in range(4):
                    ins = pe.transpose(bk(g4 % 2)[:, P * k:P * k + P], xln[:, 4 * g4 + k, :], ident)
                ins.then_inc(s["ln_xT"], 1)
            pe.wait_ge(lat_w, 48)
            for kv in range(KV):
                for h in range(REP):
                    ins = mm(bk(2)[32 * h:32 * h + 32, D * kv:D * kv + D], gwvu, gwo[:, kv * REP + h, :])
                ins.then_inc(s["wvo_mm"], 1)
            with pe.Fori(0, B * KV) as it:
                pe.wait_ge(lat_wq, it * 48 + 48)
                pe.wait_ge(s["lx_cp"], CR + it + 1)
                pe.wait_ge(s["wvo_cp"], CR + 1)
                pe.wait_ge(s["ls_exp"], CR + it * len(bodies))
                for i in range(8):
                    if i >= 2:
                        pe.wait_ge(s["lq_cp"], CR + it * 8 + i - 1)
                    mm(bk(i % 2), gwq[:, P * (i // 2):P * (i // 2) + P], gx[:, 512 * (i % 2):512 * (i % 2) + 512])\
                        .then_inc(s["lq_mm"], 1)
                for i in range(2):
                    ins = mm(bk(2 + i)[0:LAT, :], gwk, gx[:, 512 * i:512 * (i + 1)])
                ins.then_inc(s["lk_mm"], 1)
                pe.wait_ge(s["lt_cp"], CR + it * NTR)
                pe.wait_ge(s["lkl_cp"], CR + it * 2 + 1)
                for i in range(2):
                    ins = mm(bk(4 + i), gwku, gkl[:, 512 * i:512 * (i + 1)])
                ins.then_inc(s["lkk_mm"], 1)
                pe.wait_ge(s["ly_cp"], CR + it * NT)
                for t in range(NT):
                    ins = mm(bk(6)[:, LAT * t:LAT * t + LAT], gx[:, P * t:P * t + P], gwv)
                ins.then_inc(s["lvl_mm"], 1)
                pe.wait_ge(s["lq_cp"], CR + it * 8 + 8)
                pe.wait_ge(s["lkl_cp"], CR + it * 2 + 2)

                def scores(j):
                    i, h = bodies[j]
                    n = (i + 1) * P
                    if j >= 2:
                        pe.wait_ge(s["ls_exp"], CR + it * len(bodies) + j - 1)
                    for k in range(0, n, 512):
                        w = min(512, n - k)
                        ins = mm(two(2 * (j % 2))[:, k:k + w], gq[:, h, P * i:P * i + P], gk[:, k:k + w])
                    ins.then_inc(s["ls_mm"], 1)

                def finish(j):
                    i, h = bodies[j]
                    pe.wait_ge(s["ls_nrm"], CR + it * len(bodies) + j + 1)
                    for g in range(groups(i)):
                        k = done_groups(j) + g
                        if k >= 2:
                            pe.wait_ge(s["lt_cp"], CR + it * NTR + k - 1)
                        for q in range(min(4, i + 1 - 4 * g)):
                            kb = 4 * g + q
                            ins = pe.transpose(bk(4 + k % 2)[:, P * q:P * q + P], gp[:, j % 2, P * kb:P * kb + P], ident)
                        ins.then_inc(s["lt_mm"], 1)

                def outputs(i):
                    pe.wait_ge(s["lt_cp"], CR + it * NTR + done_groups((i + 1) * REP))
                    pe.wait_ge(s["lvl_cp"], CR + it + 1)
                    pe.wait_ge(s["ly_cp"], CR + it * NT + i)
                    for kb in range(i + 1):
                        for hh in range(REP):
                            ins = mm(bk(6)[32 * hh:32 * hh + 32, 256:256 + P], gvl[:, kb, :], gpt[:, hh, kb, :],
                                     kb == 0, kb == i)
                    ins.then_inc(s["ly_mm"], 1)

                def project(i):
                    pe.wait_ge(s["ly_cp"], CR + it * NT + i + 1)
                    pe.wait_ge(s["lo_add"], CR + it * NT + i)
                    mm(bk(7)[:, 0:D], gy, gvo[:, bass.ds(it % KV, 1), :].rearrange("p a n -> p (a n)")).then_inc(s["lo_mm"], 1)

                scores(0)
                scores(1)
                for j in range(len(bodies)):
                    if j + 2 < len(bodies):
                        scores(j + 2)
                    i, h = bodies[j]
                    if h == 0 and i:
                        outputs(i - 1)
                    finish(j)
                    if h == 1 and i:
                        project(i - 1)
                outputs(NT - 1)
                project(NT - 1)

            pe.wait_ge(s["zeroed"], CR + 5)
            pe.wait_ge(s["lo_add"], CR + B * KV * NT)
            with pe.Fori(0, DEPTH) as layer:
                def unit(G, par_, u):
                    if u < 2:
                        pe.wait_ge(s["v_cp"], CR + G * 2 + u - 1)
                    else:
                        pe.wait_ge(s["s_cap"], CR + G * 2 + u - 3)
                    first = (2 * NG if u < 2 else 0) + 4 * (u % 2)
                    for j in range(4):
                        w = Wqkv[:, (first + j) * P:(first + j + 1) * P]
                        ins = mm(unit_ps(u)[:, P * j:P * j + P], w, xs[:, par_, :])
                    ins.then_inc(s["u_mm"], 1)

                def square_sums(G, u, into, name):
                    pe.wait_ge(s["u_sq"], CR + G * 4 + u + 1)
                    for gg in range(2):
                        g = 2 * (u % 2) + gg
                        for a_ in range(2):
                            ins = mm(into[32 * g:32 * g + 32, :], ones4,
                                     sq[:, u % 2, P * (2 * gg + a_):P * (2 * gg + a_ + 1)], a_ == 0, a_ == 1)
                    ins.then_inc(s[name], 1)

                def score_half(q, i):
                    for g in range(2 * i, 2 * i + 2):
                        half = bk(3 + i)[:, 256 * (g % 2):256 * (g % 2) + 256].rearrange("p (h k) -> p h k", h=4)
                        for a_ in range(2):
                            j = 2 * g + a_
                            for w in range(NW):
                                o = half[32 * w:32 * w + 32, :, :]
                                l = qr[:, j, 32 * w:32 * w + 32]
                                if w:
                                    ins = mm(o, l, kd[q][:, j, :, 32 * w - 32:32 * w + 32], a_ == 0, a_ == 1)
                                else:
                                    pe.matmul(o[:, :, 0:32], l, kd[1 - q][:, j, :, 96:128], start=a_ == 0,
                                              stop=a_ == 1, skip_group_check=True)
                                    ins = pe.matmul(o[:, :, 32:64], l, kd[q][:, j, :, 0:32], start=False,
                                                    stop=a_ == 1, skip_group_check=True)
                    ins.then_inc(s["s_mm"], 1)

                def slot(layer, k, par_, a, b, c, d, more, step):
                    n = k * 2 + par_
                    G, GK = layer * TILES + n, layer * (TILES // 2) + k
                    if a:
                        pe.wait_ge(s["xs_cp"], CR + G * 2 + 2)
                        unit(G, par_, 0)
                        unit(G, par_, 1)
                    if d:
                        pe.wait_ge(s["ot_cp"], CR + (G - 2) * 2)
                        for k in range(NP):
                            ins = mm(bk(7)[:, 0:P], Wo[:, k, :], otile[:, k, :], k == 0, k == NP - 1)
                        ins.then_inc(s["wo_mm"], 1)
                    if c:
                        pe.wait_ge(s["s_exp"], CR + G - 1)
                        pe.wait_ge(s["ot_cp"], CR + G * 2 - 4)
                        for i in range(2):
                            for k in range(4):
                                ins = pe.transpose(bk(5 + i)[:, P * k:P * k + P],
                                                   prob[:, par_, P * (4 * i + k):P * (4 * i + k + 1)], ident)
                            ins.then_inc(s["pt_mm"], 1)
                    step("mid")
                    if a:
                        pe.wait_ge(s["qs_cp"], CR + G)
                        square_sums(G, 0, bk(2)[:, P:2 * P], "ss_mm")
                        square_sums(G, 1, bk(2)[:, P:2 * P], "ss_mm")
                    if b:
                        pe.wait_ge(kd_in[1 - par_], CR + (GK + par_) * 64)
                        pe.wait_ge(s["u_rot"], CR + G * 4)
                        pe.wait_ge(s["s_cap"], CR + G * 2 - 2)
                        score_half(1 - par_, 0)
                    if a or b:
                        pe.wait_ge(s["qs_cp"], CR + G)
                        if a:
                            pe.wait_ge(s["ss_cp"], CR + G + 1)
                        ins = pe.transpose(bk(2)[:, 0:P], ssc[:, 0:P], ident)
                        if a:
                            ins = pe.transpose(bk(2)[:, P:2 * P], ssc[:, P:2 * P], ident)
                        ins.then_inc(s["ssT_mm"], 1)
                    if b:
                        score_half(1 - par_, 1)
                    if a:
                        for i in range(2):
                            pe.wait_ge(s["u_s"], CR + G * 4 + 1 + i)
                            mm(bk(i), xs[:, par_, :], Wqkv[:, 2048 + 512 * i:2048 + 512 * (i + 1)]).then_inc(s["v_mm"], 1)
                        pe.wait_ge(s["rk_cp"], CR + G + 1)
                        for g in range(NG):
                            ins = pe.transpose(bk(2)[:, P * g:P * g + P], rke[:, g, :, :].rearrange("p h r -> p (h r)"), ident)
                        ins.then_inc(s["rkb_mm"], 1)
                    if c:
                        pe.wait_ge(vd_in[par_], CR + GK * 256)
                        for i in range(2):
                            pe.wait_ge(s["pt_cp"], CR + (G - 2) * 2 + i + 1)
                            for k in range(4):
                                for w in range(NW):
                                    pr = 4 * i + k
                                    rhs = vd[par_][:, w, :, 64 * pr:64 * pr + 64]
                                    ins = mm(bk(5 + i)[32 * w:32 * w + 32, P * k:P * k + P].rearrange("p (o d) -> p o d", o=2),
                                             ptile[:, pr, 32 * w:32 * w + 32], rhs)
                        ins.then_inc(s["pv_mm"], 1)
                    if a:
                        unit(G, par_, 2)
                        unit(G, par_, 3)
                    step("late")
                    if c:
                        pe.wait_ge(s["o_nrm"], CR + G - 1)
                        pe.wait_ge(s["wo_add"], CR + G - 2)
                        for i in range(2):
                            for k in range(4):
                                pr = 4 * i + k
                                ins = pe.transpose(bk(5 + 2 * i)[:, P * k:P * k + P],
                                                   osb[:, 2 * pr:2 * pr + 2, :].rearrange("p a d -> p (a d)"), ident)
                            ins.then_inc(s["ot_mm"], 1)
                    if a:
                        pe.wait_ge(s["k_nrm"], CR + G * 2 + 2)
                        square_sums(G, 2, bk(2)[:, 0:P], "qs_mm")
                        square_sums(G, 3, bk(2)[:, 0:P], "qs_mm")
                    step("end")

                pe.wait_ge(qkvw_in, layer * 32 + 32)
                def mean(c):
                    F = layer * NC + c
                    pe.wait_ge(s["f_cp"], CR + F * 2 + 2)
                    if c == 0:
                        pe.wait_ge(s["v_cp"], CR + (layer + 1) * TILES * 2)
                    else:
                        pe.wait_ge(s["f_sq"], CR + F)
                    mm(centred_ps(c), centre, fs[:, :]).then_inc(s["f_mu"], 1)

                def var(c):
                    F = layer * NC + c
                    pe.wait_ge(s["f_sq"], CR + F + 1)
                    pe.wait_ge(s["f_xn"], CR + F)
                    for k in range(4):
                        ins = mm(rstd_ps(c)[:, k:k + 1], fsq[:, P * k:P * k + P], meanw)
                    ins.then_inc(s["f_var"], 1)

                def rstd_rows(c):
                    F = layer * NC + c
                    pe.wait_ge(s["f_re"], CR + F + 1)
                    for k in range(4):
                        ins = pe.transpose(rstd_ps(c)[:, P * k:P * k + P], fre[:, k, :], ident)
                    ins.then_inc(s["f_rb"], 1)

                def up(c, j):
                    F = layer * NC + c
                    j0, m = FJ[j]
                    pe.wait_ge(s["f_aff"], CR + F + 1)
                    pe.wait_ge(s["f_h"], CR + F * 3 + (j - 1 if j == 2 else 0))
                    mm(bk(3 + j % 2)[0:m, :], W1[:, FF + j0:FF + j0 + m], xn[:, :]).then_inc(s["f_g"], 1)
                    mm(bk(j % 2)[0:m, :], W1[:, j0:j0 + m], xn[:, :]).then_inc(s["f_a"], 1)

                def down(c, steps):
                    F = layer * NC + c
                    if c >= 2:
                        pe.wait_ge(s["x_new"], CR + NC + F - 1)
                    for j in steps:
                        j0, m = FJ[j]
                        pe.wait_ge(s["f_h"], CR + F * 3 + j + 1)
                        ins = mm(out_ps(c), W2[0:m, j, :], hb[j][0:m, :], j == 0, j == 2)
                        if j == 2:
                            ins.then_inc(s["f_out_mm"], 1)

                def early(n, where):
                    if (n, where) == (TILES - 1, "end"):
                        mean(0)
                    if (n, where) == (TILES, "mid"):
                        var(0)
                    if (n, where) == (TILES, "late"):
                        rstd_rows(0)
                    if (n, where) == (TILES, "end"):
                        pe.wait_ge(ffw_in, layer * 32 + 32)
                        up(0, 0)
                    if (n, where) == (TILES + 1, "mid"):
                        up(0, 1)
                    if (n, where) == (TILES + 1, "late"):
                        up(0, 2)
                        pe.wait_ge(s["f_gl"], CR + layer * NC * 3 + 2)
                        mean(1)
                    if (n, where) == (TILES + 1, "end"):
                        var(1)
                        down(0, range(3))

                slots(pe, layer, slot, early)
                for c in range(NC):
                    if c:
                        up(c, 0)
                        if c + 1 < NC:
                            var(c + 1)
                        up(c, 1)
                        up(c, 2)
                        if c == 1:
                            pe.wait_ge(s["ot_cp"], CR + (layer + 1) * TILES * 2)
                        down(c, range(2))
                    if c + 1 < NC:
                        rstd_rows(c + 1)
                    if c:
                        down(c, range(2, 3))
                    if c + 2 < NC:
                        if c == 0:
                            pe.wait_ge(s["x_new"], CR + NC + layer * NC + 1)
                        mean(c + 2)
                        if c == 0:
                            pe.wait_ge(s["wo_add"], CR + (layer + 1) * TILES)
            pe.wait_ge(s["x_new"], CR + NC + DEPTH * NC)

            for g4 in range(TILES // 4):
                if g4 >= 2:
                    pe.wait_ge(s["fin_add"], CR + g4 - 1)
                b, t0 = divmod(4 * g4, NT)
                for k in range(4):
                    ins = pe.transpose(bk(g4 % 2)[:, P * k:P * k + P], X[:, b, 1 + P * (t0 + k):1 + P * (t0 + k + 1)], ident)
                ins.then_inc(s["fin_mm"], 1)


_OUT = ("out_0_dram", (B, T, D))


def kernel(L0_attn_x, L0_attn_wq, L0_attn_wk_down, L0_attn_wv_down, L0_attn_wk_up, L0_attn_wv_up, L0_attn_wo,
           L0_ffn_Wqkv, L0_ffn_q_scale, L0_ffn_k_scale, L0_ffn_Wo, L0_ffn_ln_g, L0_ffn_ln_b, L0_ffn_W1, L0_ffn_b1,
           L0_ffn_W2, L0_ffn_b2):
    import concourse.bacc as bacc
    from concourse.bass_utils import run_bass_kernel_spmd

    a = np.asarray
    w = a(L0_ffn_Wqkv).reshape(DEPTH, D, 3, NG, 4, 2, HALF)
    qk = w[:, :, 0:2].transpose(0, 1, 2, 3, 5, 4, 6).reshape(DEPTH, D, -1)
    v = a(L0_ffn_Wqkv)[:, :, 2 * LH * LD:].reshape(DEPTH, D, NP, 2, LD).transpose(0, 1, 3, 2, 4).reshape(DEPTH, D, -1)
    w2 = np.zeros((DEPTH, 3 * P, D), np.float32)
    w2[:, :FF] = a(L0_ffn_W2)
    par = np.zeros((DEPTH, P, V_N), np.float32)
    for col, src, half in ((V_QA, L0_ffn_q_scale, 0), (V_QB, L0_ffn_q_scale, 1), (V_KA, L0_ffn_k_scale, 0),
                           (V_KB, L0_ffn_k_scale, 1)):
        par[:, :, col] = np.tile(a(src)[:, HALF * half:HALF * (half + 1)], (1, 4))
    par[:, :, V_G], par[:, :, V_B], par[:, :, V_B2] = a(L0_ffn_ln_g), a(L0_ffn_ln_b), a(L0_ffn_b2)
    for j, (j0, m) in enumerate(FJ):
        par[:, 0:m, V_B1A + j] = a(L0_ffn_b1)[:, j0:j0 + m]
        par[:, 0:m, V_B1G + j] = a(L0_ffn_b1)[:, FF + j0:FF + j0 + m]
    cst, tabs = shape_constants()
    ins = {
        "x": a(L0_attn_x),
        "wq": a(L0_attn_wq).reshape(D, KV, REP * GD).transpose(1, 0, 2),
        "wkd": a(L0_attn_wk_down).reshape(D, KV, LAT).transpose(1, 0, 2),
        "wvd": a(L0_attn_wv_down).reshape(D, KV, LAT).transpose(1, 0, 2),
        "wku": a(L0_attn_wk_up),
        "wvuT": a(L0_attn_wv_up).T,
        "wo": a(L0_attn_wo),
        "wqkv": np.concatenate([qk, v], axis=2),
        "lwo": a(L0_ffn_Wo),
        "w1": a(L0_ffn_W1),
        "w2": w2.reshape(DEPTH, 3, P, D).transpose(0, 2, 1, 3),
        "par": par,
        "cst": cst,
        "tab": tabs,
    }
    nc = bacc.Bacc("TRN2", target_bir_lowering=False, num_devices=1)
    arrays, args = {}, []
    for name, arr in ins.items():
        arr = np.ascontiguousarray(arr)
        arrays[f"in_{name}_dram"] = arr
        args.append(nc.dram_tensor(f"in_{name}_dram", arr.shape, mybir.dt.from_np(arr.dtype), kind="ExternalInput").ap())
    args.append(nc.dram_tensor(_OUT[0], _OUT[1], F32, kind="ExternalOutput").ap())
    build(nc, *args)
    r = run_bass_kernel_spmd(nc, [arrays], core_ids=[0])
    return r.results[0][_OUT[0]]
```

```python
from contextlib import ExitStack

import numpy as np

import concourse.bass as bass
from concourse import mybir

F32 = mybir.dt.float32
F32R = mybir.dt.float32r
ALU = mybir.AluOpType
ACT = mybir.ActivationFunctionType
AXX = mybir.AxisListType.X

P = 128
B, T, D = 2, 1024, 128
NT = T // P
TILES = B * NT
GH, KV, GD, LAT = 8, 2, 128, 32
REP = GH // KV
G_SCALE = float(GD) ** -0.5
DEPTH, LH, LD, WIN = 6, 16, 64, 32
HALF = LD // 2
NG = LH // 4
NP = LH // 2
NW = P // WIN
QK_SCALE = 8.0
FF = int(D * 4 * 2 / 3)
FJ = [(0, 128), (128, 128), (256, FF - 256)]
CH = 512
NC = B * T // CH
CR = 8
NEG = -1.0e30

C_ID, C_CEN, C_CAUS, C_ONE, C_CAP, C_MEAN = 0, 128, 256, 384, 416, 416 + 64 * NT
C_1 = C_MEAN + 1
C_N = C_MEAN + 2
(V_QA, V_QB, V_KA, V_KB, V_G, V_B, V_B1A, V_B1G, V_B2) = 0, 1, 2, 3, 4, 5, 6, 9, 12
V_N = 13


RING = 2


def shape_constants():
    c = np.zeros((P, C_N), np.float32)
    i = np.arange(P)
    c[:, C_ID:C_ID + P] = np.eye(P)
    c[:, C_CEN:C_CEN + P] = np.eye(P) - 1.0 / D
    c[:, C_MEAN] = 1.0 / D
    c[:, C_1] = 1.0
    c[:, C_CAUS:C_CAUS + P] = np.where(i[None, :] <= i[:, None], 3.0e38, NEG)
    c[i, C_ONE + i // 32] = 1.0
    r, k = i[:, None] % WIN, np.arange(2 * WIN)[None, :]
    inside = (k >= r) & (k <= r + WIN)
    for n in range(NT):
        ok = inside & ((i[:, None] >= WIN) | (k >= WIN)) if n == 0 else inside
        c[:, C_CAP + 64 * n:C_CAP + 64 * (n + 1)] = np.where(ok, 3.0e38, NEG)
    f = np.float32
    half = np.arange(0, LD, 2, dtype=f)
    inv_freq = f(1.0) / np.power(f(10000.0), half / f(LD))
    t = np.arange(T, dtype=f)
    freqs = t[:, None] * inv_freq[None, :]
    base = (half + f(0.4 * LD)) / f(1.4 * LD)
    power = (t - f(T // 2)) / f(WIN // 2)
    scale = np.power(base[None, :], power[:, None])
    cos, sin = np.cos(freqs), np.sin(freqs)
    tabs = [cos * scale, sin * scale, -sin * scale, cos / scale, sin / scale, -sin / scale]
    tabs = np.stack([np.tile(x.T, (4, 1)) for x in tabs]).astype(f)
    return c, np.ascontiguousarray(tabs)


def build(nc, x, wqT, wkdT, wvd, wku, wvuT, wo, wqkv, lwo, w1, w2, par, cst_d, tab_d, out):
    ctx = ExitStack()
    with ctx:
        def sb(name, shape, dtype=F32):
            return ctx.enter_context(nc.sbuf_tensor(name, shape, dtype))

        def sem(name):
            return ctx.enter_context(nc.semaphore(name))

        cst = sb("cst", [P, C_N])
        parv = sb("parv", [P, V_N])
        scales = sb("scales", [P, 4])
        Wqk = sb("Wqk", [P, 2 * LH * LD])
        Wo = sb("Wo", [P, NP, D])
        W2 = sb("W2", [P, 3, D])
        E_V, E_1 = 2 * LH * LD, 2 * LH * LD + 4 * FF
        parts = sb("parts", [P, E_1 + 2 * CH + 2 * P], F32R)
        WvH, WvL = parts[:, 0:LH * LD], parts[:, LH * LD:E_V]
        W1H, W1L = parts[:, E_V:E_V + 2 * FF], parts[:, E_V + 2 * FF:E_1]
        xnH, xnL = parts[:, E_1:E_1 + CH], parts[:, E_1 + CH:E_1 + 2 * CH]
        xsH, xsL = parts[:, E_1 + 2 * CH:E_1 + 2 * CH + P], parts[:, E_1 + 2 * CH + P:]
        gxH = parts[:, 0:B * T].rearrange("p (b t) -> p b t", b=B)
        gxL = parts[:, B * T:2 * B * T].rearrange("p (b t) -> p b t", b=B)
        gqH, gqL = [[parts[:, 2 * B * T + (2 * k + z) * P:2 * B * T + (2 * k + z + 1) * P] for k in range(RING)]
                    for z in range(2)]
        tabs = sb("tabs", [P, 2, 2, 2, T])
        ident = cst[:, C_ID:C_ID + P]
        centre = cst[:, C_CEN:C_CEN + P]
        meanw = cst[:, C_MEAN:C_MEAN + 1]
        caus = cst[:, C_CAUS:C_CAUS + P]
        ones4 = cst[:, C_ONE:C_ONE + 32]

        X = sb("X", [P, B, T + 1])
        X1 = sb("X1", [P, B, T + 1])
        res = sb("res", [P, TILES, D])
        arena = sb("arena", [P, 4 * 4096])
        kd = [arena[:, 4096 * i:4096 * (i + 1)].rearrange("p (j h t) -> p j h t", j=2 * NG, h=4)
              for i in range(2)]
        vd = [arena[:, 8192 + 4096 * i:8192 + 4096 * (i + 1)]
              .rearrange("p (w o n) -> p w o n", w=NW, o=2) for i in range(2)]
        vs = sb("vs", [P, 2, LH * LD])
        xs = sb("xs", [P, 2, P])
        qr = sb("qr", [P, 2 * NG, P])
        kr = sb("kr", [P, 2 * NG, P])
        sq = sb("sq", [P, 2, CH])
        swp = sb("swp", [P, 2, CH])
        ssc = sb("ssc", [P, 2 * P])
        rs = sb("rs", [P, 4, 2 * LH])
        rke = sb("rke", [P, NG, 4, HALF])
        rq8 = sb("rq8", [P, LH])
        prob = sb("prob", [P, 2, LH * 64])
        nmax = sb("nmax", [P, LH])
        den = sb("den", [P, LH])
        ptile = sb("ptile", [P, NP, P])
        osb = sb("osb", [P, LH, LD])
        otile = sb("otile", [P, NP, P])
        resf = res[:, :, :].rearrange("p t d -> p (t d)")
        fs = resf[:, 0:CH]
        xc = resf[:, CH:2 * CH]
        fsq = resf[:, 2 * CH:3 * CH]
        fr = sb("fr", [P, 4, NT])
        fre = resf[:, 3 * CH:4 * CH].rearrange("p (t k) -> p t k", t=4)
        gl = [sq[:, 0, :], sq[:, 1, :], kr[:, 0:4, :].rearrange("p a b -> p (a b)")]
        xn = qr[:, 0:4, :].rearrange("p a b -> p (a b)")
        Wv = vs[:, 0, :]
        W1 = resf[:, 0:2 * FF]
        fin = arena[:, 0:TILES * D].rearrange("p (t d) -> p t d", d=D)
        hb = [swp[:, 0, :], swp[:, 1, :], kr[:, 4:8, :].rearrange("p a b -> p (a b)")]
        gq = arena[:, 0:4096].rearrange("p (h t) -> p h t", h=REP)
        gpt_long = arena[:, 4096:8192].rearrange("p (h k t) -> p h k t", h=REP, k=NT)
        gpt_short = arena[:, 8192:10240].rearrange("p (h k t) -> p h k t", h=REP, k=NT // 2)
        gwqT = arena[:, 10240:11264].rearrange("p (h n) -> p h n", h=GH)
        gwo = arena[:, 11264:12288].rearrange("p (h n) -> p h n", h=GH)
        gM = arena[:, 12288:13312].rearrange("p (h n) -> p h n", h=GH)
        gm = arena[:, 13312:13824].rearrange("p (h n) -> p h n", h=REP)
        gva = arena[:, 13824:14848].rearrange("p (t n) -> p t n", t=TILES)
        gvl = arena[:, 14848:15104].rearrange("p (t n) -> p t n", t=NT)
        gvo = arena[:, 15104:15360].rearrange("p (k n) -> p k n", k=KV)
        gy = [arena[:, 15360 + P * i:15360 + P * (i + 1)] for i in range(2)]
        gwv = arena[:, 15616:15680]
        gwku = arena[0:LAT, 15680:15808]
        gwkdT = arena[0:LAT, 15808:16064]
        gwvu = arena[:, 16064:16096]
        gkk = arena[:, 16096:16352].rearrange("p (k n) -> p k n", k=KV)
        gp = prob
        gps = arena[:, 10240:10752]
        gst = ssc

        banks = ctx.enter_context(nc.psum_tensor("banks", [P, 8 * 512], F32))

        def bk(i):
            return banks[:, 512 * i:512 * i + 512]

        def two(i):
            return banks[:, 512 * i:512 * i + 1024]

        scores_ps = two(3).rearrange("p (h k) -> p h k", h=LH)
        outputs_ps = two(5).rearrange("p (h d) -> p h d", h=LH)

        counted = {
            "pe": ("ln_xT kk_mm m_mm va_mm wvo_mm lq_mm ls_mm lt_mm ly_mm lo_mm v_mm u_mm ss_mm qs_mm ssT_mm "
                   "rkb_mm s_mm pt_mm pv_mm ot_mm wo_mm f_mu f_rb f_var f_a f_g f_out_mm fin_mm").split(),
            "act": ("xn_H xs_cp x_init kk_cp m_cp va_cp wvo_cp gm_cp lq_cp zeroed_a lvl_cp ls_exp lt_cp ly_cp v_cp u_sq s_exp pt_cp ot_cp ss_cp qs_cp rk_cp f_re f_xc "
                   "f_sq f_gl").split(),
            "dve": ("lo_add st_bn st_ag st_eps ln_x ls_cap ls_max ls_neg ls_rec ls_nrm u_c u_s rs_0 rs_n rs_f ss_cl rqT_cp k_nrm "
                   "s_cap s_max s_sum s_inv o_nrm wo_add zeroed_v f_cp f_eps f_xn f_aff xn_L f_h x_new "
                   "fin_add").split(),
            "pool": ("zeroed wv_H wv_L w1_H w1_L xs_H xs_L gx_H gx_L gq_H gq_L tab_sc u_rot s_sub s_rq").split(),
        }
        s = {n: sem(n) for v in counted.values() for n in v}

        def credit(eng, name):
            for n in counted[name]:
                eng.sem_inc(s[n], CR)
        c_in, w_in, ffw_in, w1_in, qkvw_in, wv_in, tab_in = (
            sem(n) for n in ("c_in", "w_in", "ffw_in", "w1_in", "qkvw_in", "wv_in", "tab_in"))
        lat_w, lat_wq, res_out, res_in, out_in = (sem(n) for n in ("lat_w", "lat_wq", "res_out", "res_in", "out_in"))
        xl_in = [sem(f"xl_in{i}") for i in range(4)]
        kd_in, vd_in = [sem("kd_in0"), sem("kd_in1")], [sem("vd_in0"), sem("vd_in1")]

        block = ctx.enter_context(nc.Block())

        def slots(eng, layer, slot, after=lambda n, where: None):
            def steps(n):
                return lambda where: after(n, where)

            def flags(n):
                return n < TILES, 1 <= n <= TILES, 2 <= n <= TILES + 1, n >= 3, n + 1 < TILES, steps(n)
            for n in range(4):
                slot(layer, n // 2, n % 2, *flags(n))
            with eng.Fori(2, TILES // 2 - 1) as k:
                slot(layer, k, 0, True, True, True, True, True, lambda where: None)
                slot(layer, k, 1, True, True, True, True, True, lambda where: None)
            for n in range(TILES - 2, TILES + 3):
                slot(layer, n // 2, n % 2, *flags(n))

        def column(n):
            return n * P + n // NT

        def unit_ps(u):
            return bk((0, 1, 3, 4)[u])

        def centred_ps(c):
            return bk((0, 4, 2, 2)[c])

        def rstd_ps(c):
            return bk((1, 1, 7, 7)[c])

        def out_ps(c):
            return bk((2, 5, 6, 5)[c])

        Xf = X[:, :, :].rearrange("p b t -> p (b t)")
        X1f = X1[:, :, :].rearrange("p b t -> p (b t)")
        rows = [r for k in range(NT // 2) for r in (NT - 1 - k, k)]
        bodies = [(i, h) for k in range(NT // 2) for h in range(REP) for i in (NT - 1 - k, k)]
        LAST = len(bodies) - 1

        def due(j, long, short):
            return [bodies[k][0] for k, even in ((j - long, True), (j - short, False))
                    if 0 <= k <= LAST and (k % 2 == 0) == even and bodies[k][1] == REP - 1]

        def ahead(j):
            k = j + (4 if j % 2 == 0 else 2)
            return k if k <= LAST else None

        taken = [0, 1, 2] + [ahead(j) for j in range(LAST + 1) if ahead(j) is not None]

        def pos(j):
            return taken.index(j) + 1

        apart = [j for j in taken if bodies[j][0] > 0]

        def before(j):
            return j - (4 if j % 2 == 0 else 2)

        def bi(j):
            return (j // 2) % 2 if j % 2 == 0 else 2

        def scores_of(j):
            return two(2 * bi(j)) if j % 2 == 0 else bk(6)

        def probs_of(j):
            return gp[:, bi(j), :] if j % 2 == 0 else gps

        def gpt(i):
            return gpt_long if i >= NT // 2 else gpt_short

        def groups(i):
            return (i + 4) // 4

        def done_groups(j):
            return sum(groups(bodies[k][0]) for k in range(j))

        NTR = done_groups(len(bodies))

        @block.sync
        def _(sp):
            for q in kd_in + vd_in:
                sp.sem_inc(q, CR)
            for g in range(4):
                sp.dma_start(res[:, 4 * g:4 * g + 4, :],
                             x.rearrange("b (t p) d -> p (b t) d", p=P)[:, 4 * g:4 * g + 4, :]).then_inc(xl_in[g], 16)
            sp.dma_start(cst[:, :], cst_d).then_inc(c_in, 16)
            sp.dma_start(gwku, wku).then_inc(lat_wq, 16)
            sp.dma_start(gwkdT, wkdT).then_inc(lat_wq, 16)
            sp.dma_start(gwqT, wqT.rearrange("(h p) n -> p h n", p=P)).then_inc(lat_wq, 16)
            sp.dma_start(gwv, wvd).then_inc(lat_w, 16)
            sp.dma_start(gwo, wo.rearrange("(h p) n -> p h n", p=P)).then_inc(lat_w, 16)
            sp.dma_start(gwvu, wvuT).then_inc(lat_w, 16)

            def load_tables(layer):
                sp.dma_start(scales[:, :], par[bass.ds(layer, 1), :, 0:4].rearrange("a p n -> p (a n)")).then_inc(tab_in, 16)
                for kind in range(2):
                    for fn in range(2):
                        for hf in range(2):
                            sp.dma_start(tabs[:, kind, fn, hf, :], tab_d[3 * kind + fn * (1 + hf), :, :]).then_inc(tab_in, 16)

            def load_qk(layer):
                load_tables(layer)
                sp.dma_start(Wqk[:, :], wqkv[bass.ds(layer, 1), :, 0:2 * LH * LD].rearrange("a p n -> p (a n)")).then_inc(qkvw_in, 16)

            def load_v(layer):
                sp.dma_start(Wv, wqkv[bass.ds(layer, 1), :, 2 * LH * LD:].rearrange("a p n -> p (a n)")).then_inc(wv_in, 16)

            def load_o(layer):
                sp.dma_start(Wo[:, :, :], lwo[bass.ds(layer, 1), :, :].rearrange("a (k p) n -> p (a k) n", p=P)).then_inc(qkvw_in, 16)

            sp.wait_ge(s["lq_mm"], CR + 8)
            load_qk(0)
            load_v(0)
            load_o(0)
            out_t = out.rearrange("b (t p) d -> p (b t) d", p=P)
            sp.wait_ge(s["lo_add"], CR + B * KV * NT)
            sp.dma_start(out_t, res[:, :, :]).then_inc(res_out, 16)
            sp.wait_ge(s["zeroed"], CR + 6)
            sp.wait_ge(s["zeroed_v"], CR + 1)
            sp.wait_ge(s["zeroed_a"], CR + 1)
            with sp.Fori(0, DEPTH) as layer:
                sp.wait_ge(s["x_new"], CR + layer * NC + NC)
                sp.dma_start(parv[:, :], par[bass.ds(layer, 1), :, :].rearrange("a p n -> p (a n)")).then_inc(w_in, 16)
                sp.wait_ge(res_out, 16)
                sp.dma_start(W1, w1[bass.ds(layer, 1), :, :].rearrange("a p n -> p (a n)")).then_inc(w1_in, 16)
                sp.dma_start(W2[:, :, :], w2[bass.ds(layer, 1), :, :, :].rearrange("a p k n -> p (a k) n")).then_inc(ffw_in, 16)

                def slot(layer, k, par_, a, b, c, d, more, step):
                    n = k * 2 + par_
                    G, GK = layer * TILES + n, layer * (TILES // 2) + k
                    if a:
                        sp.wait_ge(s["k_nrm"], CR + G * 2 + 2)
                        for h in range(4):
                            sp.dma_start(kd[par_][32 * h:32 * h + 32, :, h, :], kr[32 * h:32 * h + 32, :, :]).then_inc(kd_in[par_], 16)
                        sp.wait_ge(s["pv_mm"], CR + G - 1)
                        sp.wait_ge(s["v_cp"], CR + G * 2 + 2)
                        for o in range(2):
                            r = 64 * o
                            src = vs[:, par_, 512 * o:512 * (o + 1)]
                            prev = vs[:, 1 - par_, 512 * o:512 * (o + 1)]
                            for w in range(NW):
                                sp.dma_start(vd[par_][r + 32:r + 64, w, o, :], src[32 * w:32 * w + 32, :]).then_inc(vd_in[par_], 16)
                                before = src[32 * w - 32:32 * w, :] if w else prev[96:128, :]
                                sp.dma_start(vd[par_][r:r + 32, w, o, :], before).then_inc(vd_in[par_], 16)

                slots(sp, layer, slot)
                following = sp.snap((layer + 1) % DEPTH)
                sp.wait_ge(s["u_s"], CR + (layer + 1) * TILES * 4)
                load_qk(following)
                sp.wait_ge(vd_in[1], CR + (layer + 1) * (TILES // 2) * 256)
                load_v(following)
                sp.wait_ge(s["wo_mm"], CR + (layer + 1) * TILES)
                load_o(following)
            sp.wait_ge(res_out, 16)
            sp.wait_ge(s["wo_mm"], CR + DEPTH * TILES)
            sp.dma_start(fin, out_t).then_inc(res_in, 16)
            sp.wait_ge(qkvw_in, 32 * (DEPTH + 1))
            sp.wait_ge(wv_in, 16 * (DEPTH + 1))
            sp.wait_ge(tab_in, 144 * (DEPTH + 1))
            for g4 in range(TILES // 4):
                sp.wait_ge(s["fin_add"], CR + g4 + 1)
                sp.dma_start(out_t[:, 4 * g4:4 * g4 + 4, :], fin[:, 4 * g4:4 * g4 + 4, :]).then_inc(out_in, 16)
            sp.wait_ge(out_in, 16 * (TILES // 4))

        @block.gpsimd
        def _(pool):
            credit(pool, "pool")
            pool.memset(X[:, :, 0:1], 0.0).then_inc(s["zeroed"], 1)
            pool.memset(X1[:, :, 0:1], 0.0).then_inc(s["zeroed"], 1)
            pool.memset(vs[:, 1, :], 0.0).then_inc(s["zeroed"], 1)
            def scale_table(layer, m):
                kind, fn, hf = m // 4, m // 2 % 2, m % 2
                v = 2 * kind + hf
                pool.wait_ge(tab_in, layer * 144 + 144)
                pool.tensor_tensor(tabs[:, kind, fn, hf, :], tabs[:, kind, fn, hf, :],
                                   scales[:, v:v + 1].to_broadcast([P, T]), ALU.mult).then_inc(s["tab_sc"], 1)

            def scale_tables(layer):
                for m in range(8):
                    scale_table(layer, m)

            def split(w, wH, wL, nameH, nameL, count):
                one = cst[:, C_1:C_1 + 1].to_broadcast([P, w.shape[-1]])
                pool.tensor_tensor(wH, w, one, ALU.mult).then_inc(s[nameH], 1)
                pool.wait_ge(s[nameH], CR + count)
                pool.tensor_tensor(wL, w, wH, ALU.subtract).then_inc(s[nameL], 1)

            def split_values(layer):
                pool.wait_ge(wv_in, layer * 16 + 16)
                split(Wv, WvH[:, :], WvL[:, :], "wv_H", "wv_L", layer + 1)

            pool.wait_ge(c_in, 16)
            for g4 in range(TILES // 4):
                pool.wait_ge(s["x_init"], CR + g4 + 1)
                b, t0 = divmod(4 * P * g4, T)
                split(X[:, b, 1 + t0:1 + t0 + 4 * P], gxH[:, b, t0:t0 + 4 * P], gxL[:, b, t0:t0 + 4 * P], "gx_H", "gx_L", g4 + 1)

            def latent(it, tables):
                for k, j in enumerate(apart):
                    i, h = bodies[j]
                    pool.wait_ge(s["lq_cp"], CR + it * 8 + 2 * h + i // 4 + 1)
                    pool.wait_ge(s["ls_mm"], CR + (it if k >= RING else it - 1) * len(bodies) + pos(apart[k - RING]))
                    split(gq[:, h, P * i:P * i + P], gqH[k % RING], gqL[k % RING], "gq_H", "gq_L", it * len(apart) + k + 1)
                    if tables and 4 <= k < 12:
                        scale_table(0, k - 4)

            with pool.Fori(0, B * KV - 1) as it:
                latent(it, False)
            latent(B * KV - 1, True)
            pool.wait_ge(s["ls_mm"], CR + B * KV * len(bodies))
            split_values(0)
            pool.wait_ge(s["lo_add"], CR + B * KV * NT)
            pool.wait_ge(lat_w, 48)
            pool.wait_ge(s["lq_mm"], CR + B * KV * 8)
            pool.memset(ssc[:, :], 0.0).then_inc(s["zeroed"], 1)
            for i in range(2):
                pool.memset(arena[:, 4096 * i:4096 * (i + 1)], 0.0).then_inc(s["zeroed"], 1)

            with pool.Fori(0, DEPTH) as layer:
                def slot(layer, k, par_, a, b, c, d, more, step):
                    n = k * 2 + par_
                    G, GK = layer * TILES + n, layer * (TILES // 2) + k

                    def add(u):
                        pool.wait_ge(s["u_s"], CR + G * 4 + u + 1)
                        dst = kr[:, 4 * u:4 * u + 4, :] if u < 2 else qr[:, 4 * (u - 2):4 * (u - 2) + 4, :]
                        pool.tensor_tensor(dst, dst, swp[:, u % 2, :].rearrange("p (j t) -> p j t", j=4),
                                           ALU.add).then_inc(s["u_rot"], 1)

                    if a:
                        pool.wait_ge(s["xs_cp"], CR + G * 2 + 2)
                        pool.wait_ge(s["v_mm"], CR + G * 2)
                        split(xs[:, par_, :], xsH[:, :], xsL[:, :], "xs_H", "xs_L", G + 1)
                        add(0)
                        add(1)
                    step("mid")
                    if b:
                        sm3 = prob[:, 1 - par_, :].rearrange("p (i h k) -> p i h k", i=2, h=LH // 2)
                        for i in range(2):
                            pool.wait_ge(s["s_max"], CR + G * 2 - 1 + i)
                            m = nmax[:, 8 * i:8 * i + 8].rearrange("p (h o) -> p h o", o=1).to_broadcast([P, LH // 2, 64])
                            pool.tensor_tensor(sm3[:, i, :, :], sm3[:, i, :, :], m, ALU.subtract).then_inc(s["s_sub"], 1)
                        pool.wait_ge(s["rqT_cp"], CR + G)
                        for i in range(2):
                            pool.wait_ge(s["s_sub"], CR + G * 2 - 1 + i)
                            r = rq8[:, 8 * i:8 * i + 8].rearrange("p (h o) -> p h o", o=1).to_broadcast([P, LH // 2, 64])
                            pool.tensor_tensor(sm3[:, i, :, :], sm3[:, i, :, :], r, ALU.mult).then_inc(s["s_rq"], 1)
                    if a:
                        add(2)
                        add(3)

                def early(n, where):
                    if n == 3:
                        pool.wait_ge(w1_in, layer * 16 + 16)
                        split(W1, W1H[:, :], W1L[:, :], "w1_H", "w1_L", layer + 1)

                slots(pool, layer, slot, early)
                scale_tables(layer + 1)
                split_values(layer + 1)

        @block.scalar
        def _(act):
            credit(act, "act")
            act.wait_ge(s["kk_mm"], CR + 1)
            act.activation(gkk, bk(3)[:, 0:KV * P].rearrange("p (k n) -> p k n", k=KV), ACT.Copy).then_inc(s["kk_cp"], 1)
            act.wait_ge(s["m_mm"], CR + 2)
            act.activation(gM, two(4).rearrange("p (h n) -> p h n", h=GH), ACT.Copy).then_inc(s["m_cp"], 1)
            for g4 in range(TILES // 4):
                act.wait_ge(s["ln_xT"], CR + g4 + 1)
                b, t0 = divmod(4 * g4, NT)
                act.activation(X[:, b, 1 + P * t0:1 + P * (t0 + 4)], bk(g4 % 2), ACT.Copy).then_inc(s["x_init"], 1)

            def head_weights(it):
                act.wait_ge(s["m_cp"], CR + 1)
                act.wait_ge(s["lq_mm"], CR + it * 8)
                kv = it % KV
                kv = kv if isinstance(kv, int) else act.snap(kv)
                act.activation(gm, gM[:, bass.ds(kv * REP, REP), :], ACT.Copy).then_inc(s["gm_cp"], 1)

            def copy_queries(it, r):
                for i in r:
                    act.wait_ge(s["lq_mm"], CR + it * 8 + i + 1)
                    act.activation(gq[:, i // 2, 512 * (i % 2):512 * (i % 2) + 512], bk(i % 2), ACT.Copy).then_inc(s["lq_cp"], 1)

            head_weights(0)
            act.wait_ge(s["va_mm"], CR + 1)
            act.activation(gva, two(6).rearrange("p (t n) -> p t n", t=TILES), ACT.Copy).then_inc(s["va_cp"], 1)
            act.wait_ge(s["wvo_mm"], CR + 2)
            act.activation(gvo, bk(2)[:, 0:2 * D].rearrange("p (k n) -> p k n", k=KV), ACT.Copy).then_inc(s["wvo_cp"], 1)
            copy_queries(0, range(8))

            def latent(it, more):
                act.wait_ge(s["va_cp"], CR + 1)
                act.wait_ge(s["ly_mm"], CR + it * NT)
                b, kv = it // KV, it % KV
                if not isinstance(it, int):
                    b, kv = act.snap(b), act.snap(kv)
                act.activation(gvl, gva[:, bass.ds(b * NT, NT), bass.ds(kv * LAT, LAT)], ACT.Copy).then_inc(s["lvl_cp"], 1)

                def exps(j):
                    n = (bodies[j][0] + 1) * P
                    act.wait_ge(s["ls_neg"], CR + it * len(bodies) + pos(j))
                    act.wait_ge(s["lt_mm"], CR + it * NTR + (done_groups(before(j) + 1) if before(j) >= 0 else 0))
                    act.activation(probs_of(j)[:, 0:n], scores_of(j)[:, 0:n], ACT.Exp, bias=gst[:, 8 + bi(j):9 + bi(j)],
                                   scale=G_SCALE, accum_out=gst[:, 12 + bi(j):13 + bi(j)]).then_inc(s["ls_exp"], 1)

                def evacuate(j):
                    i, h = bodies[j]
                    if h == 0:
                        act.wait_ge(s["ly_mm"], CR + it * NT + rows.index(i) - 1)
                    for g in range(groups(i)):
                        k = done_groups(j) + g
                        act.wait_ge(s["lt_mm"], CR + it * NTR + k + 1)
                        nb = min(4, i + 1 - 4 * g)
                        act.activation(gpt(i)[:, h, 4 * g:4 * g + nb, :],
                                       bk(4 + k % 2)[:, 0:P * nb].rearrange("p (k t) -> p k t", k=nb), ACT.Copy)\
                           .then_inc(s["lt_cp"], 1)

                def copy_outputs(i):
                    r = rows.index(i)
                    act.wait_ge(s["ly_mm"], CR + it * NT + r + 1)
                    act.wait_ge(s["lo_mm"], CR + it * NT + r - 1)
                    act.activation(gy[r % 2], bk(7)[:, P:2 * P], ACT.Copy).then_inc(s["ly_cp"], 1)

                for j in range(3):
                    exps(j)
                for j in range(len(bodies)):
                    if more and j == LAST - 3:
                        head_weights(it + 1)
                    if more and j == LAST - 1:
                        copy_queries(it + 1, range(3))
                    if more and j == LAST:
                        copy_queries(it + 1, range(3, 6))
                    evacuate(j)
                    for i in due(j, 1, 2):
                        copy_outputs(i)
                    if ahead(j) is not None:
                        exps(ahead(j))
                if more:
                    copy_queries(it + 1, range(6, 8))
                copy_outputs(rows[-1])

            with act.Fori(0, B * KV - 1) as it:
                latent(it, True)
            latent(B * KV - 1, False)
            act.wait_ge(s["lo_mm"], CR + B * KV * NT)
            act.activation(arena[:, 13824:].rearrange("p (k t) -> p k t", t=P),
                           ident.rearrange("p (o t) -> p o t", o=1).to_broadcast([P, 20, P]), ACT.Copy,
                           scale=0.0).then_inc(s["zeroed_a"], 1)

            act.wait_ge(s["zeroed"], CR + 4)

            def shift(layer, n, par_):
                act.wait_ge(s["x_new"], CR + layer * NC + n // 4 + 1)
                act.wait_ge(s["u_mm"], CR + (layer * TILES + n) * 4 - 4)
                act.activation(xs[0:64, par_, :], Xf[0:64, bass.ds(column(n) + 1, P)], ACT.Copy).then_inc(s["xs_cp"], 1)
                act.activation(xs[64:128, par_, :], Xf[64:128, bass.ds(column(n), P)], ACT.Copy).then_inc(s["xs_cp"], 1)

            with act.Fori(0, DEPTH) as layer:
                def slot(layer, k, par_, a, b, c, d, more, step):
                    n = k * 2 + par_
                    G, GK = layer * TILES + n, layer * (TILES // 2) + k
                    if a:
                        square(G, 0)
                        square(G, 1)
                        act.wait_ge(s["ss_mm"], CR + G * 2 + 2)
                        act.activation(ssc[:, P:2 * P], bk(2)[:, P:2 * P], ACT.Copy).then_inc(s["ss_cp"], 1)
                    if c:
                        for i in range(2):
                            act.wait_ge(s["pt_mm"], CR + (G - 2) * 2 + i + 1)
                            act.activation(ptile[:, 4 * i:4 * i + 4, :], bk(5 + i).rearrange("p (k t) -> p k t", k=4),
                                           ACT.Copy).then_inc(s["pt_cp"], 1)
                    step("mid")
                    if a and not b:
                        square(G, 2)
                        square(G, 3)
                    if a:
                        act.wait_ge(s["rs_n"], CR + (layer * (TILES + 1) + n + 1) * 11)
                        act.activation(rke[:, :, :, :].rearrange("p g h r -> p (g h) r"),
                                       rs[:, 2, LH:2 * LH].rearrange("p (h o) -> p h o", o=1).to_broadcast([P, LH, HALF]),
                                       ACT.Copy).then_inc(s["rk_cp"], 1)
                        if b and not c:
                            square(G, 2)
                            square(G, 3)
                            shift(layer, n + 1, 1 - par_)
                        act.wait_ge(vd_in[1 - par_], CR + (GK + par_) * 256)
                        act.wait_ge(s["wv_L"], CR + layer + 1)
                        for i in range(2):
                            act.wait_ge(s["v_mm"], CR + G * 2 + i + 1)
                            act.activation(vs[:, par_, 512 * i:512 * (i + 1)], bk(i), ACT.Copy).then_inc(s["v_cp"], 1)
                        if more and (c or not b):
                            shift(layer, n + 1, 1 - par_)
                        if c:
                            square(G, 2)
                            square(G, 3)
                    step("late")
                    if c:
                        for i in range(2):
                            act.wait_ge(s["ot_mm"], CR + (G - 2) * 2 + i + 1)
                            act.activation(otile[:, 4 * i:4 * i + 4, :], bk(5 + 2 * i).rearrange("p (k t) -> p k t", k=4),
                                           ACT.Copy).then_inc(s["ot_cp"], 1)
                    if a:
                        act.wait_ge(s["qs_mm"], CR + G * 2 + 2)
                        act.activation(ssc[:, 0:P], bk(2)[:, 0:P], ACT.Copy).then_inc(s["qs_cp"], 1)
                    step("exp")
                    if b:
                        act.wait_ge(s["s_rq"], CR + G * 2)
                        act.activation(prob[:, 1 - par_, :], prob[:, 1 - par_, :], ACT.Exp).then_inc(s["s_exp"], 1)
                    step("end")

                def square(G, u):
                    act.wait_ge(s["u_mm"], CR + G * 4 + u + 1)
                    if u < 2:
                        act.wait_ge(s["qs_mm"], CR + G * 2 + u - 1)
                    else:
                        act.wait_ge(s["ss_mm"], CR + G * 2 + u - 1)
                    act.activation(sq[:, u % 2, :], unit_ps(u), ACT.Square).then_inc(s["u_sq"], 1)

                def ln_square(c):
                    F = layer * NC + c
                    act.wait_ge(s["f_mu"], CR + F + 1)
                    act.wait_ge(s["f_xn"], CR + F)
                    act.activation(xc[:, :], centred_ps(c), ACT.Copy).then_inc(s["f_xc"], 1)
                    act.activation(fsq[:, :], centred_ps(c), ACT.Square).then_inc(s["f_sq"], 1)

                def spread_rstd(c):
                    if c:
                        act.wait_ge(s["rs_f"], CR + (layer * (NC - 1) + c) * 11)
                        rstd = fr[:, 2, 0:4]
                    else:
                        act.wait_ge(s["rs_n"], CR + (layer + 1) * (TILES + 1) * 11)
                        rstd = rs[:, 2, LH:LH + 4]
                    act.activation(fre[:, :, :], rstd.rearrange("p (t o) -> p t o", o=1).to_broadcast([P, 4, P]),
                                   ACT.Copy).then_inc(s["f_re"], 1)

                def upper(c):
                    F = layer * NC + c
                    act.wait_ge(s["f_aff"], CR + F + 1)
                    act.wait_ge(s["f_g"], CR + F * 3)
                    act.wait_ge(s["f_a"], CR + F * 3)
                    act.activation(xnH[:, :], xn[:, :], ACT.Copy).then_inc(s["xn_H"], 1)

                def gelu(c, j):
                    F, m = layer * NC + c, FJ[j][1]
                    act.wait_ge(s["f_g"], CR + F * 3 + j + 1)
                    act.wait_ge(s["f_h"], CR + F * 3 + j - 2)
                    act.activation(gl[j][0:m, :], bk(3 + j % 2)[0:m, :], ACT.Gelu,
                                   bias=parv[0:m, V_B1G + j:V_B1G + j + 1]).then_inc(s["f_gl"], 1)

                def early(n, where):
                    if (n, where) == (TILES - 1, "end"):
                        ln_square(0)
                    if (n, where) == (TILES, "mid"):
                        spread_rstd(0)
                    if (n, where) == (TILES, "late"):
                        upper(0)
                    if (n, where) == (TILES, "end"):
                        gelu(0, 0)
                    if (n, where) == (TILES + 1, "mid"):
                        gelu(0, 1)
                    if (n, where) == (TILES + 1, "late"):
                        gelu(0, 2)
                        ln_square(1)

                shift(layer, 0, 0)
                slots(act, layer, slot, early)
                spread_rstd(1)
                ln_square(2)
                upper(1)
                for c in range(1, NC):
                    gelu(c, 0)
                    if c + 1 < NC:
                        spread_rstd(c + 1)
                    gelu(c, 1)
                    gelu(c, 2)
                    if c + 1 < NC:
                        upper(c + 1)
                    if c + 2 < NC:
                        ln_square(c + 2)

        @block.vector
        def _(dve):
            credit(dve, "dve")
            def rsqrt(w, n, name, count):
                x, h, y, q = (w[:, k, 0:n] for k in range(4))
                dve.tensor_scalar(h, x, -0.5, None, ALU.mult).then_inc(s[name], 1)
                dve.tensor_scalar(y.bitcast(mybir.dt.int32), x.bitcast(mybir.dt.int32), -0.5, float(0x5F3759DF),
                                  ALU.mult, ALU.add).then_inc(s[name], 1)
                for k in range(3):
                    dve.wait_ge(s[name], count + 3 * k + 2)
                    dve.tensor_tensor(q, y, y, ALU.mult).then_inc(s[name], 1)
                    dve.wait_ge(s[name], count + 3 * k + 3)
                    dve.tensor_tensor(q, q, h, ALU.mult).then_inc(s[name], 1)
                    dve.wait_ge(s[name], count + 3 * k + 4)
                    dve.scalar_tensor_tensor(y, q, 1.5, y, ALU.add, ALU.mult).then_inc(s[name], 1)
                dve.wait_ge(s[name], count + 11)

            st6 = otile[:, 0, 0:6 * TILES].rearrange("p (t k) -> p t k", k=6)
            ag = otile[:, 1, 0:2 * TILES].rearrange("p (t k) -> p t k", k=2)
            for t in range(TILES):
                if t % 4 == 0:
                    dve.wait_ge(xl_in[t // 4], 16)
                dve.bn_stats(st6[:, t, :], res[:, t, :]).then_inc(s["st_bn"], 1)
            for t in range(TILES):
                dve.wait_ge(s["st_bn"], CR + t + 1)
                dve.bn_aggr(ag[:, t, :], st6[:, t, :]).then_inc(s["st_ag"], 1)
            dve.wait_ge(s["st_ag"], CR + TILES)
            dve.tensor_scalar(rs[:, 0, 0:TILES], ag[:, :, 1], 1e-5, None, ALU.add).then_inc(s["st_eps"], 1)
            dve.wait_ge(s["st_eps"], CR + 1)
            rsqrt(rs, TILES, "rs_0", CR)
            xln = prob[:, :, :].rearrange("p a (t d) -> p (a t) d", d=D)
            for t in range(TILES):
                dve.tensor_scalar(xln[:, t, :], res[:, t, :], ag[:, t, 0:1], rs[:, 2, t:t + 1], ALU.subtract, ALU.mult)\
                   .then_inc(s["ln_x"], 1)
            dve.wait_ge(s["x_init"], CR + TILES // 4)
            dve.sem_inc(s["x_new"], NC)

            def add_out(it, i):
                tile = (it // KV) * NT + i
                r = res[:, bass.ds(tile, 1), :].rearrange("p a d -> p (a d)")
                dve.wait_ge(s["lo_mm"], CR + it * NT + rows.index(i) + 1)
                dve.tensor_tensor(r, bk(7)[:, 0:D], r, ALU.add).then_inc(s["lo_add"], 1)

            def latent(it):
                def inverse(j):
                    dve.wait_ge(s["ls_exp"], CR + it * len(bodies) + pos(j))
                    dve.reciprocal(gst[:, 16 + bi(j):17 + bi(j)], gst[:, 12 + bi(j):13 + bi(j)]).then_inc(s["ls_rec"], 1)

                def normalise(j):
                    pr = probs_of(j)[:, 0:(bodies[j][0] + 1) * P]
                    dve.wait_ge(s["ls_rec"], CR + it * len(bodies) + j + 1)
                    dve.tensor_scalar(pr, pr, gst[:, 16 + bi(j):17 + bi(j)], None, ALU.mult).then_inc(s["ls_nrm"], 1)

                def cap(e):
                    n, S = (bodies[e][0] + 1) * P, scores_of(e)
                    dve.wait_ge(s["ls_mm"], CR + it * len(bodies) + pos(e))
                    dve.tensor_tensor(S[:, n - P:n], S[:, n - P:n], caus, ALU.min).then_inc(s["ls_cap"], 1)

                def peak(e):
                    n, E = (bodies[e][0] + 1) * P, it * len(bodies) + pos(e)
                    dve.wait_ge(s["ls_cap"], CR + E)
                    dve.reduce_max(gst[:, 4 + bi(e):5 + bi(e)], scores_of(e)[:, 0:n], AXX).then_inc(s["ls_max"], 1)
                    dve.wait_ge(s["ls_max"], CR + E)
                    dve.tensor_scalar(gst[:, 8 + bi(e):9 + bi(e)], gst[:, 4 + bi(e):5 + bi(e)], -G_SCALE, None, ALU.mult)\
                       .then_inc(s["ls_neg"], 1)

                for e in range(3):
                    cap(e)
                    peak(e)
                inverse(0)
                for j in range(len(bodies)):
                    normalise(j)
                    if ahead(j) is not None:
                        cap(ahead(j))
                    if j < LAST:
                        inverse(j + 1)
                    if ahead(j) is not None:
                        peak(ahead(j))
                    for i in due(j, 2, 3):
                        add_out(it, i)
                for i in rows[-2:]:
                    add_out(it, i)

            with dve.Fori(0, B * KV - 1) as it:
                latent(it)
            latent(B * KV - 1)

            dve.memset(arena[:, 8192:13824], 0.0).then_inc(s["zeroed_v"], 1)
            with dve.Fori(0, DEPTH) as layer:
                dve.wait_ge(s["tab_sc"], CR + layer * 8 + 8)

                def rotate(G, GK, n, par_, u):
                    tb = tabs[:, 1 - u // 2, :, :, bass.ds((n % NT) * P, P)]
                    src = unit_ps(u).rearrange("p (g a t) -> p g a t", g=2, a=2)
                    dve.wait_ge(s["u_sq"], CR + G * 4 + u + 1)
                    if u < 2:
                        dve.wait_ge(kd_in[1 - par_], CR + (GK + par_) * 64)
                        dst = kr[:, 4 * u:4 * u + 4, :]
                    else:
                        dve.wait_ge(s["s_mm"], CR + G * 2)
                        dst = qr[:, 4 * (u - 2):4 * (u - 2) + 4, :]
                    dst = dst.rearrange("p (g a) t -> p g a t", g=2)
                    for g in range(2):
                        ins = dve.tensor_tensor(dst[:, g, :, :], src[:, g, :, :], tb[:, 0, :, :], ALU.mult)
                    ins.then_inc(s["u_c"], 1)
                    dve.wait_ge(s["u_rot"], CR + G * 4 + u - 1)
                    sw = swp[:, u % 2, :].rearrange("p (g a t) -> p g a t", g=2, a=2)[:, :, ::-1, :]
                    for g in range(2):
                        ins = dve.tensor_tensor(sw[:, g, :, :], src[:, g, :, :], tb[:, 1, :, :], ALU.mult)
                    ins.then_inc(s["u_s"], 1)

                def slot(layer, k, par_, a, b, c, d, more, step):
                    n = k * 2 + par_
                    G, GK = layer * TILES + n, layer * (TILES // 2) + k
                    sm3 = prob[:, 1 - par_, :].rearrange("p (i h k) -> p i h k", i=2, h=LH // 2)
                    if a:
                        rotate(G, GK, n, par_, 0)
                        rotate(G, GK, n, par_, 1)
                    if d:
                        dve.wait_ge(s["wo_mm"], CR + G - 2)
                        at = column(n - 3) + 1
                        dve.tensor_tensor(X1f[:, bass.ds(at, P)], bk(7)[:, 0:P], Xf[:, bass.ds(at, P)], ALU.add)\
                           .then_inc(s["wo_add"], 1)
                    if a or b:
                        N = layer * (TILES + 1) + n
                        dve.wait_ge(s["ssT_mm"], CR + N + 1)
                        dve.wait_ge(s["rk_cp"], CR + G)
                        gs = 2 * NG if a else NG
                        dve.tensor_scalar(rs[:, 0, 0:4 * gs].rearrange("p (g h) -> p g h", g=gs),
                                          bk(2)[:, 0:32 * gs].rearrange("p (g h) -> p g h", g=gs)[:, :, 0:4], 1e-24, None,
                                          ALU.max).then_inc(s["ss_cl"], 1)
                        step("norms")
                        dve.wait_ge(s["ss_cl"], CR + N + 1)
                        rsqrt(rs, 2 * LH, "rs_n", CR + N * 11)
                    if b:
                        dve.wait_ge(s["s_rq"], CR + G * 2 - 2)
                        dve.tensor_scalar(rq8[:, :], rs[:, 2, 0:LH], QK_SCALE, None, ALU.mult).then_inc(s["rqT_cp"], 1)
                    if c:
                        dve.wait_ge(s["s_exp"], CR + G - 1)
                        dve.reduce_sum(den[:, :], prob[:, par_, :].rearrange("p (h k) -> p h k", h=LH), AXX).then_inc(s["s_sum"], 1)
                        dve.wait_ge(s["s_sum"], CR + G - 1)
                        dve.reciprocal(den[:, :], den[:, :]).then_inc(s["s_inv"], 1)
                    step("mid")
                    if b:
                        cap = cst[:, bass.ds(((n - 1) % NT) * 64 + C_CAP, 64)]
                        dve.wait_ge(s["pt_mm"], CR + G * 2 - 4)
                        for i in range(2):
                            dve.wait_ge(s["s_mm"], CR + G * 2 - 1 + i)
                            dve.tensor_tensor(sm3[:, i, :, :], bk(3 + i).rearrange("p (h k) -> p h k", h=LH // 2),
                                              cap.rearrange("p (o k) -> p o k", o=1).to_broadcast([P, LH // 2, 64]),
                                              ALU.min).then_inc(s["s_cap"], 1)
                        step("capped")
                        dve.wait_ge(s["s_sub"], CR + G * 2 - 2)
                        for i in range(2):
                            dve.wait_ge(s["s_cap"], CR + G * 2 - 1 + i)
                            dve.reduce_max(nmax[:, 8 * i:8 * i + 8], sm3[:, i, :, :], AXX).then_inc(s["s_max"], 1)
                    if a:
                        dve.wait_ge(s["rkb_mm"], CR + G + 1)
                        dve.wait_ge(s["u_rot"], CR + G * 4 + 2)
                        rk = bk(2).rearrange("p (g o t) -> p g o t", g=NG, o=1)
                        for i in range(2):
                            k4 = kr[:, 4 * i:4 * i + 4, :].rearrange("p (g a) t -> p g a t", g=2)
                            dve.tensor_tensor(k4, rk[:, 2 * i:2 * i + 2, :, :].to_broadcast([P, 2, 2, P]), k4, ALU.mult)\
                               .then_inc(s["k_nrm"], 1)
                    if c:
                        dve.wait_ge(s["pv_mm"], CR + G - 1)
                        dve.wait_ge(s["s_inv"], CR + G - 1)
                        dve.tensor_tensor(osb[:, :, :], outputs_ps,
                                          den[:, :].rearrange("p (h o) -> p h o", o=1).to_broadcast([P, LH, LD]),
                                          ALU.mult).then_inc(s["o_nrm"], 1)
                    if a:
                        rotate(G, GK, n, par_, 2)
                        rotate(G, GK, n, par_, 3)
                    step("end")

                def shifted(c):
                    F = layer * NC + c
                    b, t0 = divmod(c * CH, T)
                    dve.wait_ge(s["wo_add"], CR + layer * TILES + (c + 1) * CH // P)
                    dve.wait_ge(s["f_mu"], CR + F)
                    dve.tensor_copy(fs[0:64, :], X1[0:64, b, 1 + t0:1 + t0 + CH]).then_inc(s["f_cp"], 1)
                    dve.tensor_copy(fs[64:128, :], X1[64:128, b, t0:t0 + CH]).then_inc(s["f_cp"], 1)

                def variance(c):
                    F = layer * NC + c
                    dve.wait_ge(s["f_var"], CR + F + 1)
                    dve.wait_ge(s["f_re"], CR + F)
                    to = fr[:, 0, 0:4] if c else rs[:, 0, LH:LH + 4]
                    dve.tensor_scalar(to, rstd_ps(c)[:, 0:4], 1e-5, None, ALU.add).then_inc(s["f_eps"], 1)
                    dve.wait_ge(s["f_eps"], CR + F + 1)
                    if c:
                        rsqrt(fr, 4, "rs_f", CR + (layer * (NC - 1) + c - 1) * 11)

                def affine(c):
                    F = layer * NC + c
                    dve.wait_ge(s["f_rb"], CR + F + 1)
                    dve.tensor_tensor(xn[:, :], rstd_ps(c), xc[:, :], ALU.mult).then_inc(s["f_xn"], 1)
                    dve.wait_ge(s["f_xn"], CR + F + 1)
                    dve.tensor_scalar(xn[:, :], xn[:, :], parv[:, V_G:V_G + 1], parv[:, V_B:V_B + 1], ALU.mult, ALU.add)\
                       .then_inc(s["f_aff"], 1)

                def lower(c):
                    F = layer * NC + c
                    dve.wait_ge(s["xn_H"], CR + F + 1)
                    dve.tensor_tensor(xnL[:, :], xn[:, :], xnH[:, :], ALU.subtract).then_inc(s["xn_L"], 1)

                def gated(c, j):
                    F = layer * NC + c
                    m = FJ[j][1]
                    dve.wait_ge(s["f_a"], CR + F * 3 + j + 1)
                    dve.wait_ge(s["f_gl"], CR + F * 3 + j + 1)
                    dve.wait_ge(s["f_out_mm"], CR + F)
                    dve.scalar_tensor_tensor(hb[j][0:m, :], bk(j % 2)[0:m, :], parv[0:m, V_B1A + j:V_B1A + j + 1],
                                             gl[j][0:m, :], ALU.add, ALU.mult).then_inc(s["f_h"], 1)

                def finish(c):
                    F = layer * NC + c
                    b, t0 = divmod(c * CH, T)
                    dve.wait_ge(s["f_out_mm"], CR + F + 1)
                    dve.wait_ge(s["xs_cp"], CR + (layer + 1) * TILES * 2)
                    dve.scalar_tensor_tensor(X[:, b, 1 + t0:1 + t0 + CH], out_ps(c), parv[:, V_B2:V_B2 + 1],
                                             X1[:, b, 1 + t0:1 + t0 + CH], ALU.add, ALU.add).then_inc(s["x_new"], 1)

                def early(n, where):
                    if (n, where) == (TILES - 2, "end"):
                        dve.wait_ge(res_out, 16)
                        shifted(0)
                    if (n, where) == (TILES, "norms"):
                        variance(0)
                    if (n, where) == (TILES, "mid"):
                        dve.wait_ge(w_in, layer * 16 + 16)
                        affine(0)
                    if (n, where) == (TILES, "capped"):
                        lower(0)
                    if (n, where) == (TILES, "end"):
                        shifted(1)
                    if (n, where) == (TILES + 1, "mid"):
                        gated(0, 0)
                        gated(0, 1)
                    if (n, where) == (TILES + 1, "end"):
                        gated(0, 2)
                        shifted(2)
                        variance(1)
                        finish(0)

                slots(dve, layer, slot, early)
                affine(1)
                lower(1)
                for c in range(1, NC):
                    if c + 1 < NC:
                        variance(c + 1)
                    gated(c, 0)
                    if c + 2 < NC:
                        shifted(c + 2)
                    gated(c, 1)
                    if c + 1 < NC:
                        affine(c + 1)
                    gated(c, 2)
                    if c + 1 < NC:
                        lower(c + 1)
                    finish(c)

            dve.wait_ge(res_in, 16)
            for g4 in range(TILES // 4):
                dve.wait_ge(s["fin_mm"], CR + g4 + 1)
                r4 = fin[:, 4 * g4:4 * g4 + 4, :]
                dve.tensor_tensor(r4, bk(g4 % 2).rearrange("p (t d) -> p t d", t=4), r4, ALU.add).then_inc(s["fin_add"], 1)

        @block.tensor
        def _(pe):
            credit(pe, "pe")
            def mm(o, l, r, start=True, stop=True):
                return pe.matmul(o, l, r, start=start, stop=stop)

            pe.wait_ge(lat_wq, 48)
            for kv in range(KV):
                ins = mm(bk(3)[:, P * kv:P * kv + P], gwku, gwkdT[:, P * kv:P * kv + P])
            ins.then_inc(s["kk_mm"], 1)
            pe.wait_ge(s["kk_cp"], CR + 1)
            for kv in range(KV):
                for h in range(REP):
                    ins = mm(bk(4 + kv)[:, P * h:P * h + P], gwqT[:, kv * REP + h, :], gkk[:, kv, :])
                ins.then_inc(s["m_mm"], 1)
            pe.wait_ge(c_in, 16)
            xln = prob[:, :, :].rearrange("p a (t d) -> p (a t) d", d=D)
            for g4 in range(TILES // 4):
                if g4 >= 2:
                    pe.wait_ge(s["x_init"], CR + g4 - 1)
                pe.wait_ge(s["ln_x"], CR + 4 * g4 + 4)
                for k in range(4):
                    ins = pe.transpose(bk(g4 % 2)[:, P * k:P * k + P], xln[:, 4 * g4 + k, :], ident)
                ins.then_inc(s["ln_xT"], 1)
            pe.wait_ge(lat_w, 48)
            pe.wait_ge(s["x_init"], CR + TILES // 4)
            for t in range(TILES):
                b, t0 = divmod(t, NT)
                ins = mm(two(6)[:, 2 * LAT * t:2 * LAT * (t + 1)], X[:, b, 1 + P * t0:1 + P * (t0 + 1)], gwv)
            ins.then_inc(s["va_mm"], 1)
            for kv in range(KV):
                for h in range(REP):
                    ins = mm(bk(2)[32 * h:32 * h + 32, D * kv:D * kv + D], gwvu, gwo[:, kv * REP + h, :])
                ins.then_inc(s["wvo_mm"], 1)

            def queries(it, r):
                b = it // KV
                b = b if isinstance(it, int) else pe.snap(b)
                pe.wait_ge(s["gm_cp"], CR + it + 1)
                for i in r:
                    pe.wait_ge(s["lq_cp"], CR + it * 8 + i - 1)
                    pe.wait_ge(s["ls_exp"], CR + (it - 1) * len(bodies) + pos(LAST - 3))
                    mm(bk(i % 2), gm[:, i // 2, :],
                       X[:, bass.ds(b, 1), 1 + 512 * (i % 2):1 + 512 * (i % 2 + 1)].rearrange("p a n -> p (a n)"))\
                        .then_inc(s["lq_mm"], 1)

            queries(0, range(8))
            pe.wait_ge(s["va_cp"], CR + 1)
            pe.wait_ge(s["wvo_cp"], CR + 1)

            def latent(it, more):
                b = it // KV if isinstance(it, int) else pe.snap(it // KV)
                kv = it % KV if isinstance(it, int) else pe.snap(it % KV)

                def scores(j):
                    i, h = bodies[j]
                    n = (i + 1) * P
                    pe.wait_ge(s["ls_exp"], CR + it * len(bodies) + (pos(before(j)) if before(j) >= 0 else 0))
                    if i:
                        q = apart.index(j)
                        pe.wait_ge(s["gq_L"], CR + it * len(apart) + q + 1)
                        qH, qL = gqH[q % RING], gqL[q % RING]
                    for k in range(0, n, 512):
                        w = min(512, n - k)
                        o = scores_of(j)[:, k:k + w]
                        if w >= 256:
                            xH, xL = [x_[:, bass.ds(b, 1), k:k + w].rearrange("p a n -> p (a n)") for x_ in (gxH, gxL)]
                            mm(o, qH, xH, True, False)
                            mm(o, qH, xL, False, False)
                            ins = mm(o, qL, xH, False, True)
                        else:
                            ins = mm(o, gq[:, h, P * i:P * i + P],
                                     X[:, bass.ds(b, 1), 1 + k:1 + k + w].rearrange("p a n -> p (a n)"))
                    ins.then_inc(s["ls_mm"], 1)

                def finish(j):
                    i, h = bodies[j]
                    pe.wait_ge(s["ls_nrm"], CR + it * len(bodies) + j + 1)
                    for g in range(groups(i)):
                        k = done_groups(j) + g
                        pe.wait_ge(s["lt_cp"], CR + it * NTR + k - 1)
                        for q in range(min(4, i + 1 - 4 * g)):
                            kb = 4 * g + q
                            ins = pe.transpose(bk(4 + k % 2)[:, P * q:P * q + P], probs_of(j)[:, P * kb:P * kb + P], ident)
                        ins.then_inc(s["lt_mm"], 1)

                def outputs(i):
                    pe.wait_ge(s["lt_cp"], CR + it * NTR + done_groups(bodies.index((i, REP - 1)) + 1))
                    pe.wait_ge(s["lvl_cp"], CR + it + 1)
                    pe.wait_ge(s["lo_add"], CR + it * NT + rows.index(i))
                    for kb in range(i + 1):
                        for hh in range(REP):
                            ins = mm(bk(7)[32 * hh:32 * hh + 32, P:2 * P], gvl[:, kb, :], gpt(i)[:, hh, kb, :],
                                     kb == 0, kb == i)
                    ins.then_inc(s["ly_mm"], 1)

                def project(i):
                    r = rows.index(i)
                    pe.wait_ge(s["ly_cp"], CR + it * NT + r + 1)
                    mm(bk(7)[:, 0:D], gy[r % 2], gvo[:, bass.ds(kv, 1), :].rearrange("p a n -> p (a n)")).then_inc(s["lo_mm"], 1)

                pe.wait_ge(s["lq_cp"], CR + it * 8 + 8)
                pe.wait_ge(s["gx_L"], CR + TILES // 4)
                for j in range(3):
                    scores(j)
                for j in range(len(bodies)):
                    if ahead(j) is not None:
                        scores(ahead(j))
                    if more and j == LAST - 1:
                        queries(it + 1, range(3))
                    if more and j == LAST:
                        queries(it + 1, range(3, 6))
                    for i in due(j, 1, 2):
                        outputs(i)
                    finish(j)
                    for i in due(j, 2, 3):
                        project(i)
                if more:
                    queries(it + 1, range(6, 8))
                project(rows[-2])
                outputs(rows[-1])
                project(rows[-1])

            with pe.Fori(0, B * KV - 1) as it:
                latent(it, True)
            latent(B * KV - 1, False)

            pe.wait_ge(s["zeroed"], CR + 4)
            pe.wait_ge(s["lo_add"], CR + B * KV * NT)
            with pe.Fori(0, DEPTH) as layer:
                def unit(G, par_, u):
                    if u < 2:
                        pe.wait_ge(s["v_cp"], CR + G * 2 + u - 1)
                    else:
                        pe.wait_ge(s["s_cap"], CR + G * 2 + u - 3)
                    first = (2 * NG if u < 2 else 0) + 4 * (u % 2)
                    for j in range(4):
                        w = Wqk[:, (first + j) * P:(first + j + 1) * P]
                        ins = mm(unit_ps(u)[:, P * j:P * j + P], w, xs[:, par_, :])
                    ins.then_inc(s["u_mm"], 1)

                def square_sums(G, u, into, name):
                    pe.wait_ge(s["u_sq"], CR + G * 4 + u + 1)
                    for gg in range(2):
                        g = 2 * (u % 2) + gg
                        for a_ in range(2):
                            ins = mm(into[32 * g:32 * g + 32, :], ones4,
                                     sq[:, u % 2, P * (2 * gg + a_):P * (2 * gg + a_ + 1)], a_ == 0, a_ == 1)
                    ins.then_inc(s[name], 1)

                def score_half(q, i):
                    for g in range(2 * i, 2 * i + 2):
                        half = bk(3 + i)[:, 256 * (g % 2):256 * (g % 2) + 256].rearrange("p (h k) -> p h k", h=4)
                        for a_ in range(2):
                            j = 2 * g + a_
                            for w in range(NW):
                                o = half[32 * w:32 * w + 32, :, :]
                                l = qr[:, j, 32 * w:32 * w + 32]
                                if w:
                                    ins = mm(o, l, kd[q][:, j, :, 32 * w - 32:32 * w + 32], a_ == 0, a_ == 1)
                                else:
                                    pe.matmul(o[:, :, 0:32], l, kd[1 - q][:, j, :, 96:128], start=a_ == 0,
                                              stop=a_ == 1, skip_group_check=True)
                                    ins = pe.matmul(o[:, :, 32:64], l, kd[q][:, j, :, 0:32], start=False,
                                                    stop=a_ == 1, skip_group_check=True)
                    ins.then_inc(s["s_mm"], 1)

                def slot(layer, k, par_, a, b, c, d, more, step):
                    n = k * 2 + par_
                    G, GK = layer * TILES + n, layer * (TILES // 2) + k
                    if a:
                        pe.wait_ge(s["xs_cp"], CR + G * 2 + 2)
                        unit(G, par_, 0)
                        unit(G, par_, 1)
                    if d:
                        pe.wait_ge(s["ot_cp"], CR + (G - 2) * 2)
                        for k in range(NP):
                            ins = mm(bk(7)[:, 0:P], Wo[:, k, :], otile[:, k, :], k == 0, k == NP - 1)
                        ins.then_inc(s["wo_mm"], 1)
                    if a:
                        pe.wait_ge(s["qs_cp"], CR + G)
                        square_sums(G, 0, bk(2)[:, P:2 * P], "ss_mm")
                        square_sums(G, 1, bk(2)[:, P:2 * P], "ss_mm")
                    if c:
                        pe.wait_ge(s["s_exp"], CR + G - 1)
                        pe.wait_ge(s["ot_cp"], CR + G * 2 - 4)
                        for i in range(2):
                            for k in range(4):
                                ins = pe.transpose(bk(5 + i)[:, P * k:P * k + P],
                                                   prob[:, par_, P * (4 * i + k):P * (4 * i + k + 1)], ident)
                            ins.then_inc(s["pt_mm"], 1)
                    step("mid")
                    if a or b:
                        pe.wait_ge(s["qs_cp"], CR + G)
                        if a:
                            pe.wait_ge(s["ss_cp"], CR + G + 1)
                        ins = pe.transpose(bk(2)[:, 0:P], ssc[:, 0:P], ident)
                        if a:
                            ins = pe.transpose(bk(2)[:, P:2 * P], ssc[:, P:2 * P], ident)
                        ins.then_inc(s["ssT_mm"], 1)
                    if b:
                        pe.wait_ge(kd_in[1 - par_], CR + (GK + par_) * 64)
                        pe.wait_ge(s["u_rot"], CR + G * 4)
                        pe.wait_ge(s["s_cap"], CR + G * 2 - 2)
                        score_half(1 - par_, 0)
                        score_half(1 - par_, 1)
                    step("scored")
                    if a and not b:
                        unit(G, par_, 2)
                        unit(G, par_, 3)
                    if a:
                        pe.wait_ge(s["wv_L"], CR + layer + 1)
                        pe.wait_ge(s["xs_L"], CR + G + 1)
                        for i in range(2):
                            pe.wait_ge(s["u_s"], CR + G * 4 + 1 + i)
                            c0, c1 = 512 * i, 512 * (i + 1)
                            mm(bk(i), xsH[:, :], WvH[:, c0:c1], True, False)
                            mm(bk(i), xsH[:, :], WvL[:, c0:c1], False, False)
                            mm(bk(i), xsL[:, :], WvH[:, c0:c1], False, True).then_inc(s["v_mm"], 1)
                        pe.wait_ge(s["rk_cp"], CR + G + 1)
                        for g in range(NG):
                            ins = pe.transpose(bk(2)[:, P * g:P * g + P], rke[:, g, :, :].rearrange("p h r -> p (h r)"), ident)
                        ins.then_inc(s["rkb_mm"], 1)
                    if c:
                        pe.wait_ge(vd_in[par_], CR + GK * 256)
                        for i in range(2):
                            pe.wait_ge(s["pt_cp"], CR + (G - 2) * 2 + i + 1)
                            for k in range(4):
                                for w in range(NW):
                                    pr = 4 * i + k
                                    rhs = vd[par_][:, w, :, 64 * pr:64 * pr + 64]
                                    ins = mm(bk(5 + i)[32 * w:32 * w + 32, P * k:P * k + P].rearrange("p (o d) -> p o d", o=2),
                                             ptile[:, pr, 32 * w:32 * w + 32], rhs)
                        ins.then_inc(s["pv_mm"], 1)
                    if a and b:
                        unit(G, par_, 2)
                        unit(G, par_, 3)
                    step("late")
                    if c:
                        pe.wait_ge(s["o_nrm"], CR + G - 1)
                        pe.wait_ge(s["wo_add"], CR + G - 2)
                        for i in range(2):
                            for k in range(4):
                                pr = 4 * i + k
                                ins = pe.transpose(bk(5 + 2 * i)[:, P * k:P * k + P],
                                                   osb[:, 2 * pr:2 * pr + 2, :].rearrange("p a d -> p (a d)"), ident)
                            ins.then_inc(s["ot_mm"], 1)
                    if a:
                        pe.wait_ge(s["k_nrm"], CR + G * 2 + 2)
                        square_sums(G, 2, bk(2)[:, 0:P], "qs_mm")
                        square_sums(G, 3, bk(2)[:, 0:P], "qs_mm")
                    step("end")

                pe.wait_ge(qkvw_in, layer * 32 + 32)
                def mean(c):
                    F = layer * NC + c
                    pe.wait_ge(s["f_cp"], CR + F * 2 + 2)
                    if c == 0:
                        pe.wait_ge(s["v_cp"], CR + (layer + 1) * TILES * 2)
                    else:
                        pe.wait_ge(s["f_sq"], CR + F)
                    mm(centred_ps(c), centre, fs[:, :]).then_inc(s["f_mu"], 1)

                def var(c):
                    F = layer * NC + c
                    pe.wait_ge(s["f_sq"], CR + F + 1)
                    pe.wait_ge(s["f_xn"], CR + F)
                    for k in range(4):
                        ins = mm(rstd_ps(c)[:, k:k + 1], fsq[:, P * k:P * k + P], meanw)
                    ins.then_inc(s["f_var"], 1)

                def rstd_rows(c):
                    F = layer * NC + c
                    pe.wait_ge(s["f_re"], CR + F + 1)
                    for k in range(4):
                        ins = pe.transpose(rstd_ps(c)[:, P * k:P * k + P], fre[:, k, :], ident)
                    ins.then_inc(s["f_rb"], 1)

                def up(c, j):
                    F = layer * NC + c
                    j0, m = FJ[j]
                    pe.wait_ge(s["xn_H"], CR + F + 1)
                    pe.wait_ge(s["f_h"], CR + F * 3 + (j - 1 if j == 2 else 0))
                    for into, at, name in ((bk(3 + j % 2), FF + j0, "f_g"), (bk(j % 2), j0, "f_a")):
                        mm(into[0:m, :], W1H[:, at:at + m], xnH[:, :], True, False)
                        mm(into[0:m, :], W1L[:, at:at + m], xnH[:, :], False, False)
                        pe.wait_ge(s["xn_L"], CR + F + 1)
                        mm(into[0:m, :], W1H[:, at:at + m], xnL[:, :], False, True).then_inc(s[name], 1)

                def down(c, steps):
                    F = layer * NC + c
                    if c >= 2:
                        pe.wait_ge(s["x_new"], CR + NC + F - 1)
                    for j in steps:
                        j0, m = FJ[j]
                        pe.wait_ge(s["f_h"], CR + F * 3 + j + 1)
                        ins = mm(out_ps(c), W2[0:m, j, :], hb[j][0:m, :], j == 0, j == 2)
                        if j == 2:
                            ins.then_inc(s["f_out_mm"], 1)

                def early(n, where):
                    if (n, where) == (TILES - 1, "end"):
                        mean(0)
                    if (n, where) == (TILES, "mid"):
                        var(0)
                    if (n, where) == (TILES, "scored"):
                        rstd_rows(0)
                    if (n, where) == (TILES, "late"):
                        pe.wait_ge(ffw_in, layer * 16 + 16)
                        pe.wait_ge(s["w1_L"], CR + layer + 1)
                        pe.wait_ge(s["s_cap"], CR + (layer + 1) * TILES * 2)
                        up(0, 0)
                    if (n, where) == (TILES, "end"):
                        up(0, 1)
                    if (n, where) == (TILES + 1, "late"):
                        up(0, 2)
                        pe.wait_ge(s["f_gl"], CR + layer * NC * 3 + 2)
                        mean(1)
                    if (n, where) == (TILES + 1, "end"):
                        var(1)
                        down(0, range(3))

                slots(pe, layer, slot, early)
                rstd_rows(1)
                pe.wait_ge(s["x_new"], CR + NC + layer * NC + 1)
                mean(2)
                pe.wait_ge(s["wo_add"], CR + (layer + 1) * TILES)
                pe.wait_ge(s["ot_cp"], CR + (layer + 1) * TILES * 2)
                for c in range(1, NC):
                    if c + 1 < NC:
                        var(c + 1)
                    up(c, 0)
                    up(c, 1)
                    if c + 1 < NC:
                        rstd_rows(c + 1)
                    up(c, 2)
                    if c + 2 < NC:
                        mean(c + 2)
                    down(c, range(3))
            pe.wait_ge(s["x_new"], CR + NC + DEPTH * NC)

            for g4 in range(TILES // 4):
                if g4 >= 2:
                    pe.wait_ge(s["fin_add"], CR + g4 - 1)
                b, t0 = divmod(4 * g4, NT)
                for k in range(4):
                    ins = pe.transpose(bk(g4 % 2)[:, P * k:P * k + P], X[:, b, 1 + P * (t0 + k):1 + P * (t0 + k + 1)], ident)
                ins.then_inc(s["fin_mm"], 1)


_OUT = ("out_0_dram", (B, T, D))


def kernel(L0_attn_x, L0_attn_wq, L0_attn_wk_down, L0_attn_wv_down, L0_attn_wk_up, L0_attn_wv_up, L0_attn_wo,
           L0_ffn_Wqkv, L0_ffn_q_scale, L0_ffn_k_scale, L0_ffn_Wo, L0_ffn_ln_g, L0_ffn_ln_b, L0_ffn_W1, L0_ffn_b1,
           L0_ffn_W2, L0_ffn_b2):
    import concourse.bacc as bacc
    from concourse.bass_utils import run_bass_kernel_spmd

    a = np.asarray
    w = a(L0_ffn_Wqkv).reshape(DEPTH, D, 3, NG, 4, 2, HALF)
    qk = w[:, :, 0:2].transpose(0, 1, 2, 3, 5, 4, 6).reshape(DEPTH, D, -1)
    v = a(L0_ffn_Wqkv)[:, :, 2 * LH * LD:].reshape(DEPTH, D, NP, 2, LD).transpose(0, 1, 3, 2, 4).reshape(DEPTH, D, -1)
    w2 = np.zeros((DEPTH, 3 * P, D), np.float32)
    w2[:, :FF] = a(L0_ffn_W2)
    par = np.zeros((DEPTH, P, V_N), np.float32)
    for col, src, half in ((V_QA, L0_ffn_q_scale, 0), (V_QB, L0_ffn_q_scale, 1), (V_KA, L0_ffn_k_scale, 0),
                           (V_KB, L0_ffn_k_scale, 1)):
        par[:, :, col] = np.tile(a(src)[:, HALF * half:HALF * (half + 1)], (1, 4))
    par[:, :, V_G], par[:, :, V_B], par[:, :, V_B2] = a(L0_ffn_ln_g), a(L0_ffn_ln_b), a(L0_ffn_b2)
    for j, (j0, m) in enumerate(FJ):
        par[:, 0:m, V_B1A + j] = a(L0_ffn_b1)[:, j0:j0 + m]
        par[:, 0:m, V_B1G + j] = a(L0_ffn_b1)[:, FF + j0:FF + j0 + m]
    cst, tabs = shape_constants()
    ins = {
        "x": a(L0_attn_x),
        "wqT": a(L0_attn_wq).T,
        "wkdT": a(L0_attn_wk_down).reshape(D, KV, LAT).transpose(2, 1, 0).reshape(LAT, KV * D),
        "wvd": a(L0_attn_wv_down),
        "wku": a(L0_attn_wk_up),
        "wvuT": a(L0_attn_wv_up).T,
        "wo": a(L0_attn_wo),
        "wqkv": np.concatenate([qk, v], axis=2),
        "lwo": a(L0_ffn_Wo),
        "w1": a(L0_ffn_W1),
        "w2": w2.reshape(DEPTH, 3, P, D).transpose(0, 2, 1, 3),
        "par": par,
        "cst": cst,
        "tab": tabs,
    }
    nc = bacc.Bacc("TRN2", target_bir_lowering=False, num_devices=1)
    arrays, args = {}, []
    for name, arr in ins.items():
        arr = np.ascontiguousarray(arr)
        arrays[f"in_{name}_dram"] = arr
        args.append(nc.dram_tensor(f"in_{name}_dram", arr.shape, mybir.dt.from_np(arr.dtype), kind="ExternalInput").ap())
    args.append(nc.dram_tensor(_OUT[0], _OUT[1], F32, kind="ExternalOutput").ap())
    build(nc, *args)
    r = run_bass_kernel_spmd(nc, [arrays], core_ids=[0])
    return r.results[0][_OUT[0]]
```
